# Optimizing a Trainium2 kernel written in Bass

```python
import numpy as np
import jax
import jax.numpy as jnp

def _softmax(x, axis=-1):
    return jax.nn.softmax(x, axis=axis)

def _gelu(x):
    return jax.nn.gelu(x, approximate=True)

def _silu(x):
    return jax.nn.silu(x)

def _sigmoid(x):
    return jax.nn.sigmoid(x)

def _layernorm(x, axis=-1, eps=1e-05):
    m = jnp.mean(x, axis=axis, keepdims=True)
    v = jnp.var(x, axis=axis, keepdims=True)
    return (x - m) / jnp.sqrt(v + eps)

def _scatter_add(tgt, idx, src, axis=0):
    return tgt.at[idx].add(src)

def _segment_sum(src, seg, n):
    return jax.ops.segment_sum(src, seg, n)
kernel_name = 'mk_gnn_preln_d4_gnn_r8_8a9d0d'

def setup_inputs(seed: int=0):
    np.random.seed(seed)
    _w = jnp.asarray

    def _rec_inputs():
        import jax
        import jax.numpy as jnp
        _gk = jax.random.key(seed)
        x = -0.000202 + 1 * jax.random.normal(jax.random.fold_in(_gk, 1), (6250, 128), jnp.float32)
        _s = jax.random.randint(jax.random.fold_in(_gk, 2), (50000,), 0, 6250, jnp.int32)
        _d = jax.random.randint(jax.random.fold_in(_gk, 3), (50000,), 0, 6250, jnp.int32)
        _loop = jnp.arange(6250, dtype=jnp.int32)
        src = jnp.concatenate([_s, _d, _loop])
        dst = jnp.concatenate([_d, _s, _loop])
        _o = jnp.argsort(dst, stable=True)
        src = src[_o]
        dst = dst[_o]
        edge_attr_128 = -6.47781e-05 + 0.999943 * jax.random.normal(jax.random.fold_in(_gk, 13), (106250, 128), jnp.float32)
        return (x, src, dst, edge_attr_128)
    x, src, dst, edge_attr_128 = _rec_inputs()

    def _L0_gnn_setup():
        import jax, jax.numpy as jnp
        import numpy as np
        N, E, DIM, ATTN, HID, B = (6250, 75000, 128, 64, 256, 64)

        def layernorm(x, g, b):
            m = x.mean(-1, keepdims=True)
            v = x.var(-1, keepdims=True)
            return (x - m) * jax.lax.rsqrt(v + 1e-05) * g + b

        def seg_mean(x, idx, num):
            s = jax.ops.segment_sum(x, idx, num_segments=num)
            c = jax.ops.segment_sum(jnp.ones((x.shape[0], 1), x.dtype), idx, num_segments=num)
            return s / jnp.maximum(c, 1.0)

        def _forward(X, g_token, Wg_in_w, Wg_in_b, ln1_g, ln1_b, eps, msg_w, msg_b, lin_w, lin_b, ln2_g, ln2_b, Wq, Wk, Wphi, Wy_w, Wy_b, We_w, We_b, ln3_g, ln3_b, ffn_w1, ffn_b1, ffn_w2, ffn_b2, edge_index, batch_idx, num_graphs):
            n = X.shape[0]
            src, dst = (edge_index[0], edge_index[1])
            g = g_token + seg_mean(X, batch_idx, num_graphs)
            X = X + (g @ Wg_in_w + Wg_in_b)[batch_idx]
            Xn = layernorm(X, ln1_g, ln1_b)
            msg = (Xn @ msg_w + msg_b)[dst]
            agg = jax.ops.segment_sum(msg, src, num_segments=n)
            X = X + jax.nn.relu(((1.0 + eps) * Xn + agg) @ lin_w + lin_b)
            Xn = layernorm(X, ln2_g, ln2_b)
            e = jnp.tanh((Xn @ Wq)[src] + (Xn @ Wk)[dst])
            scores = e @ Wphi
            exp_s = jnp.exp(scores - scores.max())
            denom = jax.ops.segment_sum(exp_s, src, num_segments=n)
            alpha = exp_s / (denom[src] + 1e-09)
            vmsg = alpha[:, None] * ((Xn @ Wy_w + Wy_b)[dst] + (e @ We_w + We_b))
            X = X + jax.ops.segment_sum(vmsg, src, num_segments=n)
            Xn = layernorm(X, ln3_g, ln3_b)
            return X + jax.nn.relu(Xn @ ffn_w1 + ffn_b1) @ ffn_w2 + ffn_b2
        ks = jax.random.split(jax.random.key(seed), 16)
        r = lambda i, shape: jax.random.normal(ks[i], shape, jnp.float32) * 0.05
        z = lambda d: jnp.zeros((d,), jnp.float32)
        o = lambda d: jnp.ones((d,), jnp.float32)
        return {'X': jax.random.normal(ks[0], (N, DIM), jnp.float32), 'edge_index': jax.random.randint(ks[1], (2, E), 0, N), 'batch_idx': jnp.sort(jax.random.randint(ks[2], (N,), 0, B)), 'num_graphs': B, 'g_token': r(3, (1, DIM)), 'Wg_in_w': r(4, (DIM, DIM)), 'Wg_in_b': z(DIM), 'ln1_g': o(DIM), 'ln1_b': z(DIM), 'eps': jnp.zeros((), jnp.float32), 'msg_w': r(5, (DIM, DIM)), 'msg_b': z(DIM), 'lin_w': r(6, (DIM, DIM)), 'lin_b': z(DIM), 'ln2_g': o(DIM), 'ln2_b': z(DIM), 'Wq': r(7, (DIM, ATTN)), 'Wk': r(8, (DIM, ATTN)), 'Wphi': r(9, (ATTN,)), 'Wy_w': r(10, (DIM, DIM)), 'Wy_b': z(DIM), 'We_w': r(11, (ATTN, DIM)), 'We_b': z(DIM), 'ln3_g': o(DIM), 'ln3_b': z(DIM), 'ffn_w1': r(12, (DIM, HID)), 'ffn_b1': z(HID), 'ffn_w2': r(13, (HID, DIM)), 'ffn_b2': z(DIM)}
    _L0_gnn_all = _L0_gnn_setup()
    _L0_gnn_in = {k: v for k, v in _L0_gnn_all.items() if k in ('g_token', 'Wg_in_w', 'Wg_in_b', 'ln1_g', 'ln1_b', 'eps', 'msg_w', 'msg_b', 'lin_w', 'lin_b', 'ln2_g', 'ln2_b', 'Wq', 'Wk', 'Wphi', 'Wy_w', 'Wy_b', 'We_w', 'We_b', 'ln3_g', 'ln3_b', 'ffn_w1', 'ffn_b1', 'ffn_w2', 'ffn_b2')}
    del _L0_gnn_all

    def _L1_gnn_setup():
        import jax, jax.numpy as jnp
        import numpy as np
        N, E, G, DIM = (12500, 200000, 64, 128)
        BN_EPS = 1e-05

        def _bn(h, gamma, beta):
            mu = jnp.mean(h, axis=0)
            var = jnp.var(h, axis=0)
            return (h - mu) * jax.lax.rsqrt(var + BN_EPS) * gamma + beta
        key = jax.random.key(seed)
        ks = jax.random.split(key, 20)
        inp = {'x': jax.random.normal(ks[0], (N, DIM), jnp.float32), 'edge_attr': jax.random.normal(ks[1], (E, DIM), jnp.float32), 'u': jax.random.normal(ks[2], (G, DIM), jnp.float32), 'edge_index': jax.random.randint(ks[3], (2, E), 0, N, jnp.int32), 'batch': jnp.sort(jax.random.randint(ks[4], (N,), 0, G, jnp.int32))}

        def xavier(k, shape):
            fan_in, fan_out = (shape[1], shape[0])
            lim = jnp.sqrt(6.0 / (fan_in + fan_out))
            return jax.random.uniform(k, shape, jnp.float32, -lim, lim)
        inp['W0'] = xavier(ks[5], (DIM, 3 * DIM))
        inp['b0'] = jnp.zeros((DIM,), jnp.float32)
        inp['W1'] = xavier(ks[6], (DIM, DIM))
        inp['b1'] = jnp.zeros((DIM,), jnp.float32)
        inp['W2'] = xavier(ks[7], (DIM, DIM))
        inp['b2'] = jnp.zeros((DIM,), jnp.float32)
        for i in range(3):
            inp[f'g{i}'] = jnp.ones((DIM,), jnp.float32)
            inp[f'bt{i}'] = jnp.zeros((DIM,), jnp.float32)
        return inp
    _L1_gnn_all = _L1_gnn_setup()
    _L1_gnn_in = {k: v for k, v in _L1_gnn_all.items() if k in ('u', 'W0', 'b0', 'W1', 'b1', 'W2', 'b2', 'g0', 'bt0', 'g1', 'bt1', 'g2', 'bt2')}
    del _L1_gnn_all

    def _L2_gnn_setup():
        import jax, jax.numpy as jnp
        import numpy as np
        N_NODES = 12500
        N_EDGES = 200000
        D_IN = 128
        D_OUT = 128
        key = jax.random.key(seed)
        k1, k2, k3, k4, k5 = jax.random.split(key, 5)
        feature = jax.random.normal(k1, (N_NODES, D_IN), dtype=jnp.float32)
        src = jax.random.randint(k2, (N_EDGES,), 0, N_NODES, dtype=jnp.int32)
        dst = jax.random.randint(k3, (N_EDGES,), 0, N_NODES, dtype=jnp.int32)
        bound = float(np.sqrt(6.0 / (D_IN + D_OUT)))
        W_self = jax.random.uniform(k4, (D_IN, D_OUT), jnp.float32, -bound, bound)
        W_inter = jax.random.uniform(k5, (D_IN, D_OUT), jnp.float32, -bound, bound)
        return {'feature': feature, 'src': src, 'dst': dst, 'W_self': W_self, 'W_inter': W_inter}
    _L2_gnn_all = _L2_gnn_setup()
    _L2_gnn_in = {k: v for k, v in _L2_gnn_all.items() if k in ('W_self', 'W_inter')}
    del _L2_gnn_all

    def _L3_gnn_setup():
        import jax, jax.numpy as jnp
        import numpy as np
        N_NODES = 6250
        N_EDGES = 75000
        DIM_H = 128
        LN_EPS = 1e-05

        def _layer_norm(x, gamma, beta):
            mu = jnp.mean(x, axis=-1, keepdims=True)
            var = jnp.mean(jnp.square(x - mu), axis=-1, keepdims=True)
            return gamma * (x - mu) * jax.lax.rsqrt(var + LN_EPS) + beta
        key = jax.random.key(seed)
        ks = jax.random.split(key, 8)
        s = 1.0 / np.sqrt(DIM_H)
        return {'nodes': jax.random.normal(ks[0], (N_NODES, DIM_H), jnp.float32), 'W_msg': jax.random.normal(ks[1], (DIM_H, DIM_H), jnp.float32) * s, 'b_msg': jnp.zeros((DIM_H,), jnp.float32), 'w_ih': jax.random.normal(ks[2], (3 * DIM_H, DIM_H), jnp.float32) * s, 'w_hh': jax.random.normal(ks[3], (3 * DIM_H, DIM_H), jnp.float32) * s, 'b_ih': jnp.zeros((3 * DIM_H,), jnp.float32), 'b_hh': jnp.zeros((3 * DIM_H,), jnp.float32), 'ln_gamma': jnp.ones((DIM_H,), jnp.float32), 'ln_beta': jnp.zeros((DIM_H,), jnp.float32), 'edge_src': jax.random.randint(ks[4], (N_EDGES,), 0, N_NODES, jnp.int32), 'edge_dst': jax.random.randint(ks[5], (N_EDGES,), 0, N_NODES, jnp.int32)}
    _L3_gnn_all = _L3_gnn_setup()
    _L3_gnn_in = {k: v for k, v in _L3_gnn_all.items() if k in ('W_msg', 'b_msg', 'w_ih', 'w_hh', 'b_ih', 'b_hh', 'ln_gamma', 'ln_beta')}
    del _L3_gnn_all
    return {'x': x, 'src': src, 'dst': dst, 'edge_attr_128': edge_attr_128, 'L0_gnn_g_token': _L0_gnn_in['g_token'], 'L0_gnn_Wg_in_w': _L0_gnn_in['Wg_in_w'], 'L0_gnn_Wg_in_b': _L0_gnn_in['Wg_in_b'], 'L0_gnn_ln1_g': _L0_gnn_in['ln1_g'], 'L0_gnn_ln1_b': _L0_gnn_in['ln1_b'], 'L0_gnn_eps': _L0_gnn_in['eps'], 'L0_gnn_msg_w': _L0_gnn_in['msg_w'], 'L0_gnn_msg_b': _L0_gnn_in['msg_b'], 'L0_gnn_lin_w': _L0_gnn_in['lin_w'], 'L0_gnn_lin_b': _L0_gnn_in['lin_b'], 'L0_gnn_ln2_g': _L0_gnn_in['ln2_g'], 'L0_gnn_ln2_b': _L0_gnn_in['ln2_b'], 'L0_gnn_Wq': _L0_gnn_in['Wq'], 'L0_gnn_Wk': _L0_gnn_in['Wk'], 'L0_gnn_Wphi': _L0_gnn_in['Wphi'], 'L0_gnn_Wy_w': _L0_gnn_in['Wy_w'], 'L0_gnn_Wy_b': _L0_gnn_in['Wy_b'], 'L0_gnn_We_w': _L0_gnn_in['We_w'], 'L0_gnn_We_b': _L0_gnn_in['We_b'], 'L0_gnn_ln3_g': _L0_gnn_in['ln3_g'], 'L0_gnn_ln3_b': _L0_gnn_in['ln3_b'], 'L0_gnn_ffn_w1': _L0_gnn_in['ffn_w1'], 'L0_gnn_ffn_b1': _L0_gnn_in['ffn_b1'], 'L0_gnn_ffn_w2': _L0_gnn_in['ffn_w2'], 'L0_gnn_ffn_b2': _L0_gnn_in['ffn_b2'], 'L1_gnn_u': _L1_gnn_in['u'], 'L1_gnn_W0': _L1_gnn_in['W0'], 'L1_gnn_b0': _L1_gnn_in['b0'], 'L1_gnn_W1': _L1_gnn_in['W1'], 'L1_gnn_b1': _L1_gnn_in['b1'], 'L1_gnn_W2': _L1_gnn_in['W2'], 'L1_gnn_b2': _L1_gnn_in['b2'], 'L1_gnn_g0': _L1_gnn_in['g0'], 'L1_gnn_bt0': _L1_gnn_in['bt0'], 'L1_gnn_g1': _L1_gnn_in['g1'], 'L1_gnn_bt1': _L1_gnn_in['bt1'], 'L1_gnn_g2': _L1_gnn_in['g2'], 'L1_gnn_bt2': _L1_gnn_in['bt2'], 'L2_gnn_W_self': _L2_gnn_in['W_self'], 'L2_gnn_W_inter': _L2_gnn_in['W_inter'], 'L3_gnn_W_msg': _L3_gnn_in['W_msg'], 'L3_gnn_b_msg': _L3_gnn_in['b_msg'], 'L3_gnn_w_ih': _L3_gnn_in['w_ih'], 'L3_gnn_w_hh': _L3_gnn_in['w_hh'], 'L3_gnn_b_ih': _L3_gnn_in['b_ih'], 'L3_gnn_b_hh': _L3_gnn_in['b_hh'], 'L3_gnn_ln_gamma': _L3_gnn_in['ln_gamma'], 'L3_gnn_ln_beta': _L3_gnn_in['ln_beta']}

def reference(x, src, dst, edge_attr_128, L0_gnn_g_token, L0_gnn_Wg_in_w, L0_gnn_Wg_in_b, L0_gnn_ln1_g, L0_gnn_ln1_b, L0_gnn_eps, L0_gnn_msg_w, L0_gnn_msg_b, L0_gnn_lin_w, L0_gnn_lin_b, L0_gnn_ln2_g, L0_gnn_ln2_b, L0_gnn_Wq, L0_gnn_Wk, L0_gnn_Wphi, L0_gnn_Wy_w, L0_gnn_Wy_b, L0_gnn_We_w, L0_gnn_We_b, L0_gnn_ln3_g, L0_gnn_ln3_b, L0_gnn_ffn_w1, L0_gnn_ffn_b1, L0_gnn_ffn_w2, L0_gnn_ffn_b2, L1_gnn_u, L1_gnn_W0, L1_gnn_b0, L1_gnn_W1, L1_gnn_b1, L1_gnn_W2, L1_gnn_b2, L1_gnn_g0, L1_gnn_bt0, L1_gnn_g1, L1_gnn_bt1, L1_gnn_g2, L1_gnn_bt2, L2_gnn_W_self, L2_gnn_W_inter, L3_gnn_W_msg, L3_gnn_b_msg, L3_gnn_w_ih, L3_gnn_w_hh, L3_gnn_b_ih, L3_gnn_b_hh, L3_gnn_ln_gamma, L3_gnn_ln_beta):
    import jax
    import jax.numpy as jnp

    def _L0_gnn_ref(X, edge_index, batch_idx, num_graphs, g_token, Wg_in_w, Wg_in_b, ln1_g, ln1_b, eps, msg_w, msg_b, lin_w, lin_b, ln2_g, ln2_b, Wq, Wk, Wphi, Wy_w, Wy_b, We_w, We_b, ln3_g, ln3_b, ffn_w1, ffn_b1, ffn_w2, ffn_b2):
        import jax, jax.numpy as jnp
        import numpy as np
        N, E, DIM, ATTN, HID, B = (6250, 75000, 128, 64, 256, 64)

        def layernorm(x, g, b):
            m = x.mean(-1, keepdims=True)
            v = x.var(-1, keepdims=True)
            return (x - m) * jax.lax.rsqrt(v + 1e-05) * g + b

        def seg_mean(x, idx, num):
            s = jax.ops.segment_sum(x, idx, num_segments=num)
            c = jax.ops.segment_sum(jnp.ones((x.shape[0], 1), x.dtype), idx, num_segments=num)
            return s / jnp.maximum(c, 1.0)

        def _forward(X, g_token, Wg_in_w, Wg_in_b, ln1_g, ln1_b, eps, msg_w, msg_b, lin_w, lin_b, ln2_g, ln2_b, Wq, Wk, Wphi, Wy_w, Wy_b, We_w, We_b, ln3_g, ln3_b, ffn_w1, ffn_b1, ffn_w2, ffn_b2, edge_index, batch_idx, num_graphs):
            n = X.shape[0]
            src, dst = (edge_index[0], edge_index[1])
            g = g_token + seg_mean(X, batch_idx, num_graphs)
            X = X + (g @ Wg_in_w + Wg_in_b)[batch_idx]
            Xn = layernorm(X, ln1_g, ln1_b)
            msg = (Xn @ msg_w + msg_b)[dst]
            agg = jax.ops.segment_sum(msg, src, num_segments=n)
            X = X + jax.nn.relu(((1.0 + eps) * Xn + agg) @ lin_w + lin_b)
            Xn = layernorm(X, ln2_g, ln2_b)
            e = jnp.tanh((Xn @ Wq)[src] + (Xn @ Wk)[dst])
            scores = e @ Wphi
            exp_s = jnp.exp(scores - scores.max())
            denom = jax.ops.segment_sum(exp_s, src, num_segments=n)
            alpha = exp_s / (denom[src] + 1e-09)
            vmsg = alpha[:, None] * ((Xn @ Wy_w + Wy_b)[dst] + (e @ We_w + We_b))
            X = X + jax.ops.segment_sum(vmsg, src, num_segments=n)
            Xn = layernorm(X, ln3_g, ln3_b)
            return X + jax.nn.relu(Xn @ ffn_w1 + ffn_b1) @ ffn_w2 + ffn_b2
        return _forward(X, g_token, Wg_in_w, Wg_in_b, ln1_g, ln1_b, eps, msg_w, msg_b, lin_w, lin_b, ln2_g, ln2_b, Wq, Wk, Wphi, Wy_w, Wy_b, We_w, We_b, ln3_g, ln3_b, ffn_w1, ffn_b1, ffn_w2, ffn_b2, edge_index, batch_idx, num_graphs)

    def _L1_gnn_ref(x, edge_attr, u, W0, b0, W1, b1, W2, b2, g0, bt0, g1, bt1, g2, bt2, edge_index, batch):
        import jax, jax.numpy as jnp
        import numpy as np
        N, E, G, DIM = (12500, 200000, 64, 128)
        BN_EPS = 1e-05

        def _bn(h, gamma, beta):
            mu = jnp.mean(h, axis=0)
            var = jnp.var(h, axis=0)
            return (h - mu) * jax.lax.rsqrt(var + BN_EPS) * gamma + beta
        n = x.shape[0]
        src = edge_index[0]
        sums = jax.ops.segment_sum(edge_attr, src, num_segments=n)
        cnt = jax.ops.segment_sum(jnp.ones((edge_attr.shape[0],), edge_attr.dtype), src, num_segments=n)
        v_e = sums / jnp.maximum(cnt, 1.0)[:, None]
        out = jnp.concatenate([x, v_e, u[batch]], axis=1)
        for W, b, g, bt in ((W0, b0, g0, bt0), (W1, b1, g1, bt1), (W2, b2, g2, bt2)):
            out = jax.nn.relu(out @ W.T + b)
            out = _bn(out, g, bt)
        return out

    def _L2_gnn_ref(feature, src, dst, W_self, W_inter):
        import jax, jax.numpy as jnp
        import numpy as np
        N_NODES = 12500
        N_EDGES = 200000
        D_IN = 128
        D_OUT = 128
        n = feature.shape[0]
        ones = jnp.ones_like(src, dtype=jnp.float32)
        out_deg = jnp.clip(jax.ops.segment_sum(ones, src, num_segments=n), 1.0)
        in_deg = jnp.clip(jax.ops.segment_sum(ones, dst, num_segments=n), 1.0)
        h = feature * (out_deg ** (-0.5))[:, None]
        h_self = jax.ops.segment_sum(h[src], dst, num_segments=n)
        m_inter = h[src] * feature[dst]
        h_inter = jax.ops.segment_sum(m_inter, dst, num_segments=n)
        rst = h_self @ W_self + h_inter @ W_inter
        rst = rst * (in_deg ** (-0.5))[:, None]
        rst = rst + feature @ W_self
        return rst

    def _L3_gnn_ref(nodes, W_msg, b_msg, w_ih, w_hh, b_ih, b_hh, ln_gamma, ln_beta, edge_src, edge_dst):
        import jax, jax.numpy as jnp
        import numpy as np
        N_NODES = 6250
        N_EDGES = 75000
        DIM_H = 128
        LN_EPS = 1e-05

        def _layer_norm(x, gamma, beta):
            mu = jnp.mean(x, axis=-1, keepdims=True)
            var = jnp.mean(jnp.square(x - mu), axis=-1, keepdims=True)
            return gamma * (x - mu) * jax.lax.rsqrt(var + LN_EPS) + beta
        n_nodes = nodes.shape[0]
        msg_e = nodes[edge_src] @ W_msg.T + b_msg
        messages = jax.ops.segment_sum(msg_e, edge_dst, num_segments=n_nodes)
        msg = messages + jnp.mean(nodes, axis=0)
        gi = msg @ w_ih.T + b_ih
        gh = nodes @ w_hh.T + b_hh
        i_r, i_z, i_n = jnp.split(gi, 3, axis=-1)
        h_r, h_z, h_n = jnp.split(gh, 3, axis=-1)
        r = jax.nn.sigmoid(i_r + h_r)
        z = jax.nn.sigmoid(i_z + h_z)
        n = jnp.tanh(i_n + r * h_n)
        h_next = (1.0 - z) * n + z * nodes
        out = _layer_norm(h_next, ln_gamma, ln_beta)
        out = out + messages
        return out
    edge_index = jnp.stack([src, dst])
    batch0 = jnp.zeros((6250,), jnp.int32)
    h = jnp.maximum(_layernorm(x, axis=-1), 0.0)
    x = x + _L0_gnn_ref(h, edge_index, batch0, 64, L0_gnn_g_token, L0_gnn_Wg_in_w, L0_gnn_Wg_in_b, L0_gnn_ln1_g, L0_gnn_ln1_b, L0_gnn_eps, L0_gnn_msg_w, L0_gnn_msg_b, L0_gnn_lin_w, L0_gnn_lin_b, L0_gnn_ln2_g, L0_gnn_ln2_b, L0_gnn_Wq, L0_gnn_Wk, L0_gnn_Wphi, L0_gnn_Wy_w, L0_gnn_Wy_b, L0_gnn_We_w, L0_gnn_We_b, L0_gnn_ln3_g, L0_gnn_ln3_b, L0_gnn_ffn_w1, L0_gnn_ffn_b1, L0_gnn_ffn_w2, L0_gnn_ffn_b2)
    h = jnp.maximum(_layernorm(x, axis=-1), 0.0)
    x = x + _L1_gnn_ref(h, edge_attr_128, L1_gnn_u, L1_gnn_W0, L1_gnn_b0, L1_gnn_W1, L1_gnn_b1, L1_gnn_W2, L1_gnn_b2, L1_gnn_g0, L1_gnn_bt0, L1_gnn_g1, L1_gnn_bt1, L1_gnn_g2, L1_gnn_bt2, edge_index, batch0)
    h = jnp.maximum(_layernorm(x, axis=-1), 0.0)
    x = x + _L2_gnn_ref(h, src, dst, L2_gnn_W_self, L2_gnn_W_inter)
    h = jnp.maximum(_layernorm(x, axis=-1), 0.0)
    x = x + _L3_gnn_ref(h, L3_gnn_W_msg, L3_gnn_b_msg, L3_gnn_w_ih, L3_gnn_w_hh, L3_gnn_b_ih, L3_gnn_b_hh, L3_gnn_ln_gamma, L3_gnn_ln_beta, src, dst)
    return x

_drawn_inputs = setup_inputs


def setup_inputs(seed=0):
    import zlib

    import numpy as np

    out = dict(_drawn_inputs(seed))
    spreads = {'L0_gnn_Wg_in_b': (0.0, 0.1),
     'L0_gnn_ln1_g': (1.0, 0.2),
     'L0_gnn_ln1_b': (0.0, 0.1),
     'L0_gnn_msg_b': (0.0, 0.1),
     'L0_gnn_lin_b': (0.0, 0.1),
     'L0_gnn_ln2_g': (1.0, 0.2),
     'L0_gnn_ln2_b': (0.0, 0.328),
     'L0_gnn_Wy_b': (0.0, 0.1),
     'L0_gnn_We_b': (0.0, 0.1),
     'L0_gnn_ln3_g': (1.0, 0.6),
     'L0_gnn_ln3_b': (0.0, 0.8),
     'L0_gnn_ffn_b1': (0.0, 0.53),
     'L0_gnn_ffn_b2': (0.0, 0.1),
     'L1_gnn_b0': (0.0, 0.1),
     'L1_gnn_b1': (0.0, 0.8),
     'L1_gnn_b2': (0.0, 0.8),
     'L1_gnn_g0': (1.0, 0.2),
     'L1_gnn_bt0': (0.0, 0.746),
     'L1_gnn_g1': (1.0, 0.2),
     'L1_gnn_bt1': (0.0, 0.8),
     'L1_gnn_g2': (1.0, 0.2),
     'L1_gnn_bt2': (0.0, 0.1),
     'L3_gnn_b_msg': (0.0, 0.1),
     'L3_gnn_b_ih': (0.0, 2.0),
     'L3_gnn_b_hh': (0.0, 2.0),
     'L3_gnn_ln_gamma': (1.0, 0.6),
     'L3_gnn_ln_beta': (0.0, 0.8)}
    factors = {'L0_gnn_Wphi': 8.0, 'L3_gnn_w_hh': 5.216}
    for name, (base, spread) in spreads.items():
        noise = np.random.default_rng([zlib.crc32(name.encode()), seed]).standard_normal(out[name].shape)
        drawn = base * np.exp(spread * noise) if base else spread * noise
        out[name] = jnp.asarray(drawn.astype(out[name].dtype))
    for name, factor in factors.items():
        out[name] = (out[name] * factor).astype(out[name].dtype)
    return out
```

```python
import math
from contextlib import ExitStack

import concourse.bass as bass
from concourse import mybir

F32 = mybir.dt.float32
I32 = mybir.dt.int32
ALU = mybir.AluOpType
ACT = mybir.ActivationFunctionType
AX = mybir.AxisListType

P = 128
D = 128
N = 6250
E = 106250
NB = -(-N // P)
NP = NB * P
LAST = N - (NB - 1) * P
GB = 7
NG = NB // GB
GW = GB * P
EJ = E // P
ER = E - EJ * P
EC = EJ + 1
BT = 10
RING = 2 * BT
CHUNKS = -(-(E // P + NB) // RING) * RING
TURNS = CHUNKS // RING
SLOTS = CHUNKS * P
TAILS = CHUNKS - (-(-E // P))
ATTN = 64
HID = 256
PAY = D + 3
ROW = D + PAY
KY = ATTN + D
AGW = D + ATTN + 1
ACW = AGW + 1
SW = D + 1
EPS = 1e-5
BANKS = 5
ABANKS = 2
LOW = -1.0e30
FAR = 1.0e6

CONST = {}
_c = 0
for _n, _w in (("ident", P), ("strict", P), ("ones", P), ("iota", P), ("before", NB), ("upto", NB),
               ("blocks", NB), ("chunks", CHUNKS), ("part", 1)):
    CONST[_n] = (_c, _w)
    _c += _w
CONST_W = _c

WEIGHTS = {}
_c = 0
for _n, _w in (("Wg", D), ("msg", D), ("lin", D), ("qky", 2 * ATTN + D), ("We", D), ("w1", HID), ("w2", HID),
               ("W0", 3 * D), ("W1", D), ("W2", D), ("self", D), ("inter", D), ("Wm", D), ("ih", 3 * D),
               ("hh", 3 * D), ("g_token", 1), ("ln2_g", 1), ("ln2_b", 1), ("ln3_g", 1), ("ln3_b", 1),
               ("ffn_b1", 2), ("u", 1), ("b0", 1), ("b1", 1), ("b2", 1), ("g0", 1), ("g1", 1), ("g2", 1),
               ("bt0", 1), ("bt1", 1), ("bt2", 1), ("b_ih", 3), ("b_hh", 3)):
    WEIGHTS[_n] = (_c, _w)
    _c += _w
WEIGHTS_W = _c

ROWS = {}
_c = 0
for _n, _w in (("eps", 1), ("Wg_b", D), ("ln1_g", D), ("ln1_b", D), ("msg_b", D), ("lin_b", D), ("Wy_b", D),
               ("We_b", D), ("ffn_b2", D), ("b_msg", D), ("gamma", D), ("beta", D), ("phi", ATTN)):
    ROWS[_n] = (_c, _w)
    _c += _w
ROWS_W = _c


def gnn_kernel(nc, x, src, dst, edge_attr, const, weights, rows, out):
    ctx = ExitStack()
    with ctx:
        def sb(name, shape, dt=F32):
            return ctx.enter_context(nc.sbuf_tensor(name, shape, dt))

        def sem(name):
            return ctx.enter_context(nc.semaphore(name))

        def dram(name, shape):
            return nc.dram_tensor(name, shape, F32, kind="Internal").ap()

        payload = dram("payload", (SLOTS, PAY))
        dst_meta = dram("dst_meta", (SLOTS, 2))
        xn_table = dram("xn_table", (NP, D))
        ky_table = dram("ky_table", (NP, KY))
        h2_table = dram("h2_table", (NP, D))
        h3_table = dram("h3_table", (NP, D))

        cst = sb("cst", [P, CONST_W])
        wts = sb("wts", [P, WEIGHTS_W])
        rws = sb("rws", [P, ROWS_W])
        big = sb("big", [P, 2 * NP])
        att = sb("att", [P, NB * SW])
        hst = sb("hst", [P, NB, D])
        qst = sb("qst", [P, NB, ATTN])
        ring = sb("ring", [P, RING, ROW])
        onehot = sb("onehot", [P, RING, P])
        onehotT = sb("onehotT", [P, BT * P])
        meta_s = sb("meta_s", [P, CHUNKS, 2])
        meta_d = sb("meta_d", [P, CHUNKS, 2])
        ends = [meta_s[:, 0:EC, :], meta_d[:, 0:EC, :]]
        blk_s = sb("blk_s", [1, CHUNKS], I32)
        idx = sb("idx", [P, RING], I32)
        sidx = sb("sidx", [P, RING], I32)
        padidx = sb("padidx", [P, NB + TAILS], I32)
        padrow = sb("padrow", [P, PAY])
        stage = sb("stage", [P, RING, 2])
        kyt = sb("kyt", [P, GB, KY])
        zpr = sb("zpr", [P, 2, BT, ATTN])
        zt, pr = zpr[:, 0], zpr[:, 1]
        pos = [zpr[:, :, :, :].rearrange("p a b c -> p (a b c)")[:, 0:EC], sb("pos_d", [P, EC])[:, :]]
        sc = sb("sc", [P, BT])
        neg = sb("neg", [P, BT])
        wexp = sb("wexp", [P, BT])
        mrun = sb("mrun", [P, 8])
        mb = sb("mb", [P, 8])
        deg = sb("deg", [P, NB])
        outn = sb("outn", [P, NB])
        inn = sb("inn", [P, NB])
        st = sb("st", [P, 64])
        bns = sb("bns", [P, 14 * 6])
        col = sb("col", [P, 32])
        cnt = sb("cnt", [P, NB])
        nrm = sb("nrm", [P, 32])
        rootv = sb("rootv", [P, 128])
        tm1 = sb("tm1", [P, NB])
        endt = sb("endt", [P, NB])
        tt = sb("tt", [P, NB])
        chb = sb("chb", [P, P])
        chcol = sb("chcol", [P, 8])
        chint = sb("chint", [P, 8], I32)
        ps = ctx.enter_context(nc.psum_tensor("ps", [P, 8 * 512], F32))

        def c_(n, lo=0, hi=None):
            a, w = CONST[n]
            return cst[:, a + lo:a + (w if hi is None else hi)]

        def w_(n, lo=0, hi=None):
            a, w = WEIGHTS[n]
            return wts[:, a + lo:a + (w if hi is None else hi)]

        def r_(n):
            a, w = ROWS[n]
            return rws[:, a:a + w]

        def over(v, n):
            return v.unsqueeze(1).to_broadcast([P, n, v.shape[1]])

        def along(v, w):
            return v.unsqueeze(2).to_broadcast([P, v.shape[1], w])

        blk = [blk_s[:, :], c_("chunks")[0:1, :].bitcast(I32)]

        ring_f = ring[:, :, :].rearrange("p a b -> p (a b)")
        oh_f = onehot[:, :, :].rearrange("p a b -> p (a b)")
        temps = [ring_f[:, i * GW:(i + 1) * GW] for i in range(5)] + \
                [oh_f[:, i * GW:(i + 1) * GW] for i in range(2)] + [onehotT[:, 0:GW]]
        xgrp = kyt[:, :, :].rearrange("p a b -> p (a b)")[:, 0:GW]
        q_f = qst[:, :, :].rearrange("p a b -> p (a b)")
        early = [q_f[:, i * GW:(i + 1) * GW] for i in range(3)]

        def g3(v):
            return v.rearrange("p (b d) -> p b d", b=GB)

        xn1 = big[:, 0:NP].rearrange("p (b d) -> p b d", d=D)
        agg = big[:, NP:2 * NP].rearrange("p (b d) -> p b d", d=D)
        acc_a = big[:, 0:NB * ACW].rearrange("p (b d) -> p b d", d=ACW)
        acc_p = big[:, 0:NB * SW].rearrange("p (b d) -> p b d", d=SW)
        att3 = att[:, :].rearrange("p (b d) -> p b d", d=SW)
        xs = att[:, 0:NP].rearrange("p (b d) -> p b d", d=D)
        h_f = hst[:, :, :].rearrange("p b d -> p (b d)")
        o = NP
        hi_i = big[:, o:o + EC].bitcast(I32)
        lo_i = big[:, o + EC:o + 2 * EC].bitcast(I32)
        hi = big[:, o + 2 * EC:o + 3 * EC]
        mask = big[:, o + 3 * EC:o + 4 * EC].bitcast(I32)
        csum = big[:, o + 4 * EC:o + 5 * EC]
        key_i = big[:, o + 5 * EC:o + 6 * EC].bitcast(I32)
        oth_i = big[:, o + 6 * EC:o + 7 * EC].bitcast(I32)
        assert 7 * EC <= NP
        ge = oh_f[0:NB, 0:CHUNKS]
        one_e = oh_f[:, CHUNKS:CHUNKS + EC]
        padf = col

        psA = ps[:, 0:1024]
        psB = ps[:, 1024:3072]
        psC = ps[:, 3072:4096]

        s_const = sem("s_const")
        s_keys = sem("s_keys")
        s_x = sem("s_x")
        dve_step = sem("dve_step")
        act_step = sem("act_step")
        pool_step = sem("pool_step")
        names = ("cnt_done totals slots_in slots chunk_col ends_ready ge_ready blk_psum pad_ready pos_ready "
                 "h0_sum h0_col g_col g_row xn1_ready xn1_stored pads_set bucketed zeroed "
                 "n1_agg n1_aggT n1_aggTc n1_msg n1_t n1_tT n1_tTc n1_lin n1_z n1_zT n1_zTc n1_qky n1_q n1_ky ky_stored "
                 "a_T a_Tc a_q a_z a_e a_bm a_mt a_mr a_mb a_w a_free "
                 "n2_sc n2_sce n2_ue n2_ueT n2_ueTc n2_we n2_z n2_zT n2_zTc n2_hid n2_relu n2_ffn n2_x n2_xg "
                 "n2_h1T n2_h1Tc n2_veT n2_veTc n2_o0 n2_r0 n2_ub n2_ubc "
                 "bn_ac bn_bias bn_w l1_mm l1_relu n3_o n3_T n3_hs n3_st "
                 "n4_in n4_m n4_T n4_Tc n4_mm n4_h n4_st n4_sum n4_mean n4_meanc "
                 "n5_s n5_sT n5_sTc n5_m n5_msg n5_T n5_Tc n5_hc n5_rz n5_rza n5_nn n5_npre n5_n n5_hn n5_hnT n5_out n5_st "
                 "s_var s_std s_root s_rooted s_idx s_hold s_ps s_free meta_pre meta_in").split()
        S = {n: sem(n) for n in names}
        s_pay = [sem(f"s_pay{i}") for i in range(2)]
        s_oh = [sem(f"s_oh{i}") for i in range(2)]
        s_row = [sem(f"s_row{i}") for i in range(RING)]

        class Chain:

            def __init__(self, eng, s):
                self.eng, self.s, self.n, self.turn, self.per = eng, s, 0, None, 0

            def __call__(self, ins):
                ins.then_inc(self.s, 1)
                self.n += 1
                at = self.n if self.turn is None else self.turn * self.per + self.n
                self.eng.wait_ge(self.s, at)

            def loop(self, turn, per):
                self.turn, self.per, self.first = turn, per, self.n

            def end(self, turns):
                assert self.n - self.first == self.per, (self.n - self.first, self.per)
                self.turn = None
                self.n = self.first + self.per * turns

        block = ctx.enter_context(nc.Block())

        def hold(eng):
            eng.sem_inc(S["s_hold"], 1)

        SCAT_TURNS = EJ // RING
        SCAT_LEFT = EJ - SCAT_TURNS * RING
        assert SCAT_LEFT == BT and ER > 1

        def scattered(slot, turns, tail=True):
            return 16 * (turns + (1 if slot < SCAT_LEFT else 0) + (1 if slot == SCAT_LEFT else 0))

        S0 = [scattered(k, SCAT_TURNS) for k in range(RING)]
        ROW_E1 = S0
        s_dst = [sem(f"s_dst{i}") for i in range(2)]
        s_pad = sem("s_pad")
        DST0 = [16 * BT * (SCAT_TURNS + 1), 16 * (BT * SCAT_TURNS + 1)]

        def free(eng, n, turn, h):
            eng.wait_ge(S["s_ps"], n * CHUNKS + turn * RING + (h + 1) * BT)

        def product(n, turn, h, k):
            return n * CHUNKS + turn * RING + (RING + h * BT + k + 1)

        def row_base(slot, n):
            return S0[slot] + 16 * TURNS * n

        @block.sync
        def _(sp):
            sp.dma_start(cst[:, :], const).then_inc(s_const, 16)
            sp.dma_start(key_i, src).then_inc(s_keys, 16)
            sp.dma_start(oth_i, dst).then_inc(s_keys, 16)
            sp.dma_start(rws[:, :], rows.to_broadcast([P, ROWS_W])).then_inc(s_const, 16)
            sp.dma_start(wts[:, :], weights).then_inc(s_const, 16)
            sp.dma_start(hst[:, :, :], x).then_inc(s_x, 16)
            ea = edge_attr[0:EJ * P, :].rearrange("(p j) f -> p j f", j=EJ)
            with sp.Fori(0, SCAT_TURNS) as turn:
                for h in range(2):
                    for k in range(BT):
                        sp.wait_ge(s_row[h * BT + k], turn * 16)
                    sp.dma_start(ring[:, h * BT:(h + 1) * BT, D:2 * D],
                                 ea[:, bass.ds(turn * RING + h * BT, BT), :]).then_inc(s_pay[h], 16)
            for k in range(BT):
                sp.wait_ge(s_row[k], SCAT_TURNS * 16)
            sp.dma_start(ring[:, 0:BT, D:2 * D], ea[:, SCAT_TURNS * RING:EJ, :]).then_inc(s_pay[0], 16)
            sp.wait_ge(s_row[BT], SCAT_TURNS * 16)
            sp.dma_start(ring[0:ER, BT, D:2 * D], edge_attr[EJ * P:E, :]).then_inc(s_pay[1], 16)
            sp.wait_ge(S["meta_pre"], 1)
            dm = dst_meta.rearrange("(p c) w -> p c w", p=P)
            sp.dma_start(dm, meta_d[:, :, :]).then_inc(S["meta_in"], 16)
            sp.wait_ge(S["pos_ready"], 1)
            sp.dma_start(key_i, dst).then_inc(s_keys, 16)
            sp.dma_start(oth_i, src).then_inc(s_keys, 16)
            xt = xn_table.rearrange("(b p) d -> p b d", p=P)
            sp.wait_ge(S["xn1_ready"], NG)
            sp.dma_start(xt, xn1).then_inc(S["xn1_stored"], 16)
            for k in range(RING):
                sp.wait_ge(s_row[k], S0[k])
            sp.wait_ge(s_pad, 16 * (NB + TAILS))
            pl = payload.rearrange("(c p) w -> p c w", p=P)
            with sp.Fori(0, TURNS) as turn:
                for h in range(2):
                    free(sp, 0, turn, h)
                    sp.dma_start(ring[:, h * BT:(h + 1) * BT, D:ROW],
                                 pl[:, bass.ds(turn * RING + h * BT, BT), :]).then_inc(s_pay[h], 16)
            kt = ky_table.rearrange("(b p) d -> p b d", p=P)
            with sp.Fori(0, NG) as t:
                sp.wait_ge(S["n1_ky"], t + 1)
                sp.dma_start(kt[:, bass.ds(t * GB, GB), :], kyt[:, :, :]).then_inc(S["ky_stored"], 16)
            with sp.Fori(0, NG) as t:
                sp.wait_ge(S["ky_stored"], 16 * NG)
                sp.wait_ge(S["n2_x"], t)
                sp.dma_start(g3(xgrp), x[:, bass.ds(t * GB, GB), :]).then_inc(S["n2_xg"], 16)
            for h in range(2):
                sp.wait_ge(s_dst[h], DST0[h])
            sp.dma_start(meta_d[:, :, :], dst_meta.rearrange("(c p) w -> p c w", p=P)).then_inc(S["meta_in"], 16)
            h2 = h2_table.rearrange("(b p) d -> p b d", p=P)
            with sp.Fori(0, NG) as t:
                sp.wait_ge(S["n3_hs"], t + 1)
                sp.dma_start(h2[:, bass.ds(t * GB, GB), :], g3(temps[4])).then_inc(S["n3_st"], 16)
            h3 = h3_table.rearrange("(b p) d -> p b d", p=P)
            sp.wait_ge(S["n4_h"], NG)
            sp.dma_start(h3, hst[:, :, :]).then_inc(S["n4_st"], 16)
            with sp.Fori(0, NG) as t:
                sp.wait_ge(S["n5_out"], t + 1)
                sp.dma_start(out[:, bass.ds(t * GB, GB), :], g3(temps[7])).then_inc(S["n5_st"], 16)
            sp.wait_ge(S["n5_st"], 16 * NG)

        @block.gpsimd
        def _(pool):
            chain = Chain(pool, pool_step)

            def scatter_dst_turns(lo, hi_):
                with pool.Fori(lo, hi_) as turn:
                    for h in range(2):
                        lot = slice(h * BT, (h + 1) * BT)
                        pool.wait_ge(s_dst[h], turn * 16 * BT)
                        hold(pool)
                        pool.tensor_copy(stage[:, lot, :], ends[1][:, bass.ds(turn * RING + h * BT, BT), :])
                        pool.tensor_copy(sidx[:, lot], pos[1][:, bass.ds(turn * RING + h * BT, BT)])\
                            .then_inc(S["s_idx"], 1)
                        pool.wait_ge(S["s_idx"], turn * 2 + h + 1 + 2 * SCAT_TURNS + 2 + 2 * TURNS * dst_after)
                        hold(pool)
                        for k in range(h * BT, (h + 1) * BT):
                            pool.indirect_dma_start(
                                out=dst_meta, out_offset=bass.IndirectOffsetOnAxis(ap=sidx[:, k:k + 1], axis=0),
                                in_=stage[:, k, :], in_offset=None).then_inc(s_dst[h], 16)

            def gathers(n, table, width, index, waits):
                with pool.Fori(0, TURNS) as turn:
                    for h in range(2):
                        lot = slice(h * BT, (h + 1) * BT)
                        waits(turn, h)
                        hold(pool)
                        pool.tensor_copy(idx[:, lot], index(turn, h)).then_inc(S["s_idx"], 1)
                        pool.wait_ge(S["s_idx"], turn * 2 + h + 1 + idx_before[n])
                        hold(pool)
                        for k in range(h * BT, (h + 1) * BT):
                            pool.indirect_dma_start(
                                out=ring[:, k, 0:width], out_offset=None, in_=table,
                                in_offset=bass.IndirectOffsetOnAxis(ap=idx[:, k:k + 1], axis=0))\
                                .then_inc(s_row[k], 16)

            scat = 2 * SCAT_TURNS + 2
            idx_before = [scat, scat + 2 * TURNS + scat, scat * 2 + 4 * TURNS, scat * 2 + 6 * TURNS]
            dst_after = 1

            pool.wait_ge(S["pad_ready"], 1)
            for i in range(NB + TAILS):
                pool.indirect_dma_start(
                    out=payload, out_offset=bass.IndirectOffsetOnAxis(ap=padidx[:, i:i + 1], axis=0),
                    in_=padrow[:, :], in_offset=None, bounds_check=SLOTS - 1, oob_is_err=False)\
                    .then_inc(s_pad, 16)
            pool.wait_ge(S["pos_ready"], 1)
            with pool.Fori(0, SCAT_TURNS) as turn:
                for h in range(2):
                    lot = slice(h * BT, (h + 1) * BT)
                    pool.wait_ge(s_pay[h], turn * 16 + 16)
                    for k in range(BT):
                        pool.wait_ge(s_row[h * BT + k], turn * 16)
                    hold(pool)
                    pool.tensor_copy(ring[:, lot, 2 * D + 1:ROW], ends[0][:, bass.ds(turn * RING + h * BT, BT), :])
                    pool.tensor_copy(sidx[:, lot], pos[0][:, bass.ds(turn * RING + h * BT, BT)])\
                        .then_inc(S["s_idx"], 1)
                    pool.wait_ge(S["s_idx"], turn * 2 + h + 1)
                    hold(pool)
                    for k in range(h * BT, (h + 1) * BT):
                        pool.indirect_dma_start(
                            out=payload, out_offset=bass.IndirectOffsetOnAxis(ap=sidx[:, k:k + 1], axis=0),
                            in_=ring[:, k, D:ROW], in_offset=None).then_inc(s_row[k], 16)
            pool.wait_ge(s_pay[0], SCAT_TURNS * 16 + 16)
            pool.wait_ge(s_pay[1], SCAT_TURNS * 16 + 16)
            j = SCAT_TURNS * RING
            pool.tensor_copy(ring[:, 0:BT + 1, 2 * D + 1:ROW], ends[0][:, j:j + BT + 1, :])
            pool.tensor_copy(sidx[:, 0:BT + 1], pos[0][:, j:j + BT + 1]).then_inc(S["s_idx"], 2)
            pool.wait_ge(S["s_idx"], scat)
            for k in range(BT + 1):
                n = P if k < BT else ER
                pool.indirect_dma_start(
                    out=payload, out_offset=bass.IndirectOffsetOnAxis(ap=sidx[0:n, k:k + 1], axis=0),
                    in_=ring[0:n, k, D:ROW], in_offset=None).then_inc(s_row[k], 16)

            pool.wait_ge(S["xn1_stored"], 16)
            gathers(0, xn_table, D, lambda turn, h: ring[:, h * BT:(h + 1) * BT, ROW - 1],
                    lambda turn, h: (pool.wait_ge(s_pay[h], turn * 16 + 16 + 16 * (SCAT_TURNS + 1)),
                                     free(pool, 0, turn, h)))

            pool.wait_ge(S["pos_ready"], 2)
            pool.wait_ge(S["meta_in"], 16)
            scatter_dst_turns(0, SCAT_TURNS)
            for h in range(2):
                pool.wait_ge(s_dst[h], SCAT_TURNS * 16 * BT)
            pool.tensor_copy(stage[:, 0:BT + 1, :], ends[1][:, j:j + BT + 1, :])
            pool.tensor_copy(sidx[:, 0:BT + 1], pos[1][:, j:j + BT + 1]).then_inc(S["s_idx"], 2)
            pool.wait_ge(S["s_idx"], scat + 2 * TURNS + scat)
            for k in range(BT + 1):
                n = P if k < BT else ER
                pool.indirect_dma_start(
                    out=dst_meta, out_offset=bass.IndirectOffsetOnAxis(ap=sidx[0:n, k:k + 1], axis=0),
                    in_=stage[0:n, k, :], in_offset=None).then_inc(s_dst[k // BT], 16)

            pool.wait_ge(S["ky_stored"], 16 * NG)
            pool.wait_ge(S["n1_q"], NG)
            gathers(1, ky_table, KY, lambda turn, h: meta_s[:, bass.ds(turn * RING + h * BT, BT), 1],
                    lambda turn, h: free(pool, 1, turn, h))
            pool.wait_ge(S["meta_in"], 32)
            pool.wait_ge(S["n3_st"], 16 * NG)
            pool.wait_ge(S["zeroed"], 3)
            gathers(2, h2_table, D, lambda turn, h: meta_d[:, bass.ds(turn * RING + h * BT, BT), 1],
                    lambda turn, h: free(pool, 2, turn, h))
            pool.wait_ge(S["n4_st"], 16)
            pool.wait_ge(S["zeroed"], 4)
            gathers(3, h3_table, D, lambda turn, h: meta_d[:, bass.ds(turn * RING + h * BT, BT), 1],
                    lambda turn, h: free(pool, 3, turn, h))

        @block.vector
        def _(dve):
            chain = Chain(dve, dve_step)
            v = nc.vector

            def bucket(which):
                dve.wait_ge(s_keys, 32 + 32 * which)
                chain(v.tensor_scalar(hi_i, key_i, 7, None, ALU.arith_shift_right))
                chain(v.tensor_scalar(lo_i, key_i, P - 1, None, ALU.bitwise_and))
                if which == 1:
                    dve.wait_ge(S["meta_in"], 16)
                v.tensor_copy(ends[which][:, :, 0], lo_i)
                v.tensor_copy(ends[which][:, :, 1], oth_i)
                chain(v.tensor_copy(hi, hi_i))
                chain(v.memset(pos[which], 0.0))
                with dve.Fori(0, NB) as b:
                    chain.loop(b, 1)
                    a = CONST["blocks"][0]
                    chain(v.tensor_scalar(csum, hi, cst[:, bass.ds(b + a, 1)], 0.0, ALU.is_equal, ALU.add,
                                          accum_out=cnt[:, bass.ds(b, 1)]))
                chain.end(NB)
                v.memset(st[:, 0:1], 0.0).then_inc(S["cnt_done"], 1)
                dve.wait_ge(S["totals"], which + 1)
                chain(v.tensor_scalar(chint[0:NB, 0:1], psC[0:NB, 0:1], float(P - 1), None, ALU.add))
                chain(v.tensor_scalar(chint[0:NB, 1:2], chint[0:NB, 0:1], 7, None, ALU.arith_shift_right))
                chain(v.tensor_scalar(chcol[0:NB, 0:1], chint[0:NB, 1:2], 1.0, None, ALU.max))
                v.tensor_scalar(chb[0:NB, :], c_("ones")[0:NB, :], chcol[0:NB, 0:1], float(P), ALU.mult, ALU.mult)\
                    .then_inc(S["slots_in"], 1)
                dve.wait_ge(S["slots"], which + 1)
                chain(v.tensor_scalar(tm1[:, :], psC[:, 64:64 + NB], 1.0, None, ALU.subtract))
                chain(v.tensor_copy(endt[:, :], psC[:, 128:128 + NB]))
                chain(v.tensor_copy(chcol[0:NB, 1:2], psC[0:NB, 256:257]))
                v.tensor_scalar(ge, c_("chunks")[0:NB, :], chcol[0:NB, 1:2], None, ALU.is_ge)\
                    .then_inc(S["ge_ready"], 1)
                if which == 0:
                    chain(v.tensor_scalar(tt[:, :], psC[:, 192:192 + NB], c_("part"), None, ALU.add))
                    chain(v.tensor_tensor(cnt[:, :], tt[:, :], endt[:, :], ALU.is_ge))
                    chain(v.scalar_tensor_tensor(padidx[:, 0:NB], cnt[:, :], FAR, tt[:, :], ALU.mult, ALU.add))
                    chain(v.tensor_scalar(chcol[:, 2:3], endt[:, NB - 1:NB], c_("part"), None, ALU.add))
                    v.tensor_scalar(padidx[:, NB:NB + TAILS], c_("chunks", 0, TAILS), float(P), chcol[:, 2:3],
                                    ALU.mult, ALU.add).then_inc(S["pad_ready"], 1)
                dve.wait_ge(S["blk_psum"], which + 1)
                chain(v.tensor_scalar(blk[which], psA[0:1, 0:CHUNKS], float(NB - 1), None, ALU.min))
                with dve.Fori(0, NB) as b:
                    chain.loop(b, 3)
                    a = CONST["blocks"][0]
                    chain(v.tensor_scalar(mask, hi, cst[:, bass.ds(b + a, 1)], None, ALU.is_equal))
                    chain(v.tensor_tensor_scan(csum, one_e, mask, tm1[:, bass.ds(b, 1)], ALU.mult, ALU.add))
                    hold(dve)
                    chain(v.copy_predicated(pos[which], mask, csum))
                chain.end(NB)
                v.memset(st[:, 0:1], 0.0).then_inc(S["pos_ready"], 1)

            def norm(at, src3, z, sq):
                hold(dve)
                chain(v.reduce_sum(nrm[:, 0:GB], src3, AX.X))
                chain(v.scalar_tensor_tensor(z, along(nrm[:, 0:GB], D), -1.0 / D, src3, ALU.mult, ALU.add))
                chain(v.tensor_tensor(sq, z, z, ALU.mult))
                chain(v.reduce_sum(nrm[:, 8:8 + GB], sq, AX.X))
                v.tensor_scalar(nrm[:, 16:16 + GB], nrm[:, 8:8 + GB], 1.0 / D, EPS, ALU.mult, ALU.add)\
                    .then_inc(S["s_var"], 1)
                dve.wait_ge(S["s_std"], at + 1)
                chain(v.reciprocal(nrm[:, 0:GB], nrm[:, 24:24 + GB]))
                chain(v.tensor_tensor(z, z, along(nrm[:, 0:GB], D), ALU.mult))

            def root(at, value, out_):
                n = value.shape[1]
                v.tensor_copy(rootv[:, 0:n], value).then_inc(S["s_root"], 1)
                dve.wait_ge(S["s_rooted"], at)
                chain(v.reciprocal(out_, rootv[:, 64:64 + n]))

            def batch_onehot(meta, turn, h, waits):
                waits()
                key = meta[:, bass.ds(turn * RING + h * BT, BT), 0]
                v.tensor_tensor(onehot[:, h * BT:(h + 1) * BT, :], over(c_("iota"), BT), along(key, P),
                                ALU.is_equal).then_inc(s_oh[h], 1)

            def load_blocks(which, turn, h, hold):
                regs = hold
                dve.load(regs, blk[which][0:1, bass.ds(turn * RING + h * BT, BT)])
                return [dve.snap(r, min_val=0, max_val=NB - 1) for r in regs]

            regs = [dve.alloc_register(f"dve_blk{k}") for k in range(BT)]

            def plain_pass(n, meta, which, first, waits, add):
                with dve.Fori(0, TURNS) as turn:
                    if n == 0:
                        chain.loop(turn, 2 * BT + 2)
                    for h in range(2):
                        if n == 0:
                            dve.wait_ge(s_pay[h], turn * 16 + 16 + 16 * (SCAT_TURNS + 1))
                            chain(v.tensor_copy(meta[:, bass.ds(turn * RING + h * BT, BT), :],
                                                ring[:, h * BT:(h + 1) * BT, 2 * D + 1:ROW]))
                        batch_onehot(meta, turn, h, lambda: free(dve, n, turn, h))
                        bs = load_blocks(which, turn, h, regs)
                        for k in range(BT):
                            dve.wait_ge(S["s_ps"], product(n, turn, h, k))
                            c = turn * RING + h * BT + k + CHUNKS * plain_no[n]
                            add((h * BT + k) % BANKS, bs[k], c)
                if n == 0:
                    chain.end(TURNS)
                dve.wait_ge(S["s_free"], BANKS + CHUNKS * (plain_no[n] + 1))

            plain_no = {0: 0, 2: 1, 3: 2}

            v.memset(padrow[:, :], 0.0)
            v.memset(rootv[:, :], 1.0)
            chain(v.memset(one_e, 1.0))
            chain(v.memset(padrow[:, D + 1:D + 2], -1.0))
            v.memset(meta_d[:, :, 1], 0.0)
            v.memset(meta_d[:, :, 0], -1.0).then_inc(S["meta_pre"], 1)
            chain(v.memset(ring[:, :, 2 * D:2 * D + 1], 1.0))
            dve.wait_ge(s_const, 48)
            bucket(0)

            dve.wait_ge(s_x, 16)
            with dve.Fori(0, NG) as t:
                chain.loop(t, 7)
                hg = hst[:, bass.ds(t * GB, GB), :]
                norm(t, hg, g3(early[0]), g3(early[1]))
                chain(v.tensor_scalar(hg, g3(early[0]), 0.0, None, ALU.max))
            chain.end(NG)
            v.reduce_sum(early[2][:, 0:D], hst[:, :, :].rearrange("p b d -> p d b"), AX.X).then_inc(S["h0_sum"], 1)
            dve.wait_ge(S["h0_col"], 1)
            chain(v.scalar_tensor_tensor(col[:, 0:1], psC[:, 0:1], 1.0 / N, w_("g_token"), ALU.mult, ALU.add))
            v.tensor_scalar(chb[:, :], c_("ones"), col[:, 0:1], None, ALU.mult).then_inc(S["g_col"], 1)
            dve.wait_ge(S["g_row"], 1)
            chain(v.tensor_tensor(early[2][:, 0:D], psC[:, 64:64 + D], r_("Wg_b"), ALU.add))
            chain(v.tensor_tensor(hst[:, :, :], hst[:, :, :], over(early[2][:, 0:D], NB), ALU.add))
            with dve.Fori(0, NG) as t:
                chain.loop(t, 7)
                xg = xn1[:, bass.ds(t * GB, GB), :]
                norm(t + NG, hst[:, bass.ds(t * GB, GB), :], g3(early[0]), g3(early[1]))
                chain(v.tensor_tensor(g3(early[1]), g3(early[0]), over(r_("ln1_g"), GB), ALU.mult))
                v.tensor_tensor(xg, g3(early[1]), over(r_("ln1_b"), GB), ALU.add).then_inc(S["xn1_ready"], 1)
            chain.end(NG)
            bucket(1)
            chain(v.memset(big[:, NP:2 * NP], 0.0))
            chain(v.memset(att[:, :], 0.0))
            chain(v.tensor_scalar(col[:, 1:2], r_("eps"), 1.0, None, ALU.add))
            dve.sem_inc(S["s_free"], BANKS)

            def add1(bank, b, c):
                p = ps[:, (1 + bank) * 512:(1 + bank) * 512 + D + SW]
                a = agg[:, bass.ds(b, 1), :].rearrange("p a d -> p (a d)")
                chain(v.tensor_tensor(a, a, p[:, 0:D], ALU.add))
                a = att3[:, bass.ds(b, 1), :].rearrange("p a d -> p (a d)")
                dve.wait_ge(S["s_free"], BANKS + c)
                v.tensor_tensor(a, a, p[:, D:D + SW], ALU.add).then_inc(S["s_free"], 1)
            plain_pass(0, meta_s, 0, 0, None, add1)

            chain(v.tensor_copy(deg[:, :], att3[:, :, D]))
            with dve.Fori(0, NG) as t:
                chain.loop(t, 9 + 3)
                T = temps
                hg = hst[:, bass.ds(t * GB, GB), :]
                dve.wait_ge(S["n1_msg"], t + 1)
                chain(v.scalar_tensor_tensor(g3(T[2]), xn1[:, bass.ds(t * GB, GB), :], col[:, 1:2],
                                             g3(psB[:, 0:GW]), ALU.mult, ALU.add))
                chain(v.tensor_tensor(g3(T[3]), over(r_("msg_b"), GB), along(deg[:, bass.ds(t * GB, GB)], D), ALU.mult))
                v.tensor_tensor(T[2], T[2], T[3], ALU.add).then_inc(S["n1_t"], 1)
                dve.wait_ge(S["n1_lin"], t + 1)
                chain(v.tensor_tensor(g3(T[3]), g3(psB[:, 0:GW]), over(r_("lin_b"), GB), ALU.add))
                chain(v.scalar_tensor_tensor(hg, g3(T[3]), 0.0, hg, ALU.max, ALU.add))
                norm(t + 2 * NG, hg, g3(T[4]), g3(T[5]))
                v.memset(st[:, 40:41], 0.0).then_inc(S["n1_z"], 1)
                dve.wait_ge(S["n1_q"], t + 1)
                dve.wait_ge(S["ky_stored"], t * 16)
                pq = psB[:, 0:GB * HID].rearrange("p (b d) -> p b d", b=GB)
                chain(v.tensor_copy(kyt[:, :, 0:ATTN], pq[:, :, ATTN:2 * ATTN]))
                chain(v.tensor_tensor(kyt[:, :, ATTN:KY], pq[:, :, 2 * ATTN:HID], over(r_("Wy_b"), GB), ALU.add))
                v.memset(st[:, 41:42], 0.0).then_inc(S["n1_ky"], 1)
            chain.end(NG)

            dve.wait_ge(S["n1_q"], NG)
            chain(v.memset(big[:, 0:NB * ACW], 0.0))
            chain(v.memset(ring[:, :, D + 2 * ATTN:D + 2 * ATTN + 1], 1.0))
            chain(v.memset(mrun[:, :], LOW))
            v.memset(mb[:, :], LOW).then_inc(S["zeroed"], 1)
            dve.sem_inc(S["a_free"], ABANKS)
            with dve.Fori(0, TURNS) as turn:
                chain.loop(turn, 2 * 5)
                for h in range(2):
                    bt = turn * 2 + h
                    lot = slice(h * BT, (h + 1) * BT)
                    key = meta_s[:, bass.ds(turn * RING + h * BT, BT), 0]
                    batch_onehot(meta_s, turn, h, lambda: free(dve, 1, turn, h))
                    chain(v.tensor_scalar(neg[:, :], key, 0.0, LOW, ALU.is_lt, ALU.mult))
                    dve.wait_ge(S["a_q"], bt + 1)
                    for k in range(h * BT, (h + 1) * BT):
                        dve.wait_ge(s_row[k], turn * 16 + 16 + row_base(k, 1))
                    v.tensor_tensor(zt, ps[:, 0:BT * ATTN].rearrange("p (c a) -> p c a", a=ATTN),
                                    ring[:, lot, 0:ATTN], ALU.add).then_inc(S["a_z"], 1)
                    dve.wait_ge(S["a_e"], bt + 1)
                    chain(v.tensor_tensor(pr, ring[:, lot, KY:KY + ATTN], over(r_("phi"), BT), ALU.mult))
                    chain(v.reduce_sum(sc[:, :], pr, AX.X))
                    chain(v.tensor_tensor(sc[:, :], sc[:, :], neg[:, :], ALU.add))
                    v.reduce_max(st[:, 24:25], sc[:, :], AX.X).then_inc(S["a_bm"], 1)
                    dve.wait_ge(S["a_mt"], bt + 1)
                    chain(v.reduce_max(st[0:1, 25:26], ps[0:1, 4 * 512 + 256:4 * 512 + 384], AX.X))
                    v.tensor_tensor(mrun[0:1, 0:1], mrun[0:1, 0:1], st[0:1, 25:26], ALU.max)\
                        .then_inc(S["a_mr"], 1)
                    bs = load_blocks(0, turn, h, regs)
                    dve.wait_ge(S["a_w"], bt + 1)
                    for k in range(BT):
                        c = turn * RING + h * BT + k
                        dve.wait_ge(S["s_ps"], product(1, turn, h, k))
                        dve.wait_ge(S["a_free"], ABANKS + c)
                        a = acc_a[:, bass.ds(bs[k], 1), 0:AGW].rearrange("p a d -> p (a d)")
                        m = acc_a[:, bass.ds(bs[k], 1), AGW:ACW].rearrange("p a d -> p (a d)")
                        p = ps[:, (5 + k % 2) * 512:(5 + k % 2) * 512 + AGW]
                        v.tensor_copy(m, mb[:, h:h + 1])
                        if k == 0:
                            ins = v.scalar_tensor_tensor(a, a, mb[:, 4 + h:5 + h], p, ALU.mult, ALU.add)
                        else:
                            ins = v.tensor_tensor(a, a, p, ALU.add)
                        ins.then_inc(S["a_free"], 1)
            chain.end(TURNS)
            dve.wait_ge(S["a_free"], ABANKS + CHUNKS)
            chain(v.memset(st[:, 42:43], 0.0))
            v.memset(st[:, 43:44], 0.0).then_inc(S["zeroed"], 1)

            chain(v.tensor_scalar(deg[:, :], deg[:, :], 1.0, None, ALU.max))
            chain(v.reciprocal(tt[:, :], deg[:, :]))
            root(1, deg[:, :], outn[:, :])
            v.tensor_scalar(cnt[:, :], acc_a[:, :, AGW], mb[:, 1:2], None, ALU.subtract).then_inc(S["n2_sc"], 1)
            dve.wait_ge(S["n2_sce"], 1)
            dve.wait_ge(S["n2_ub"], 1)
            v.tensor_tensor(col[:, 2:3], psC[:, 0:1], w_("b0"), ALU.add).then_inc(S["n2_ubc"], 1)
            with dve.Fori(0, NG) as t:
                chain.loop(t, 26)
                T = temps
                gs = bass.ds(t * GB, GB)
                hg, xg = hst[:, gs, :], xs[:, gs, :]
                chain(v.tensor_tensor(st[:, 40:40 + GB], acc_a[:, gs, AGW - 1], endt[:, gs], ALU.mult))
                chain(v.tensor_scalar(st[:, 48:48 + GB], st[:, 40:40 + GB], 1e-9, None, ALU.add))
                chain(v.reciprocal(st[:, 40:40 + GB], st[:, 48:48 + GB]))
                chain(v.tensor_tensor(st[:, 48:48 + GB], st[:, 40:40 + GB], endt[:, gs], ALU.mult))
                dve.wait_ge(S["n2_we"], t + 1)
                chain(v.tensor_tensor(g3(T[2]), g3(psB[:, 0:GW]), acc_a[:, gs, 0:D], ALU.add))
                chain(v.tensor_tensor(g3(T[3]), over(r_("We_b"), GB), along(acc_a[:, gs, AGW - 1], D), ALU.mult))
                chain(v.tensor_tensor(T[2], T[2], T[3], ALU.add))
                chain(v.tensor_tensor(g3(T[2]), g3(T[2]), along(st[:, 48:48 + GB], D), ALU.mult))
                chain(v.tensor_tensor(hg, hg, g3(T[2]), ALU.add))
                norm(t * 2 + 3 * NG, hg, g3(T[4]), g3(T[3]))
                v.memset(st[:, 60:61], 0.0).then_inc(S["n2_z"], 1)
                dve.wait_ge(S["n2_ffn"], t + 1)
                chain(v.tensor_tensor(g3(T[2]), g3(psA[:, 0:GW]), over(r_("ffn_b2"), GB), ALU.add))
                chain(v.tensor_tensor(g3(T[2]), g3(T[2]), hg, ALU.add))
                dve.wait_ge(S["n2_xg"], t * 16 + 16)
                chain(v.tensor_tensor(T[2], T[2], xgrp, ALU.add))
                chain(v.tensor_tensor(g3(T[7]), att3[:, gs, 0:D], along(tt[:, gs], D), ALU.mult))
                chain(v.tensor_copy(xg, g3(T[2])))
                norm(t * 2 + 3 * NG + 1, g3(T[2]), g3(T[4]), g3(T[3]))
                v.tensor_scalar(T[4], T[4], 0.0, None, ALU.max).then_inc(S["n2_x"], 1)
            chain.end(NG)

            def batch_norm(i, arr):
                n = 0
                for lo in range(0, N, 512):
                    hi_ = min(lo + 512, N)
                    v.bn_stats(bns[:, n * 6:n * 6 + 6], arr[:, lo:hi_])
                    n += 1
                chain(v.memset(st[:, 60:61], 0.0))
                chain(v.bn_aggr(col[:, 16:18], bns[:, 0:n * 6]))
                chain(v.tensor_scalar(col[:, 17:18], col[:, 17:18], EPS, None, ALU.add))
                root(2 + i, col[:, 17:18], col[:, 18:19])
                a, c = col[:, 4 + 2 * i:5 + 2 * i], col[:, 5 + 2 * i:6 + 2 * i]
                chain(v.tensor_tensor(a, col[:, 18:19], w_(f"g{i}"), ALU.mult))
                chain(v.tensor_tensor(col[:, 19:20], col[:, 16:17], a, ALU.mult))
                chain(v.tensor_tensor(c, w_(f"bt{i}"), col[:, 19:20], ALU.subtract))
                v.memset(st[:, 60:61], 0.0).then_inc(S["bn_ac"], 1)

            dve.wait_ge(S["n2_r0"], NG)
            batch_norm(0, h_f)
            for i, arr in ((1, big[:, 0:NP]), (2, big[:, NP:2 * NP])):
                dve.wait_ge(S["bn_bias"], i)
                v.tensor_tensor(col[:, 10 + i:11 + i], psC[:, 0:1], w_(f"b{i}"), ALU.add)
                v.tensor_scalar(chb[:, :], w_(f"W{i}"), col[:, 2 + 2 * i:3 + 2 * i], None, ALU.mult)\
                    .then_inc(S["bn_w"], 1)
                dve.wait_ge(S["l1_relu"], NG * i)
                batch_norm(i, arr)

            with dve.Fori(0, NG) as t:
                chain.loop(t, 8)
                T = temps
                gs = bass.ds(t * GB, GB)
                xg, hg = xs[:, gs, :], hst[:, gs, :]
                dve.wait_ge(S["n3_T"], t + 1)
                chain(v.tensor_tensor(xg, xg, g3(psA[:, 0:GW]), ALU.add))
                norm(t + 5 * NG, xg, g3(T[2]), g3(T[3]))
                chain(v.tensor_scalar(hg, g3(T[2]), 0.0, None, ALU.max))
                dve.wait_ge(S["n3_st"], t * 16)
                v.tensor_tensor(g3(T[4]), hg, along(outn[:, gs], D), ALU.mult).then_inc(S["n3_hs"], 1)
            chain.end(NG)

            def add3(bank, b, c):
                p = ps[:, (1 + bank) * 512:(1 + bank) * 512 + SW]
                a = acc_p[:, bass.ds(b, 1), :].rearrange("p a d -> p (a d)")
                dve.wait_ge(S["s_free"], BANKS + c)
                v.tensor_tensor(a, a, p, ALU.add).then_inc(S["s_free"], 1)

            chain(v.memset(big[:, 0:NB * SW], 0.0))
            dve.wait_ge(S["n3_st"], 16 * NG)
            v.memset(ring[:, :, D:D + 1], 1.0).then_inc(S["zeroed"], 1)
            dve.wait_ge(S["meta_in"], 32)
            plain_pass(2, meta_d, 1, 2 * TURNS, None, add3)
            chain(v.tensor_copy(deg[:, :], acc_p[:, :, D]))
            chain(v.tensor_scalar(tt[:, :], deg[:, :], 1.0, None, ALU.max))
            root(5, tt[:, :], inn[:, :])

            with dve.Fori(0, NG) as t:
                chain.loop(t, 3 + 6 + 1)
                T = temps
                gs = bass.ds(t * GB, GB)
                xg, hg = xs[:, gs, :], hst[:, gs, :]
                dve.wait_ge(S["n4_in"], t + 1)
                v.tensor_tensor(T[2], T[0], T[3], ALU.mult).then_inc(S["n4_m"], 1)
                dve.wait_ge(S["n4_mm"], t + 1)
                chain(v.tensor_tensor(g3(T[7]), g3(psB[:, 0:GW]), along(inn[:, gs], D), ALU.mult))
                chain(v.tensor_tensor(T[7], T[7], psB[:, 1024:1024 + GW], ALU.add))
                chain(v.tensor_tensor(xg, xg, g3(T[7]), ALU.add))
                norm(t + 6 * NG, xg, g3(T[7]), g3(T[4]))
                chain(v.tensor_scalar(hg, g3(T[7]), 0.0, None, ALU.max))
                v.memset(st[:, 60:61], 0.0).then_inc(S["n4_h"], 1)
            chain.end(NG)
            v.reduce_sum(chb[:, :], hst[:, 0:NB - 1, :].rearrange("p b d -> p d b"), AX.X).then_inc(S["n4_sum"], 1)
            dve.wait_ge(S["n4_mean"], 1)
            chain(v.tensor_scalar(col[:, 3:4], psC[:, 0:1], 1.0 / N, None, ALU.mult))
            chain(v.tensor_tensor(col[:, 20:23], w_("b_ih"), w_("b_hh"), ALU.add))
            v.tensor_scalar(col[:, 24:27], col[:, 20:23], 0.5, None, ALU.mult).then_inc(S["n4_meanc"], 1)
            chain(v.memset(big[:, 0:NB * SW], 0.0))
            dve.wait_ge(S["n4_st"], 16)
            v.memset(ring[:, :, D:D + 1], 1.0).then_inc(S["zeroed"], 1)
            plain_pass(3, meta_d, 1, 3 * TURNS, None, add3)

            with dve.Fori(0, NG) as t:
                chain.loop(t, 14)
                T = temps
                gs = bass.ds(t * GB, GB)
                dve.wait_ge(S["n5_m"], t + 1)
                chain(v.tensor_tensor(g3(T[4]), over(r_("b_msg"), GB), along(deg[:, gs], D), ALU.mult))
                v.tensor_tensor(T[2], T[4], psB[:, 0:GW], ALU.add).then_inc(S["n5_msg"], 1)
                dve.wait_ge(S["n5_rza"], t + 1)
                v.tensor_scalar(T[5], T[5], 0.5, 0.5, ALU.mult, ALU.add)
                chain(v.tensor_scalar(T[4], T[4], 0.5, 0.5, ALU.mult, ALU.add))
                dve.wait_ge(S["n5_nn"], t + 1)
                chain(v.scalar_tensor_tensor(T[6], psB[:, 1024:1024 + GW], w_("b_hh", 2, 3), T[4], ALU.add, ALU.mult))
                v.tensor_tensor(T[6], T[6], psB[:, 0:GW], ALU.add).then_inc(S["n5_npre"], 1)
                dve.wait_ge(S["n5_n"], t + 1)
                chain(v.tensor_tensor(T[3], T[1], T[0], ALU.subtract))
                chain(v.tensor_tensor(T[3], T[3], T[5], ALU.mult))
                v.tensor_tensor(T[3], T[3], T[0], ALU.add).then_inc(S["n5_hn"], 1)
                dve.wait_ge(S["n5_hnT"], t + 1)
                norm(t + 7 * NG, g3(psA[:, 0:GW]), g3(T[6]), g3(T[4]))
                chain(v.tensor_tensor(g3(T[6]), g3(T[6]), over(r_("gamma"), GB), ALU.mult))
                chain(v.tensor_tensor(g3(T[6]), g3(T[6]), over(r_("beta"), GB), ALU.add))
                chain(v.tensor_tensor(T[6], T[6], T[2], ALU.add))
                dve.wait_ge(S["n5_st"], t * 16)
                v.tensor_tensor(g3(T[7]), g3(T[6]), xs[:, gs, :], ALU.add).then_inc(S["n5_out"], 1)
            chain.end(NG)

        @block.scalar
        def _(act):
            chain = Chain(act, act_step)
            a = nc.scalar

            def copy(out_, in_):
                return a.activation(out_, in_, ACT.Copy)

            def std(at):
                act.wait_ge(S["s_var"], at + 1)
                a.activation(nrm[:, 24:24 + GB], nrm[:, 16:16 + GB], ACT.Sqrt).then_inc(S["s_std"], 1)

            def rooted(at):
                act.wait_ge(S["s_root"], at)
                a.activation(rootv[:, 64:64 + NB], rootv[:, 0:NB], ACT.Sqrt).then_inc(S["s_rooted"], 1)

            with act.Fori(0, 2 * NG) as t:
                std(t)

            act.wait_ge(S["s_free"], BANKS + CHUNKS)
            with act.Fori(0, NG) as t:
                T = temps
                act.wait_ge(S["n1_lin"], t)
                copy(g3(T[0]), agg[:, bass.ds(t * GB, GB), :]).then_inc(S["n1_agg"], 1)
                act.wait_ge(S["n1_aggT"], t + 1)
                copy(T[1], psA[:, 0:GW]).then_inc(S["n1_aggTc"], 1)
                act.wait_ge(S["n1_tT"], t + 1)
                copy(T[0], psA[:, 0:GW]).then_inc(S["n1_tTc"], 1)
                std(t + 2 * NG)
                act.wait_ge(S["n1_zT"], t + 1)
                a.activation(T[1], psA[:, 0:GW], ACT.Identity, bias=w_("ln2_b"), scale=w_("ln2_g"))\
                    .then_inc(S["n1_zTc"], 1)
                act.wait_ge(S["n1_qky"], t + 1)
                pq = psB[:, 0:GB * HID].rearrange("p (b d) -> p b d", b=GB)
                copy(qst[:, bass.ds(t * GB, GB), :], pq[:, :, 0:ATTN]).then_inc(S["n1_q"], 1)

            act.wait_ge(S["zeroed"], 1)
            with act.Fori(0, TURNS) as turn:
                chain.loop(turn, 2 * 3)
                for h in range(2):
                    bt = turn * 2 + h
                    lot = slice(h * BT, (h + 1) * BT)
                    act.wait_ge(S["a_T"], bt + 1)
                    act.wait_ge(S["a_q"], bt)
                    copy(onehotT[:, :], ps[:, 1024:1024 + BT * P]).then_inc(S["a_Tc"], 1)
                    act.wait_ge(S["a_z"], bt + 1)
                    a.activation(ring[:, lot, KY:KY + ATTN], zt, ACT.Tanh).then_inc(S["a_e"], 1)
                    act.wait_ge(S["a_mb"], bt + 1)
                    chain(copy(mb[:, h:h + 1], ps[:, 4 * 512 + 384:4 * 512 + 385]))
                    chain(a.activation(mb[:, 2 + h:3 + h], mb[:, h:h + 1], ACT.Copy, scale=-1.0))
                    a.activation(mb[:, 4 + h:5 + h], mb[:, 1 - h:2 - h], ACT.Exp, bias=mb[:, 2 + h:3 + h])
                    chain(a.activation(wexp[:, :], sc[:, :], ACT.Exp, bias=mb[:, 2 + h:3 + h]))
                    for k in range(BT):
                        o_ = onehot[:, h * BT + k, :]
                        ins = a.activation(o_, o_, ACT.Copy, scale=wexp[:, k:k + 1])
                    ins.then_inc(S["a_w"], 1)
            chain.end(TURNS)

            act.wait_ge(S["zeroed"], 2)
            rooted(1)
            act.wait_ge(S["n2_sc"], 1)
            a.activation(endt[:, :], cnt[:, :], ACT.Exp).then_inc(S["n2_sce"], 1)
            act.wait_ge(S["n2_ubc"], 1)
            with act.Fori(0, NG) as t:
                T = temps
                gs = bass.ds(t * GB, GB)
                act.wait_ge(S["n2_o0"], t)
                ue = T[0][:, 0:GB * ATTN]
                copy(ue.rearrange("p (b d) -> p b d", b=GB), acc_a[:, gs, D:D + ATTN]).then_inc(S["n2_ue"], 1)
                act.wait_ge(S["n2_ueT"], t + 1)
                copy(T[1][0:ATTN, :], psA[0:ATTN, 0:GW]).then_inc(S["n2_ueTc"], 1)
                std(t * 2 + 3 * NG)
                act.wait_ge(S["n2_zT"], t + 1)
                a.activation(T[1], psA[:, 0:GW], ACT.Identity, bias=w_("ln3_b"), scale=w_("ln3_g"))\
                    .then_inc(S["n2_zTc"], 1)
                act.wait_ge(S["n2_hid"], t + 1)
                for k in range(2):
                    ins = a.activation(T[5 + k], psB[:, 1024 * k:1024 * k + GW], ACT.Relu,
                                       bias=w_("ffn_b1", k, k + 1))
                ins.then_inc(S["n2_relu"], 1)
                std(t * 2 + 3 * NG + 1)
                act.wait_ge(S["n2_h1T"], t + 1)
                copy(T[0], psA[:, 0:GW]).then_inc(S["n2_h1Tc"], 1)
                act.wait_ge(S["n2_veT"], t + 1)
                copy(T[1], psA[:, 0:GW]).then_inc(S["n2_veTc"], 1)
                act.wait_ge(S["n2_o0"], t + 1)
                a.activation(h_f[:, bass.ds(t * GW, GW)], psB[:, 0:GW], ACT.Relu, bias=col[:, 2:3])\
                    .then_inc(S["n2_r0"], 1)

            rooted(2)
            for i in (1, 2):
                with act.Fori(0, NG) as t:
                    act.wait_ge(S["l1_mm"], t + 1 + NG * (i - 1))
                    a.activation(big[:, bass.ds(t * GW + (i - 1) * NP, GW)], psB[:, 0:GW], ACT.Relu,
                                 bias=col[:, 10 + i:11 + i]).then_inc(S["l1_relu"], 1)
                rooted(2 + i)
            act.wait_ge(S["bn_ac"], 3)
            with act.Fori(0, NG) as t:
                act.wait_ge(S["n3_T"], t)
                a.activation(temps[0], big[:, bass.ds(t * GW + NP, GW)], ACT.Identity, bias=col[:, 9:10],
                             scale=col[:, 8:9]).then_inc(S["n3_o"], 1)
                std(t + 5 * NG)

            act.wait_ge(S["s_free"], BANKS + 2 * CHUNKS)
            rooted(5)
            with act.Fori(0, NG) as t:
                T = temps
                gs = bass.ds(t * GB, GB)
                act.wait_ge(S["n4_mm"], t)
                copy(g3(T[0]), acc_p[:, gs, 0:D])
                copy(g3(T[3]), hst[:, gs, :]).then_inc(S["n4_in"], 1)
                for i, d in enumerate((1, 5, 6)):
                    act.wait_ge(S["n4_T"], t * 3 + i + 1)
                    copy(T[d], psA[:, 0:GW]).then_inc(S["n4_Tc"], 1)
                std(t + 6 * NG)

            act.wait_ge(S["s_free"], BANKS + 3 * CHUNKS)
            act.wait_ge(S["n4_meanc"], 1)
            with act.Fori(0, NG) as t:
                T = temps
                gs = bass.ds(t * GB, GB)
                act.wait_ge(S["n5_hnT"], t)
                copy(g3(T[0]), acc_p[:, gs, 0:D]).then_inc(S["n5_s"], 1)
                act.wait_ge(S["n5_sT"], t + 1)
                copy(T[1], psA[:, 0:GW]).then_inc(S["n5_sTc"], 1)
                copy(g3(T[3]), hst[:, gs, :]).then_inc(S["n5_hc"], 1)
                act.wait_ge(S["n5_T"], t * 2 + 1)
                a.activation(T[0], psA[:, 0:GW], ACT.Identity, bias=col[:, 3:4]).then_inc(S["n5_Tc"], 1)
                act.wait_ge(S["n5_T"], t * 2 + 2)
                copy(T[1], psA[:, 0:GW]).then_inc(S["n5_Tc"], 1)
                act.wait_ge(S["n5_rz"], t + 1)
                for k in range(2):
                    ins = a.activation(T[4 + k], psB[:, 1024 * k:1024 * k + GW], ACT.Tanh, scale=0.5,
                                       bias=col[:, 24 + k:25 + k])
                ins.then_inc(S["n5_rza"], 1)
                act.wait_ge(S["n5_npre"], t + 1)
                a.activation(T[0], T[6], ACT.Tanh, bias=w_("b_ih", 2, 3)).then_inc(S["n5_n"], 1)
                std(t + 7 * NG)

        @block.tensor
        def _(pe):
            m = nc.tensor
            ident = c_("ident")
            PIECES = ((0, 512), (512, GW))

            def turnT(src_, dst_=psA, n=P):
                for j in range(GB):
                    ins = m.transpose(dst_[0:n, j * P:(j + 1) * P], src_[:, j * n:(j + 1) * n], ident)
                return ins

            def nodes(dst_, pairs, width=P, stride=P):
                for j in range(GB):
                    for i, (l, r) in enumerate(pairs):
                        ins = m.matmul(dst_[:, j * stride:j * stride + width], l[:, j * P:(j + 1) * P], r,
                                       start=i == 0, stop=i == len(pairs) - 1)
                return ins

            def feats(dst_, pairs):
                for lo, hi_ in PIECES:
                    for i, (l, r) in enumerate(pairs):
                        ins = m.matmul(dst_[:, lo:hi_], l, r(lo, hi_), start=i == 0, stop=i == len(pairs) - 1)
                return ins

            def bucket(which):
                pe.wait_ge(S["cnt_done"], which + 1)
                m.matmul(psC[0:NB, 0:1], cnt[:, :], c_("ones", 0, 1), start=True, stop=True)\
                    .then_inc(S["totals"], 1)
                pe.wait_ge(S["slots_in"], which + 1)
                ch = chb[0:NB, :]
                before, upto = c_("before")[0:NB, :], c_("upto")[0:NB, :]
                m.matmul(psC[:, 64:64 + NB], ch, before, start=True, stop=False)
                m.matmul(psC[:, 64:64 + NB], c_("strict"), cnt[:, :], start=False, stop=True)
                m.matmul(psC[:, 128:128 + NB], ch, upto, start=True, stop=True)
                m.matmul(psC[:, 192:192 + NB], ch, before, start=True, stop=False)
                m.matmul(psC[:, 192:192 + NB], c_("ones"), cnt[:, :], start=False, stop=True)
                m.matmul(psC[0:NB, 256:257], upto, chcol[0:NB, 0:1], start=True, stop=True).then_inc(S["slots"], 1)
                pe.wait_ge(S["ge_ready"], which + 1)
                for lo in range(0, CHUNKS, 512):
                    hi_ = min(lo + 512, CHUNKS)
                    ins = m.matmul(psA[0:1, lo:hi_], c_("ones", 0, 1)[0:NB, :], ge[:, lo:hi_], start=True, stop=True)
                ins.then_inc(S["blk_psum"], 1)

            regs = [pe.alloc_register(f"pe_blk{k}") for k in range(BT)]

            def plain_pass(n, q, width):
                with pe.Fori(0, TURNS) as turn:
                    for h in range(2):
                        pe.wait_ge(s_oh[h], turn + 1 + n * TURNS)
                        for k in range(BT):
                            slot = h * BT + k
                            pe.wait_ge(s_row[slot], turn * 16 + 16 + row_base(slot, n))
                            pe.wait_ge(S["s_free"], turn * RING + slot + 1 + q * CHUNKS)
                            bank = (1 + slot % BANKS) * 512
                            ins = m.matmul(ps[:, bank:bank + width], onehot[:, slot, :], ring[:, slot, 0:width],
                                           start=True, stop=True)
                            ins.then_inc(S["s_ps"], 1)

            pe.sem_inc(S["s_ps"], RING)
            pe.wait_ge(s_const, 48)
            bucket(0)
            pe.wait_ge(S["h0_sum"], 1)
            m.matmul(psC[:, 0:1], early[2][:, 0:D], c_("ones", 0, 1), start=True, stop=True).then_inc(S["h0_col"], 1)
            pe.wait_ge(S["g_col"], 1)
            m.matmul(psC[:, 64:64 + D], chb[:, :], w_("Wg"), start=True, stop=True).then_inc(S["g_row"], 1)
            bucket(1)
            plain_pass(0, 0, D + SW)

            with pe.Fori(0, NG) as t:
                T = temps
                pe.wait_ge(S["n1_agg"], t + 1)
                turnT(T[0]).then_inc(S["n1_aggT"], 1)
                pe.wait_ge(S["n1_aggTc"], t + 1)
                pe.wait_ge(S["n1_q"], t)
                pe.wait_ge(S["n1_ky"], t)
                nodes(psB, [(T[1], w_("msg"))]).then_inc(S["n1_msg"], 1)
                pe.wait_ge(S["n1_t"], t + 1)
                turnT(T[2]).then_inc(S["n1_tT"], 1)
                pe.wait_ge(S["n1_tTc"], t + 1)
                nodes(psB, [(T[0], w_("lin"))]).then_inc(S["n1_lin"], 1)
                pe.wait_ge(S["n1_z"], t + 1)
                turnT(T[4]).then_inc(S["n1_zT"], 1)
                pe.wait_ge(S["n1_zTc"], t + 1)
                nodes(psB, [(T[1], w_("qky"))], HID, HID).then_inc(S["n1_qky"], 1)

            pe.wait_ge(S["n1_q"], NG)
            pe.wait_ge(S["n1_ky"], NG)
            with pe.Fori(0, TURNS) as turn:
                for h in range(2):
                    bt = turn * 2 + h
                    pe.load(regs, blk[0][0:1, bass.ds(turn * RING + h * BT, BT)])
                    bs = [pe.snap(r, min_val=0, max_val=NB - 1) for r in regs]
                    pe.wait_ge(s_oh[h], turn + 1 + TURNS)
                    pe.wait_ge(S["a_Tc"], bt)
                    for k in range(BT):
                        ins = m.transpose(ps[:, 1024 + k * P:1024 + (k + 1) * P], onehot[:, h * BT + k, :], ident)
                    ins.then_inc(S["a_T"], 1)
                    pe.wait_ge(S["a_Tc"], bt + 1)
                    pe.wait_ge(S["a_z"], bt)
                    for k in range(BT):
                        q = qst[:, bass.ds(bs[k], 1), :].rearrange("p a d -> p (a d)")
                        ins = m.matmul(ps[:, k * ATTN:(k + 1) * ATTN], onehotT[:, k * P:(k + 1) * P], q,
                                       start=True, stop=True)
                    ins.then_inc(S["a_q"], 1)
                    pe.wait_ge(S["a_bm"], bt + 1)
                    m.matmul(ps[0:1, 4 * 512 + 256:4 * 512 + 384], st[:, 24:25], ident, start=True, stop=True)\
                        .then_inc(S["a_mt"], 1)
                    pe.wait_ge(S["a_mr"], bt + 1)
                    m.matmul(ps[:, 4 * 512 + 384:4 * 512 + 385], c_("ones")[0:1, :], mrun[0:1, 0:1],
                             start=True, stop=True).then_inc(S["a_mb"], 1)
                    pe.wait_ge(S["a_w"], bt + 1)
                    for k in range(BT):
                        slot = h * BT + k
                        pe.wait_ge(S["a_free"], turn * RING + slot + 1)
                        bank = (5 + k % 2) * 512
                        ins = m.matmul(ps[:, bank:bank + AGW], onehot[:, slot, :], ring[:, slot, ATTN:ATTN + AGW],
                                       start=True, stop=True)
                        ins.then_inc(S["s_ps"], 1)

            pe.wait_ge(S["a_free"], ABANKS + CHUNKS)
            m.matmul(psC[:, 0:1], w_("W0", 2 * D, 3 * D), w_("u"), start=True, stop=True).then_inc(S["n2_ub"], 1)
            with pe.Fori(0, NG) as t:
                T = temps
                pe.wait_ge(S["n2_ue"], t + 1)
                hold(pe)
                turnT(T[0], psA, ATTN).then_inc(S["n2_ueT"], 1)
                pe.wait_ge(S["n2_ueTc"], t + 1)
                pe.wait_ge(S["n2_r0"], t)
                nodes(psB, [(T[1][0:ATTN, :], w_("We")[0:ATTN, :])]).then_inc(S["n2_we"], 1)
                pe.wait_ge(S["n2_z"], t + 1)
                turnT(T[4]).then_inc(S["n2_zT"], 1)
                pe.wait_ge(S["n2_zTc"], t + 1)
                for k in range(2):
                    ins = feats(psB[:, 1024 * k:1024 * k + GW], [(w_("w1", k * P, (k + 1) * P), lambda l, r: T[1][:, l:r])])
                ins.then_inc(S["n2_hid"], 1)
                pe.wait_ge(S["n2_relu"], t + 1)
                nodes(psA, [(T[5], w_("w2", 0, D)), (T[6], w_("w2", D, 2 * D))]).then_inc(S["n2_ffn"], 1)
                pe.wait_ge(S["n2_x"], t + 1)
                turnT(T[4]).then_inc(S["n2_h1T"], 1)
                pe.wait_ge(S["n2_h1Tc"], t + 1)
                turnT(T[7]).then_inc(S["n2_veT"], 1)
                pe.wait_ge(S["n2_veTc"], t + 1)
                feats(psB[:, 0:GW], [(w_("W0", 0, D), lambda l, r: T[0][:, l:r]),
                                     (w_("W0", D, 2 * D), lambda l, r: T[1][:, l:r])]).then_inc(S["n2_o0"], 1)

            for i in (1, 2):
                pe.wait_ge(S["bn_ac"], i)
                m.matmul(psC[:, 0:1], w_(f"W{i}"), col[:, 3 + 2 * i:4 + 2 * i], start=True, stop=True)\
                    .then_inc(S["bn_bias"], 1)
                pe.wait_ge(S["bn_w"], i)
                with pe.Fori(0, NG) as t:
                    pe.wait_ge(S["l1_relu"], t + NG * (i - 1))
                    f = (lambda l, r: h_f[:, bass.ds(t * GW + l, r - l)]) if i == 1 else \
                        (lambda l, r: big[:, bass.ds(t * GW + l, r - l)])
                    feats(psB[:, 0:GW], [(chb[:, :], f)]).then_inc(S["l1_mm"], 1)
            with pe.Fori(0, NG) as t:
                pe.wait_ge(S["n3_o"], t + 1)
                pe.wait_ge(S["n3_hs"], t)
                turnT(temps[0]).then_inc(S["n3_T"], 1)

            plain_pass(2, 1, SW)
            with pe.Fori(0, NG) as t:
                T = temps
                pe.wait_ge(S["n4_in"], t + 1)
                turnT(T[0]).then_inc(S["n4_T"], 1)
                pe.wait_ge(S["n4_m"], t + 1)
                pe.wait_ge(S["n4_Tc"], t * 3 + 1)
                turnT(T[2]).then_inc(S["n4_T"], 1)
                pe.wait_ge(S["n4_Tc"], t * 3 + 2)
                turnT(T[3]).then_inc(S["n4_T"], 1)
                pe.wait_ge(S["n4_Tc"], t * 3 + 3)
                pe.wait_ge(S["n4_h"], t)
                nodes(psB[:, 0:GW], [(T[1], w_("self")), (T[5], w_("inter"))])
                nodes(psB[:, 1024:1024 + GW], [(T[6], w_("self"))]).then_inc(S["n4_mm"], 1)
            pe.wait_ge(S["n4_sum"], 1)
            m.matmul(psC[:, 0:1], chb[:, :], c_("ones", 0, 1), start=True, stop=False)
            m.matmul(psC[:, 0:1], hst[0:LAST, NB - 1, :], c_("ones", 0, 1)[0:LAST, :], start=False, stop=True)\
                .then_inc(S["n4_mean"], 1)

            plain_pass(3, 2, SW)
            with pe.Fori(0, NG) as t:
                T = temps
                pe.wait_ge(S["n5_s"], t + 1)
                pe.wait_ge(S["n5_out"], t)
                turnT(T[0]).then_inc(S["n5_sT"], 1)
                pe.wait_ge(S["n5_sTc"], t + 1)
                nodes(psB[:, 0:GW], [(T[1], w_("Wm"))]).then_inc(S["n5_m"], 1)
                pe.wait_ge(S["n5_msg"], t + 1)
                turnT(T[2]).then_inc(S["n5_T"], 1)
                pe.wait_ge(S["n5_Tc"], t * 2 + 1)
                pe.wait_ge(S["n5_hc"], t + 1)
                turnT(T[3]).then_inc(S["n5_T"], 1)
                pe.wait_ge(S["n5_Tc"], t * 2 + 2)
                for k in range(2):
                    ins = feats(psB[:, 1024 * k:1024 * k + GW],
                                [(w_("ih", k * D, (k + 1) * D), lambda l, r: T[0][:, l:r]),
                                 (w_("hh", k * D, (k + 1) * D), lambda l, r: T[1][:, l:r])])
                ins.then_inc(S["n5_rz"], 1)
                pe.wait_ge(S["n5_rza"], t + 1)
                feats(psB[:, 0:GW], [(w_("ih", 2 * D, 3 * D), lambda l, r: T[0][:, l:r])])
                feats(psB[:, 1024:1024 + GW], [(w_("hh", 2 * D, 3 * D), lambda l, r: T[1][:, l:r])])\
                    .then_inc(S["n5_nn"], 1)
                pe.wait_ge(S["n5_hn"], t + 1)
                turnT(T[3]).then_inc(S["n5_hnT"], 1)


def _constants(np):
    c = np.zeros((P, CONST_W), np.float32)

    def put(n, v):
        a, w = CONST[n]
        c[:v.shape[0], a:a + w] = v
    put("ident", np.eye(P))
    put("strict", np.triu(np.ones((P, P)), 1))
    put("ones", np.ones((P, P)))
    put("iota", np.tile(np.arange(P), (P, 1)))
    put("before", np.triu(np.ones((NB, NB)), 1))
    put("upto", np.triu(np.ones((NB, NB))))
    put("blocks", np.tile(np.arange(NB), (P, 1)))
    put("chunks", np.tile(np.arange(CHUNKS), (P, 1)))
    put("part", np.arange(P)[:, None])
    return c


def kernel(**inputs):
    import numpy as np
    import concourse.bacc as bacc
    from concourse.bass_utils import run_bass_kernel_spmd

    i = {k: np.asarray(v) for k, v in inputs.items()}
    L0 = {k[7:]: v for k, v in i.items() if k.startswith("L0_gnn_")}
    L1 = {k[7:]: v for k, v in i.items() if k.startswith("L1_gnn_")}
    L2 = {k[7:]: v for k, v in i.items() if k.startswith("L2_gnn_")}
    L3 = {k[7:]: v for k, v in i.items() if k.startswith("L3_gnn_")}

    xp = np.zeros((NP, D), np.float32)
    xp[:N] = i["x"]
    xp = np.ascontiguousarray(xp.reshape(NB, P, D).transpose(1, 0, 2))

    def columns(e):
        k = np.full((P, EC), -1, np.int32)
        k[:, :EJ] = e[:EJ * P].reshape(P, EJ)
        k[:ER, EJ] = e[EJ * P:]
        return k

    w = np.zeros((P, WEIGHTS_W), np.float32)

    def put(n, v):
        a, width = WEIGHTS[n]
        w[:v.shape[0], a:a + width] = v

    def halves(v):
        return v.reshape(-1, P, v.shape[1]).transpose(1, 0, 2).reshape(P, -1)

    put("Wg", L0["Wg_in_w"])
    put("msg", L0["msg_w"])
    put("lin", L0["lin_w"])
    put("qky", np.concatenate([L0["Wq"], L0["Wk"], L0["Wy_w"]], 1))
    put("We", L0["We_w"])
    put("w1", L0["ffn_w1"])
    put("w2", halves(L0["ffn_w2"]))
    put("W0", halves(L1["W0"].T))
    put("W1", L1["W1"].T)
    put("W2", L1["W2"].T)
    put("self", L2["W_self"])
    put("inter", L2["W_inter"])
    put("Wm", L3["W_msg"].T)
    put("ih", L3["w_ih"].T)
    put("hh", L3["w_hh"].T)
    put("g_token", L0["g_token"].reshape(D, 1))
    for n in ("ln2_g", "ln2_b", "ln3_g", "ln3_b"):
        put(n, L0[n][:, None])
    put("ffn_b1", L0["ffn_b1"].reshape(2, P).T)
    put("u", L1["u"][0][:, None])
    for n in ("b0", "b1", "b2", "g0", "g1", "g2", "bt0", "bt1", "bt2"):
        put(n, L1[n][:, None])
    put("b_ih", L3["b_ih"].reshape(3, P).T)
    put("b_hh", L3["b_hh"].reshape(3, P).T)

    r = np.zeros((1, ROWS_W), np.float32)
    for n, v in (("eps", L0["eps"]), ("Wg_b", L0["Wg_in_b"]), ("ln1_g", L0["ln1_g"]), ("ln1_b", L0["ln1_b"]),
                 ("msg_b", L0["msg_b"]), ("lin_b", L0["lin_b"]), ("Wy_b", L0["Wy_b"]), ("We_b", L0["We_b"]),
                 ("ffn_b2", L0["ffn_b2"]), ("b_msg", L3["b_msg"]), ("gamma", L3["ln_gamma"]),
                 ("beta", L3["ln_beta"]), ("phi", L0["Wphi"])):
        a, width = ROWS[n]
        r[0, a:a + width] = v

    arrays = {"in_x": xp, "in_src": columns(i["src"]), "in_dst": columns(i["dst"]),
              "in_edge_attr": np.ascontiguousarray(i["edge_attr_128"]), "in_const": _constants(np),
              "in_weights": w, "in_rows": r}
    nc = bacc.Bacc("TRN2", target_bir_lowering=False, num_devices=1)
    args = [nc.dram_tensor(n, a.shape, mybir.dt.from_np(a.dtype), kind="ExternalInput").ap()
            for n, a in arrays.items()]
    out = nc.dram_tensor("out", (P, NB, D), F32, kind="ExternalOutput").ap()
    gnn_kernel(nc, *args, out)
    got = run_bass_kernel_spmd(nc, [arrays], core_ids=[0]).results[0]["out"]
    return np.ascontiguousarray(got.transpose(1, 0, 2).reshape(NP, D)[:N])
```

```python
import math
from contextlib import ExitStack

import concourse.bass as bass
from concourse import mybir

F32 = mybir.dt.float32
I32 = mybir.dt.int32
BF16 = mybir.dt.bfloat16
ALU = mybir.AluOpType
ACT = mybir.ActivationFunctionType
AX = mybir.AxisListType

P = 128
D = 128
N = 6250
E = 106250
NB = -(-N // P)
NP = NB * P
LAST = N - (NB - 1) * P
GB = 7
NG = NB // GB
GW = GB * P
EJ = E // P
ER = E - EJ * P
EC = EJ + 1
BT = 10
RING = 2 * BT
CHUNKS = -(-(E // P + NB) // RING) * RING
TURNS = CHUNKS // RING
BATCHES = CHUNKS // BT
BSTRIDE = 12
SLOTS = CHUNKS * P
TAILS = CHUNKS - (-(-E // P))
ATTN = 64
HID = 256
PAY = D + 3
ROW = D + PAY
KY = ATTN + D
AGW = D + ATTN + 1
SW = D + 1
EPS = 1e-5
BANKS = 5
APAIRS = 3
ADEEP = 3
LOW = -1.0e30
FAR = 1.0e6

CONST = {}
_c = 0
for _n, _w in (("ident", P), ("strict", P), ("ones", P), ("iota", 2 * P), ("before", NB), ("upto", NB),
               ("blocks", NB), ("starts", NB), ("part", 1)):
    CONST[_n] = (_c, _w)
    _c += _w
CONST_W = _c

WEIGHTS = {}
_c = 0
for _n, _w in (("Wg", D), ("msg", D), ("lin", D), ("qky", 2 * ATTN + D), ("We", D), ("w1", HID), ("w2", HID),
               ("W0", 3 * D), ("W1", D), ("W2", D), ("self", D), ("inter", D), ("Wm", D), ("ih", 3 * D),
               ("hh", 3 * D), ("g_token", 1), ("ln2_g", 1), ("ln2_b", 1), ("ln3_g", 1), ("ln3_b", 1),
               ("ffn_b1", 2), ("u", 1), ("b0", 1), ("b1", 1), ("b2", 1), ("g0", 1), ("g1", 1), ("g2", 1),
               ("bt0", 1), ("bt1", 1), ("bt2", 1), ("b_ih", 3), ("b_hh", 3)):
    WEIGHTS[_n] = (_c, _w)
    _c += _w
WEIGHTS_W = _c

ROWS = {}
_c = 0
for _n, _w in (("eps", 1), ("Wg_b", D), ("ln1_g", D), ("ln1_b", D), ("msg_b", D), ("lin_b", D), ("Wy_b", D),
               ("We_b", D), ("ffn_b2", D), ("b_msg", D), ("gamma", D), ("beta", D), ("phi", ATTN)):
    ROWS[_n] = (_c, _w)
    _c += _w
ROWS_W = _c


def gnn_kernel(nc, x, src, dst, src_c, dst_c, edge_attr, chunk_numbers, const, weights, rows, out):
    ctx = ExitStack()
    with ctx:
        def sb(name, shape, dt=F32):
            return ctx.enter_context(nc.sbuf_tensor(name, shape, dt))

        def sem(name):
            return ctx.enter_context(nc.semaphore(name))

        def dram(name, shape):
            return nc.dram_tensor(name, shape, F32, kind="Internal").ap()

        payload = dram("payload", (SLOTS, PAY))
        xn_table = dram("xn_table", (NP, D))
        ky_table = dram("ky_table", (NP, KY))
        h2_table = dram("h2_table", (NP, D))
        h3_table = dram("h3_table", (NP, D))

        cst = sb("cst", [P, CONST_W])
        wts = sb("wts", [P, WEIGHTS_W])
        rws = sb("rws", [P, ROWS_W])
        big = sb("big", [P, 2 * NP])
        att = sb("att", [P, NB * SW])
        hst = sb("hst", [P, NB, D])
        qst = sb("qst", [P, NB, ATTN])
        ring = sb("ring", [P, RING, ROW])
        oh_f = sb("onehots", [P, 2 * (BT * P + 64)])
        onehot = oh_f[:, 0:RING * P].rearrange("p (k s) -> p k s", k=RING)
        identb = sb("identb", [P, P], BF16)
        onehotT = sb("onehotT", [P, BT * P])
        meta_s = sb("meta_s", [P, CHUNKS + BT, 2])
        idx_d = sb("idx_d", [P, EC], I32)
        key_d = sb("key_d", [P, EC])
        low_d = sb("low_d", [P, EC])
        ends = meta_s[:, 0:EC, :]
        blk_s = sb("blk_s", [1, BATCHES * BSTRIDE], I32)
        blk_d = sb("blk_d", [1, (EJ // BT + 1) * BSTRIDE], I32)
        wide = sb("wide", [1, 1], I32)
        idx = sb("idx", [P, ADEEP * BT], I32)
        sidx = sb("sidx", [P, RING], I32)
        padidx = sb("padidx", [P, NB + TAILS], I32)
        padrow = sb("padrow", [P, PAY])
        kyt = sb("kyt", [P, GB, KY])
        zpr = sb("zpr", [P, 2, BT, ATTN])
        zt, pr = zpr[:, 0], zpr[:, 1]
        pos = zpr[:, :, :, :].rearrange("p a b c -> p (a b c)")[:, 0:EC]
        sc = sb("sc", [P, BT])
        wexp = sb("wexp", [P, BT])
        mrun = sb("mrun", [P, 1])
        mb = sb("mb", [P, 3 * ADEEP])
        deg = sb("deg", [P, NB])
        outn = sb("outn", [P, NB])
        inn = sb("inn", [P, NB])
        st = sb("st", [P, 64])
        bns = sb("bns", [P, 14 * 6])
        col = sb("col", [P, 32])
        cnt = sb("cnt", [P, NB])
        mblk = sb("mblk", [P, NB + BT])
        nrm = sb("nrm", [P, 32])
        rootv = sb("rootv", [P, 128])
        tm1 = sb("tm1", [P, NB])
        endt = sb("endt", [P, NB])
        tt = sb("tt", [P, NB])
        chb = sb("chb", [P, P])
        chcol = sb("chcol", [P, 8])
        chint = sb("chint", [P, 8], I32)
        ps = ctx.enter_context(nc.psum_tensor("ps", [P, 8 * 512], F32))

        def c_(n, lo=0, hi=None):
            a, w = CONST[n]
            return cst[:, a + lo:a + (w if hi is None else hi)]

        def w_(n, lo=0, hi=None):
            a, w = WEIGHTS[n]
            return wts[:, a + lo:a + (w if hi is None else hi)]

        def r_(n):
            a, w = ROWS[n]
            return rws[:, a:a + w]

        def over(v, n):
            return v.unsqueeze(1).to_broadcast([P, n, v.shape[1]])

        def along(v, w):
            return v.unsqueeze(2).to_broadcast([P, v.shape[1], w])

        ring_f = ring[:, :, :].rearrange("p a b -> p (a b)")
        temps = [ring_f[:, i * GW:(i + 1) * GW] for i in range(5)] + \
                [oh_f[:, i * GW:(i + 1) * GW] for i in range(2)] + [onehotT[:, 0:GW]]
        xgrp = kyt[:, :, :].rearrange("p a b -> p (a b)")[:, 0:GW]
        q_f = qst[:, :, :].rearrange("p a b -> p (a b)")
        early = [q_f[:, i * GW:(i + 1) * GW] for i in range(3)]

        def g3(v):
            return v.rearrange("p (b d) -> p b d", b=GB)

        xn1 = big[:, 0:NP].rearrange("p (b d) -> p b d", d=D)
        agg = big[:, NP:2 * NP].rearrange("p (b d) -> p b d", d=D)
        acc_a = big[:, 0:NB * AGW].rearrange("p (b d) -> p b d", d=AGW)
        acc_p = big[:, 0:(NB + 1) * SW].rearrange("p (b d) -> p b d", d=SW)
        att3 = att[:, :].rearrange("p (b d) -> p b d", d=SW)
        xs = att[:, 0:NP].rearrange("p (b d) -> p b d", d=D)
        h_f = hst[:, :, :].rearrange("p b d -> p (b d)")
        o = NP
        hi_i = big[:, o:o + EC].bitcast(I32)
        lo_i = big[:, o + EC:o + 2 * EC].bitcast(I32)
        hi = big[:, o + 2 * EC:o + 3 * EC]
        mask = big[:, o + 3 * EC:o + 4 * EC].bitcast(I32)
        csum = big[:, o + 4 * EC:o + 5 * EC]
        key_i = big[:, o + 5 * EC:o + 6 * EC].bitcast(I32)
        oth_i = big[:, o + 6 * EC:o + 7 * EC].bitcast(I32)
        assert 7 * EC <= NP
        keyp = hi
        lob = big[:, o + 5 * EC:o + 5 * EC + 7 * P].rearrange("p (g e) -> p g e", e=P)
        behind = big[:, NB * AGW:NB * AGW + BT * (D + 2 * ATTN + 1)].rearrange("p (k d) -> p k d", k=BT)
        arows = [ring[:, 0:BT, :], ring[:, BT:RING, :], behind]
        ky_f = kyt[:, :, :].rearrange("p a b -> p (a b)")
        hots = [oh_f[:, 0:BT * P + 64], oh_f[:, BT * P + 64:2 * (BT * P + 64)], ky_f]
        ahot = [v_[:, 0:BT * P].rearrange("p (k s) -> p k s", k=BT) for v_ in hots]
        abit = [v_[:, BT * 64 + 64:BT * P + 64].bitcast(BF16).rearrange("p (k s) -> p k s", k=BT) for v_ in hots]
        dhot = [oh_f[:, 0:BT * 2 * P].rearrange("p (k s) -> p k s", k=BT),
                q_f[:, 0:BT * 2 * P].rearrange("p (k s) -> p k s", k=BT)]
        chunks = onehotT[:, 0:CHUNKS]
        ge = oh_f[0:NB, 0:CHUNKS]
        one_e = oh_f[:, CHUNKS:CHUNKS + EC]
        padf = col

        psA = ps[:, 0:1024]
        psB = ps[:, 1024:3072]
        psC = ps[:, 3072:4096]
        psT = ps[:, 1024:1024 + BT * 64].bitcast(BF16)
        MCOL = 7 * 512

        def pair_at(h, k):
            return (4 + (h * BT + k) // 2 % APAIRS) * 512 + k % 2 * 256

        s_const = sem("s_const")
        s_keys = sem("s_keys")
        s_dkeys = sem("s_dkeys")
        s_x = sem("s_x")
        dve_step = sem("dve_step")
        act_step = sem("act_step")
        names = ("k_counts k_sums pad_ready pos_ready "
                 "g_in g_out xn1_ready xn1_stored zeroed d_keys d_turned d_wide f_hot f_ps f_row f_idx f_done f_zero f_step f_add added "
                 "n1_agg n1_T n1_Tc n1_msg n1_t n1_lin n1_z n1_qky n1_q n1_ky ky_stored "
                 "a_hot a_T a_Tc a_q a_z a_e a_bm a_mt a_mr a_mb a_w a_free "
                 "n2_sc n2_sce n2_ue n2_T n2_Tc n2_we n2_z n2_hid n2_relu n2_ffn n2_x n2_xg "
                 "n2_o0 n2_r0 n2_ub n2_ubc "
                 "bn_ac bn_bias bn_w l1_mm l1_relu n3_o n3_T n3_hs n3_st "
                 "n4_in n4_m n4_T n4_Tc n4_mm n4_h n4_st n4_sum n4_mean n4_meanc "
                 "n5_s n5_sT n5_sTc n5_m n5_msg n5_T n5_Tc n5_hc n5_rz n5_rza n5_nn n5_npre n5_n n5_hn n5_hnT n5_out n5_st "
                 "s_var s_std s_root s_rooted s_idx s_hold s_ps s_free").split()
        S = {n: sem(n) for n in names}
        s_pay = [sem(f"s_pay{i}") for i in range(2)]
        s_oh = [sem(f"s_oh{i}") for i in range(2)]
        s_row = [sem(f"s_row{i}") for i in range(ADEEP * BT)]

        SP_OPEN = ("ky_stored", "n3_st", "n5_st")
        DVE_OPEN = ("n2_x", "n1_ky", "n3_hs", "n4_h", "n5_out", "f_done")
        ACT_OPEN = ("n1_q", "n2_r0")
        PE_OPEN = ("n1_lin", "n2_o0", "n3_T", "n4_mm", "n5_hnT")

        def opened(eng, names_, by=1):
            for n in names_:
                eng.sem_inc(S[n], by)

        class Chain:

            def __init__(self, eng, s):
                self.eng, self.s, self.n, self.turn, self.per = eng, s, 0, None, 0

            def __call__(self, ins):
                ins.then_inc(self.s, 1)
                self.n += 1
                at = self.n if self.turn is None else self.turn * self.per + self.n
                self.eng.wait_ge(self.s, at)

            def loop(self, turn, per):
                self.turn, self.per, self.first = turn, per, self.n

            def end(self, turns):
                assert self.n - self.first == self.per, (self.n - self.first, self.per)
                self.turn = None
                self.n = self.first + self.per * turns

        block = ctx.enter_context(nc.Block())

        def hold(eng):
            eng.sem_inc(S["s_hold"], 1)

        SCAT_TURNS = EJ // RING
        SCAT_LEFT = EJ - SCAT_TURNS * RING
        assert SCAT_LEFT == BT and ER > 1
        PADS = NB + TAILS

        def columns_done(slot):
            return SCAT_TURNS + (slot <= SCAT_LEFT)

        def row_base(slot, n):
            if slot >= RING:
                uses = -(-(PADS - (slot - RING)) // BT) + (0 if n < 2 else len(range(2, BATCHES, ADEEP)))
            else:
                uses = columns_done(slot)
                uses += TURNS * (n > 0)
                uses += len(range(slot // BT, BATCHES, ADEEP)) * (n > 1)
                uses += columns_done(slot) * (n > 2)
            return 16 * uses

        PS0 = [0, CHUNKS, 2 * CHUNKS, 2 * CHUNKS + EC]

        def free(eng, n, bt, deep=2):
            eng.wait_ge(S["s_ps"], bt * BT + (PS0[n] + RING - (deep - 1) * BT))

        def product(n, bt, k):
            return bt * BT + (PS0[n] + RING + k + 1)

        FREE0 = {0: 0, 2: CHUNKS, 3: CHUNKS + EC}

        @block.sync
        def _(sp):
            opened(sp, SP_OPEN, 16)
            sp.dma_start(key_i, src).then_inc(s_keys, 16)
            sp.dma_start(cst[:, :], const).then_inc(s_const, 16)
            sp.dma_start(oth_i, dst).then_inc(s_keys, 16)
            sp.dma_start(hst[:, :, :], x).then_inc(s_x, 16)
            sp.dma_start(rws[:, :], rows.to_broadcast([P, ROWS_W])).then_inc(s_const, 16)
            sp.dma_start(wts[:, :], weights).then_inc(s_const, 16)
            sp.dma_start(chunks, chunk_numbers.to_broadcast([P, CHUNKS])).then_inc(s_const, 16)
            sp.dma_start(idx_d[:, :], src_c).then_inc(s_dkeys, 16)
            sp.dma_start(low_d[:, :].bitcast(I32), dst_c).then_inc(s_dkeys, 16)
            ea = edge_attr[0:EJ * P, :].rearrange("(p j) f -> p j f", j=EJ)
            for h in range(2):
                sp.dma_start(ring[:, h * BT:(h + 1) * BT, D:2 * D], ea[:, h * BT:(h + 1) * BT, :])\
                    .then_inc(s_pay[h], 16)
            with sp.Fori(1, SCAT_TURNS) as turn:
                for h in range(2):
                    for k in range(BT):
                        sp.wait_ge(s_row[h * BT + k], turn * 16)
                    sp.dma_start(ring[:, h * BT:(h + 1) * BT, D:2 * D],
                                 ea[:, bass.ds(turn * RING + h * BT, BT), :]).then_inc(s_pay[h], 16)
            for k in range(BT):
                sp.wait_ge(s_row[k], SCAT_TURNS * 16)
            sp.dma_start(ring[:, 0:BT, D:2 * D], ea[:, SCAT_TURNS * RING:EJ, :]).then_inc(s_pay[0], 16)
            sp.wait_ge(s_row[BT], SCAT_TURNS * 16)
            sp.dma_start(ring[0:ER, BT, D:2 * D], edge_attr[EJ * P:E, :]).then_inc(s_pay[1], 16)
            xt = xn_table.rearrange("(b p) d -> p b d", p=P)
            sp.wait_ge(S["xn1_ready"], NG)
            sp.dma_start(xt, xn1).then_inc(S["xn1_stored"], 16)
            for k in range(ADEEP * BT):
                sp.wait_ge(s_row[k], row_base(k, 0))
            pl = payload.rearrange("(c p) w -> p c w", p=P)
            with sp.Fori(0, TURNS) as turn:
                for h in range(2):
                    free(sp, 0, turn * 2 + h)
                    sp.dma_start(ring[:, h * BT:(h + 1) * BT, D:ROW],
                                 pl[:, bass.ds(turn * RING + h * BT, BT), :]).then_inc(s_pay[h], 16)
            kt = ky_table.rearrange("(b p) d -> p b d", p=P)
            with sp.Fori(0, NG) as t:
                sp.wait_ge(S["n1_ky"], t + 2)
                sp.dma_start(kt[:, bass.ds(t * GB, GB), :], kyt[:, :, :]).then_inc(S["ky_stored"], 16)
            with sp.Fori(0, NG) as t:
                sp.wait_ge(S["zeroed"], 2)
                sp.wait_ge(S["n2_x"], t + 1)
                sp.dma_start(g3(xgrp), x[:, bass.ds(t * GB, GB), :]).then_inc(S["n2_xg"], 16)
            h2 = h2_table.rearrange("(b p) d -> p b d", p=P)
            with sp.Fori(0, NG) as t:
                sp.wait_ge(S["n3_hs"], t + 2)
                sp.dma_start(h2[:, bass.ds(t * GB, GB), :], g3(temps[4])).then_inc(S["n3_st"], 16)
            h3 = h3_table.rearrange("(b p) d -> p b d", p=P)
            sp.wait_ge(S["n4_h"], NG + 1)
            sp.dma_start(h3, hst[:, :, :]).then_inc(S["n4_st"], 16)
            with sp.Fori(0, NG) as t:
                sp.wait_ge(S["n5_out"], t + 2)
                sp.dma_start(out[:, bass.ds(t * GB, GB), :], g3(temps[7])).then_inc(S["n5_st"], 16)
            sp.wait_ge(S["n5_st"], 16 * NG + 16)

        @block.gpsimd
        def _(pool):
            def batch(n, bt, lot, table, width, index, count=BT):
                pool.tensor_copy(idx[:, lot:lot + count], index(bt * BT, count)).then_inc(S["s_idx"], 1)
                pool.wait_ge(S["s_idx"], bt + (IDX0[n] + 1))
                hold(pool)
                for k in range(lot, lot + count):
                    to = ring[:, k, 0:width] if k < RING else arows[2][:, k - RING, 0:width]
                    pool.indirect_dma_start(
                        out=to, out_offset=None, in_=table,
                        in_offset=bass.IndirectOffsetOnAxis(ap=idx[:, k:k + 1], axis=0)).then_inc(s_row[k], 16)

            def by_dst(n, table):
                index = lambda c, w: idx_d[:, bass.ds(c, w)]
                with pool.Fori(0, SCAT_TURNS) as turn:
                    for h in range(2):
                        free(pool, n, turn * 2 + h)
                        hold(pool)
                        batch(n, turn * 2 + h, h * BT, table, D, index)
                for h, count in ((0, BT), (1, 1)):
                    free(pool, n, SCAT_TURNS * 2 + h)
                    batch(n, SCAT_TURNS * 2 + h, h * BT, table, D, index, count)
                w = pool.alloc_register(f"pool_wide{n}")
                pool.load([w], wide[0:1, 0:1])
                with pool.If_ne(w, 0):
                    pool.wait_ge(S["s_ps"], PS0[n] + RING + EC)
                    with pool.Fori(0, EC) as c:
                        pool.wait_ge(S["f_done"], c + (1 + EC * (n - 2)))
                        hold(pool)
                        pool.tensor_copy(idx[:, 0:1], idx_d[:, bass.ds(c, 1)]).then_inc(S["f_idx"], 1)
                        pool.wait_ge(S["f_idx"], c + (1 + EC * (n - 2)))
                        hold(pool)
                        pool.indirect_dma_start(
                            out=ring[:, 0, 0:D], out_offset=None, in_=table,
                            in_offset=bass.IndirectOffsetOnAxis(ap=idx[:, 0:1], axis=0)).then_inc(S["f_row"], 16)

            IDX0 = [2 * SCAT_TURNS + 2]
            IDX0 += [IDX0[0] + BATCHES]
            IDX0 += [IDX0[1] + BATCHES]
            IDX0 += [IDX0[2] + 2 * SCAT_TURNS + 2]

            pool.wait_ge(S["pad_ready"], 1)
            for i in range(PADS):
                if i >= BT:
                    pool.wait_ge(s_row[RING + i % BT], 16 * (i // BT))
                pool.indirect_dma_start(
                    out=payload, out_offset=bass.IndirectOffsetOnAxis(ap=padidx[:, i:i + 1], axis=0),
                    in_=padrow[:, :], in_offset=None, bounds_check=SLOTS - 1, oob_is_err=False)\
                    .then_inc(s_row[RING + i % BT], 16)
            pool.wait_ge(S["pos_ready"], 1)

            def scatter(turn, h, first=False):
                lot = slice(h * BT, (h + 1) * BT)
                pool.wait_ge(s_pay[h], turn * 16 + 16)
                for k in range(h * BT, (h + 1) * BT):
                    if not first:
                        pool.wait_ge(s_row[k], turn * 16)
                hold(pool)
                pool.tensor_copy(ring[:, lot, 2 * D + 1:ROW], ends[:, bass.ds(turn * RING + h * BT, BT), :])
                pool.tensor_copy(sidx[:, lot], pos[:, bass.ds(turn * RING + h * BT, BT)])\
                    .then_inc(S["s_idx"], 1)
                pool.wait_ge(S["s_idx"], turn * 2 + h + 1)
                hold(pool)
                for k in range(h * BT, (h + 1) * BT):
                    pool.indirect_dma_start(
                        out=payload, out_offset=bass.IndirectOffsetOnAxis(ap=sidx[:, k:k + 1], axis=0),
                        in_=ring[:, k, D:ROW], in_offset=None).then_inc(s_row[k], 16)

            for h in range(2):
                scatter(0, h, True)
            with pool.Fori(1, SCAT_TURNS) as turn:
                for h in range(2):
                    scatter(turn, h)
            pool.wait_ge(s_pay[0], SCAT_TURNS * 16 + 16)
            pool.wait_ge(s_pay[1], SCAT_TURNS * 16 + 16)
            j = SCAT_TURNS * RING
            pool.tensor_copy(ring[:, 0:BT + 1, 2 * D + 1:ROW], ends[:, j:j + BT + 1, :])
            pool.tensor_copy(sidx[:, 0:BT + 1], pos[:, j:j + BT + 1]).then_inc(S["s_idx"], 2)
            pool.wait_ge(S["s_idx"], 2 * SCAT_TURNS + 2)
            for k in range(BT + 1):
                n = P if k < BT else ER
                pool.indirect_dma_start(
                    out=payload, out_offset=bass.IndirectOffsetOnAxis(ap=sidx[0:n, k:k + 1], axis=0),
                    in_=ring[0:n, k, D:ROW], in_offset=None).then_inc(s_row[k], 16)

            pool.wait_ge(S["xn1_stored"], 16)
            with pool.Fori(0, TURNS) as turn:
                for h in range(2):
                    pool.wait_ge(s_pay[h], turn * 16 + 16 + 16 * (SCAT_TURNS + 1))
                    free(pool, 0, turn * 2 + h)
                    hold(pool)
                    batch(0, turn * 2 + h, h * BT, xn_table, D, lambda c, w: ring[:, h * BT:(h + 1) * BT, ROW - 1])

            pool.wait_ge(S["ky_stored"], 16 * NG + 16)
            pool.wait_ge(S["n1_q"], NG + 1)
            pool.wait_ge(S["zeroed"], 1)
            other = lambda c, w: meta_s[:, bass.ds(c, w), 1]
            with pool.Fori(0, BATCHES // ADEEP) as turn:
                for h in range(ADEEP):
                    free(pool, 1, turn * ADEEP + h, ADEEP)
                    hold(pool)
                    batch(1, turn * ADEEP + h, h * BT, ky_table, KY, other)
            assert BATCHES % ADEEP == 1
            free(pool, 1, BATCHES - 1, ADEEP)
            batch(1, BATCHES - 1, 0, ky_table, KY, other)
            pool.wait_ge(S["n3_st"], 16 * NG + 16)
            pool.wait_ge(S["zeroed"], 3)
            by_dst(2, h2_table)
            pool.wait_ge(S["n4_st"], 16)
            pool.wait_ge(S["zeroed"], 4)
            by_dst(3, h3_table)

        @block.vector
        def _(dve):
            chain = Chain(dve, dve_step)
            v = nc.vector

            def bucket():
                dve.wait_ge(s_keys, 32)
                chain(v.tensor_scalar(hi_i, key_i, 7, None, ALU.arith_shift_right))
                chain(v.tensor_scalar(lo_i, key_i, P - 1, None, ALU.bitwise_and))
                v.tensor_copy(ends[:, :, 0], lo_i)
                v.tensor_copy(ends[:, :, 1], oth_i)
                chain(v.tensor_copy(hi, hi_i))
                chain(v.memset(pos, 0.0))
                with dve.Fori(0, NB) as b:
                    chain.loop(b, 1)
                    a = CONST["blocks"][0]
                    chain(v.tensor_scalar(csum, hi, cst[:, bass.ds(b + a, 1)], 0.0, ALU.is_equal, ALU.add,
                                          accum_out=cnt[:, bass.ds(b, 1)]))
                chain.end(NB)
                v.memset(st[:, 0:1], 0.0).then_inc(S["k_counts"], 1)
                dve.wait_ge(S["k_sums"], 1)
                chain(v.tensor_scalar(chint[0:NB, 0:1], psC[0:NB, 0:1], float(P - 1), None, ALU.add))
                chain(v.tensor_scalar(chint[0:NB, 1:2], chint[0:NB, 0:1], 7, None, ALU.arith_shift_right))
                chain(v.tensor_scalar(chcol[0:NB, 0:1], chint[0:NB, 1:2], 1.0, None, ALU.max))
                v.tensor_scalar(chb[0:NB, :], c_("ones")[0:NB, :], chcol[0:NB, 0:1], float(P), ALU.mult, ALU.mult)\
                    .then_inc(S["k_counts"], 1)
                dve.wait_ge(S["k_sums"], 2)
                chain(v.tensor_scalar(tm1[:, :], psC[:, 64:64 + NB], 1.0, None, ALU.subtract))
                chain(v.tensor_copy(endt[:, :], psC[:, 128:128 + NB]))
                chain(v.tensor_copy(chcol[0:NB, 1:2], psC[0:NB, 256:257]))
                v.tensor_scalar(ge, chunks[0:NB, :], chcol[0:NB, 1:2], None, ALU.is_ge)\
                    .then_inc(S["k_counts"], 1)
                chain(v.tensor_scalar(tt[:, :], psC[:, 192:192 + NB], c_("part"), None, ALU.add))
                chain(v.tensor_tensor(cnt[:, :], tt[:, :], endt[:, :], ALU.is_ge))
                chain(v.scalar_tensor_tensor(padidx[:, 0:NB], cnt[:, :], FAR, tt[:, :], ALU.mult, ALU.add))
                chain(v.tensor_scalar(chcol[:, 2:3], endt[:, NB - 1:NB], c_("part"), None, ALU.add))
                v.tensor_scalar(padidx[:, NB:NB + TAILS], chunks[:, 0:TAILS], float(P), chcol[:, 2:3],
                                ALU.mult, ALU.add).then_inc(S["pad_ready"], 1)
                dve.wait_ge(S["k_sums"], 3)
                chain(v.tensor_scalar(
                    blk_s[0:1, :].rearrange("p (b s) -> p b s", s=BSTRIDE)[:, :, 0:BT],
                    psA[0:1, 0:CHUNKS].rearrange("p (b k) -> p b k", k=BT), float(NB - 1), None, ALU.min))
                with dve.Fori(0, NB) as b:
                    chain.loop(b, 3)
                    a = CONST["blocks"][0]
                    chain(v.tensor_scalar(mask, hi, cst[:, bass.ds(b + a, 1)], None, ALU.is_equal))
                    chain(v.tensor_tensor_scan(csum, one_e, mask, tm1[:, bass.ds(b, 1)], ALU.mult, ALU.add))
                    hold(dve)
                    chain(v.copy_predicated(pos, mask, csum))
                chain.end(NB)
                v.memset(st[:, 0:1], 0.0).then_inc(S["pos_ready"], 1)

            def norm(at, src3, z, sq):
                hold(dve)
                chain(v.reduce_sum(nrm[:, 0:GB], src3, AX.X))
                chain(v.scalar_tensor_tensor(z, along(nrm[:, 0:GB], D), -1.0 / D, src3, ALU.mult, ALU.add))
                chain(v.tensor_tensor(sq, z, z, ALU.mult))
                chain(v.reduce_sum(nrm[:, 8:8 + GB], sq, AX.X))
                v.tensor_scalar(nrm[:, 16:16 + GB], nrm[:, 8:8 + GB], 1.0 / D, EPS, ALU.mult, ALU.add)\
                    .then_inc(S["s_var"], 1)
                dve.wait_ge(S["s_std"], at + 1)
                chain(v.reciprocal(nrm[:, 0:GB], nrm[:, 24:24 + GB]))
                chain(v.tensor_tensor(z, z, along(nrm[:, 0:GB], D), ALU.mult))

            def root(at, value, out_):
                n = value.shape[1]
                v.tensor_copy(rootv[:, 0:n], value).then_inc(S["s_root"], 1)
                dve.wait_ge(S["s_rooted"], at)
                chain(v.reciprocal(out_, rootv[:, 64:64 + n]))

            def by_dst_chunks():
                G = -(-EC // P)
                last = EC - (G - 1) * P
                dve.wait_ge(s_dkeys, 32)
                chain(v.tensor_copy(key_d[:, :], low_d[:, :].bitcast(I32)))
                chain(v.tensor_scalar(csum, key_d[:, :], 0.0, FAR, ALU.is_lt, ALU.mult))
                v.tensor_tensor(keyp, key_d[:, :], csum, ALU.add).then_inc(S["d_keys"], 1)
                dve.wait_ge(S["d_turned"], 1)
                chain(v.memset(st[:, 0:16], 0.0))
                for at, op in ((0, ALU.min), (1, ALU.max)):
                    t_ = psB[:, at * 1024:at * 1024 + G * P].rearrange("p (g e) -> p g e", e=P)
                    v.tensor_reduce(st[:, at * 8:at * 8 + G - 1], t_[:, 0:G - 1, :], AX.X, op)
                    chain(v.tensor_reduce(st[0:last, at * 8 + G - 1:at * 8 + G], t_[0:last, G - 1, :], AX.X, op))
                sti = rootv[:, 0:16].bitcast(I32)
                chain(v.tensor_copy(sti, st[:, 0:16]))
                chain(v.tensor_scalar(sti, sti, 7, None, ALU.arith_shift_right))
                chain(v.tensor_copy(st[:, 0:16], sti))
                chain(v.tensor_tensor(st[:, 16:16 + G], st[:, 8:8 + G], st[:, 0:G], ALU.subtract))
                chain(v.reduce_max(st[:, 24:25], st[:, 16:16 + G], AX.X))
                v.tensor_tensor(lob, over(c_("ones"), G), along(st[:, 0:G], P), ALU.mult).then_inc(S["d_keys"], 1)
                dve.wait_ge(S["d_turned"], 2)
                chain(v.tensor_scalar(low_d[:, :], psA[:, 0:EC], float(P), None, ALU.mult))
                chain(v.tensor_tensor(key_d[:, :], key_d[:, :], low_d[:, :], ALU.subtract))
                v.tensor_copy(blk_d[0:1, :].rearrange("p (b s) -> p b s", s=BSTRIDE)[:, 0:EJ // BT, 0:BT],
                              psA[0:1, 0:EJ].rearrange("p (b k) -> p b k", k=BT))
                v.tensor_copy(blk_d[0:1, EJ // BT * BSTRIDE:EJ // BT * BSTRIDE + 1], psA[0:1, EJ:EC])
                chain(v.reduce_max(st[0:1, 26:27], psC[0:1, 0:P], AX.X))
                v.tensor_scalar(wide[:, :], st[0:1, 26:27], 2.0, None, ALU.is_ge).then_inc(S["d_wide"], 1)

            regs = [dve.alloc_register(f"dve_blk{k}") for k in range(BT)]

            def blocks(table, bt, count=BT):
                dve.load(regs[:count], table[0:1, bass.ds(bt * BSTRIDE, count)])
                return [dve.snap(r, min_val=0, max_val=NB - 1) for r in regs[:count]]

            def by_dst(n):
                def body(bt, h, turn, count=BT):
                    free(dve, n, bt)
                    v.tensor_tensor(dhot[h][:, 0:count, :], over(c_("iota"), count),
                                    along(key_d[:, bass.ds(bt * BT, count)], 2 * P), ALU.is_equal)\
                        .then_inc(s_oh[h], 1)
                    bs = blocks(blk_d, bt, count)
                    for k in range(count):
                        bank = (1 + (h * BT + k) % BANKS) * 512
                        a = acc_p[:, bass.ds(bs[k], 2), :].rearrange("p a d -> p (a d)")
                        dve.wait_ge(S["s_ps"], product(n, bt, k))
                        dve.wait_ge(S["s_free"], bt * BT + (BANKS + FREE0[n] + k))
                        v.tensor_tensor(a, a, ps[:, bank:bank + 2 * SW], ALU.add).then_inc(S["s_free"], 1)

                with dve.Fori(0, SCAT_TURNS) as turn:
                    for h in range(2):
                        body(turn * 2 + h, h, turn)
                body(2 * SCAT_TURNS, 0, SCAT_TURNS)
                body(2 * SCAT_TURNS + 1, 1, SCAT_TURNS, 1)
                dve.wait_ge(S["s_free"], BANKS + FREE0[n] + EC)
                w = dve.alloc_register(f"dve_wide{n}")
                dve.load([w], wide[0:1, 0:1])
                with dve.If_ne(w, 0):
                    v.memset(big[:, 0:(NB + 1) * SW], 0.0).then_inc(S["f_zero"], 1)
                    dve.wait_ge(S["f_zero"], n - 1)
                    with dve.Fori(0, EC) as c:
                        with dve.Fori(0, NB) as b:
                            i = c * NB + b
                            v.tensor_tensor(st[:, 1:2], key_d[:, bass.ds(c, 1)], low_d[:, bass.ds(c, 1)], ALU.add)\
                                .then_inc(S["f_step"], 1)
                            dve.wait_ge(S["f_step"], i * 2 + (1 + 2 * NB * EC * (n - 2)))
                            v.tensor_tensor(st[:, 0:1], st[:, 1:2], c_("starts")[:, bass.ds(b, 1)], ALU.subtract)\
                                .then_inc(S["f_step"], 1)
                            dve.wait_ge(S["f_step"], i * 2 + (2 + 2 * NB * EC * (n - 2)))
                            v.tensor_scalar(onehot[:, 0, :], c_("iota", 0, P), st[:, 0:1], None, ALU.is_equal)\
                                .then_inc(S["f_hot"], 1)
                            dve.wait_ge(S["f_ps"], i + (1 + NB * EC * (n - 2)))
                            a = acc_p[:, bass.ds(b, 1), :].rearrange("p a d -> p (a d)")
                            v.tensor_tensor(a, a, ps[:, 0:SW], ALU.add).then_inc(S["f_add"], 1)
                            dve.wait_ge(S["f_add"], i + (1 + NB * EC * (n - 2)))
                        v.memset(st[:, 2:3], 0.0).then_inc(S["f_done"], 1)
                v.memset(st[:, 3:4], 0.0).then_inc(S["added"], 1)

            opened(dve, DVE_OPEN)
            v.memset(padrow[:, :], 0.0)
            v.memset(rootv[:, :], 1.0)
            v.memset(meta_s[:, CHUNKS:CHUNKS + BT, :], 0.0)
            chain(v.memset(one_e, 1.0))
            chain(v.memset(padrow[:, D + 1:D + 2], LOW))
            chain(v.memset(ring[:, :, 2 * D:2 * D + 1], 1.0))
            dve.wait_ge(s_const, 64)
            v.tensor_copy(identb[:, :], c_("ident"))
            bucket()

            dve.wait_ge(s_x, 16)
            with dve.Fori(0, NG) as t:
                chain.loop(t, 7)
                hg = hst[:, bass.ds(t * GB, GB), :]
                norm(t, hg, g3(early[0]), g3(early[1]))
                chain(v.tensor_scalar(hg, g3(early[0]), 0.0, None, ALU.max))
            chain.end(NG)
            v.reduce_sum(early[2][:, 0:D], hst[:, :, :].rearrange("p b d -> p d b"), AX.X).then_inc(S["g_in"], 1)
            dve.wait_ge(S["g_out"], 1)
            chain(v.scalar_tensor_tensor(col[:, 0:1], psC[:, 0:1], 1.0 / N, w_("g_token"), ALU.mult, ALU.add))
            v.tensor_scalar(chb[:, :], c_("ones"), col[:, 0:1], None, ALU.mult).then_inc(S["g_in"], 1)
            dve.wait_ge(S["g_out"], 2)
            chain(v.tensor_tensor(early[2][:, 0:D], psC[:, 64:64 + D], r_("Wg_b"), ALU.add))
            chain(v.tensor_tensor(hst[:, :, :], hst[:, :, :], over(early[2][:, 0:D], NB), ALU.add))
            with dve.Fori(0, NG) as t:
                chain.loop(t, 7)
                xg = xn1[:, bass.ds(t * GB, GB), :]
                norm(t + NG, hst[:, bass.ds(t * GB, GB), :], g3(early[0]), g3(early[1]))
                chain(v.tensor_tensor(g3(early[1]), g3(early[0]), over(r_("ln1_g"), GB), ALU.mult))
                v.tensor_tensor(xg, g3(early[1]), over(r_("ln1_b"), GB), ALU.add).then_inc(S["xn1_ready"], 1)
            chain.end(NG)
            by_dst_chunks()
            chain(v.memset(big[:, NP:2 * NP], 0.0))
            chain(v.memset(att[:, :], 0.0))
            chain(v.tensor_scalar(col[:, 1:2], r_("eps"), 1.0, None, ALU.add))
            dve.sem_inc(S["s_free"], BANKS)

            with dve.Fori(0, TURNS) as turn:
                chain.loop(turn, 2 * BT + 2)
                for h in range(2):
                    bt = turn * 2 + h
                    lot = slice(h * BT, (h + 1) * BT)
                    dve.wait_ge(s_pay[h], turn * 16 + 16 + 16 * (SCAT_TURNS + 1))
                    chain(v.tensor_copy(meta_s[:, bass.ds(bt * BT, BT), :], ring[:, lot, 2 * D + 1:ROW]))
                    free(dve, 0, bt)
                    v.tensor_tensor(onehot[:, lot, :], over(c_("iota", 0, P), BT),
                                    along(meta_s[:, bass.ds(bt * BT, BT), 0], P), ALU.is_equal).then_inc(s_oh[h], 1)
                    bs = blocks(blk_s, bt)
                    for k in range(BT):
                        bank = (1 + (h * BT + k) % BANKS) * 512
                        p = ps[:, bank:bank + D + SW]
                        dve.wait_ge(S["s_ps"], product(0, bt, k))
                        a = agg[:, bass.ds(bs[k], 1), :].rearrange("p a d -> p (a d)")
                        chain(v.tensor_tensor(a, a, p[:, 0:D], ALU.add))
                        a = att3[:, bass.ds(bs[k], 1), :].rearrange("p a d -> p (a d)")
                        dve.wait_ge(S["s_free"], bt * BT + (BANKS + k))
                        v.tensor_tensor(a, a, p[:, D:D + SW], ALU.add).then_inc(S["s_free"], 1)
            chain.end(TURNS)
            dve.wait_ge(S["s_free"], BANKS + CHUNKS)

            chain(v.tensor_copy(deg[:, :], att3[:, :, D]))
            with dve.Fori(0, NG) as t:
                chain.loop(t, 9 + 3)
                T = temps
                hg = hst[:, bass.ds(t * GB, GB), :]
                dve.wait_ge(S["n1_msg"], t + 1)
                chain(v.scalar_tensor_tensor(g3(T[2]), xn1[:, bass.ds(t * GB, GB), :], col[:, 1:2],
                                             g3(psB[:, 0:GW]), ALU.mult, ALU.add))
                chain(v.tensor_tensor(g3(T[3]), over(r_("msg_b"), GB), along(deg[:, bass.ds(t * GB, GB)], D), ALU.mult))
                v.tensor_tensor(T[2], T[2], T[3], ALU.add).then_inc(S["n1_t"], 1)
                dve.wait_ge(S["n1_lin"], t + 2)
                chain(v.tensor_tensor(g3(T[3]), g3(psB[:, 0:GW]), over(r_("lin_b"), GB), ALU.add))
                chain(v.scalar_tensor_tensor(hg, g3(T[3]), 0.0, hg, ALU.max, ALU.add))
                norm(t + 2 * NG, hg, g3(T[4]), g3(T[5]))
                v.memset(st[:, 40:41], 0.0).then_inc(S["n1_z"], 1)
                dve.wait_ge(S["n1_q"], t + 2)
                dve.wait_ge(S["ky_stored"], t * 16 + 16)
                pq = psB[:, 0:GB * HID].rearrange("p (b d) -> p b d", b=GB)
                chain(v.tensor_copy(kyt[:, :, 0:ATTN], pq[:, :, ATTN:2 * ATTN]))
                chain(v.tensor_tensor(kyt[:, :, ATTN:KY], pq[:, :, 2 * ATTN:HID], over(r_("Wy_b"), GB), ALU.add))
                v.memset(st[:, 41:42], 0.0).then_inc(S["n1_ky"], 1)
            chain.end(NG)

            dve.wait_ge(S["n1_q"], NG + 1)
            chain(v.memset(big[:, 0:NB * AGW], 0.0))
            chain(v.memset(big[:, NB * AGW:2 * NP], 1.0))
            chain(v.memset(ring[:, :, D + 2 * ATTN:D + 2 * ATTN + 1], 1.0))
            chain(v.memset(mrun[:, :], LOW))
            v.memset(mb[:, :], LOW).then_inc(S["zeroed"], 1)
            dve.sem_inc(S["a_free"], 2 * APAIRS)

            def a_hot(bt, h):
                free(dve, 1, bt, ADEEP)
                v.tensor_tensor(abit[h], over(c_("iota", 0, P), BT), along(meta_s[:, bass.ds(bt * BT, BT), 0], P),
                                ALU.is_equal).then_inc(S["a_hot"], 1)

            def a_args(bt, h, use):
                for k in range(h * BT, (h + 1) * BT):
                    dve.wait_ge(s_row[k], use * 16 + (16 + row_base(k, 1)))
                dve.wait_ge(S["a_q"], bt + 1)
                v.tensor_tensor(zt, ps[:, 0:BT * ATTN].rearrange("p (c a) -> p c a", a=ATTN),
                                arows[h][:, :, 0:ATTN], ALU.add).then_inc(S["a_z"], 1)

            def a_scores(bt, h):
                dve.wait_ge(S["a_e"], bt + 1)
                chain(v.tensor_tensor(pr, arows[h][:, :, KY:KY + ATTN], over(r_("phi"), BT), ALU.mult))
                chain(v.reduce_sum(sc[:, :], pr, AX.X))
                chain(v.scalar_tensor_tensor(sc[:, :], meta_s[:, bass.ds(bt * BT, BT), 0], 0.0, sc[:, :],
                                             ALU.min, ALU.add))
                v.reduce_max(st[:, 24:25], sc[:, :], AX.X).then_inc(S["a_bm"], 1)

            def a_max(bt):
                dve.wait_ge(S["a_mt"], bt + 1)
                chain(v.reduce_max(st[0:1, 25:26], ps[0:1, MCOL:MCOL + P], AX.X))
                v.tensor_tensor(mrun[0:1, 0:1], mrun[0:1, 0:1], st[0:1, 25:26], ALU.max).then_inc(S["a_mr"], 1)

            def a_sums(bt, h, bs, pairs):
                for k in range(2 * pairs.start, 2 * pairs.stop):
                    dve.wait_ge(S["s_ps"], product(1, bt, k | 1))
                    dve.wait_ge(S["a_free"], bt * BT + (2 * APAIRS + k))
                    a = acc_a[:, bass.ds(bs[k], 1), :].rearrange("p a d -> p (a d)")
                    p = ps[:, pair_at(h, k):pair_at(h, k) + AGW]
                    if k == 0:
                        v.tensor_copy(mblk[:, bass.ds(bs[0], BT)], mb[:, h:h + 1].to_broadcast([P, BT]))
                        ins = v.scalar_tensor_tensor(a, a, mb[:, 6 + h:7 + h], p, ALU.mult, ALU.add)
                    else:
                        ins = v.tensor_tensor(a, a, p, ALU.add)
                    ins.then_inc(S["a_free"], 1)

            a_hot(0, 0)
            a_hot(1, 1)
            a_args(0, 0, 0)
            a_scores(0, 0)
            a_max(0)
            with dve.Fori(0, BATCHES // ADEEP) as turn:
                chain.loop(turn, ADEEP * 4)
                for h in range(ADEEP):
                    bt, h1, h2 = turn * ADEEP + h, (h + 1) % ADEEP, (h + 2) % ADEEP
                    a_hot(bt + 2, h2)
                    a_args(bt + 1, h1, turn + (h + 1) // ADEEP)
                    bs = blocks(blk_s, bt)
                    a_sums(bt, h, bs, range(0, 1))
                    a_scores(bt + 1, h1)
                    a_sums(bt, h, bs, range(1, 2))
                    a_max(bt + 1)
                    a_sums(bt, h, bs, range(2, BT // 2))
            chain.end(BATCHES // ADEEP)
            bs = blocks(blk_s, BATCHES - 1)
            a_sums(BATCHES - 1, 0, bs, range(0, BT // 2))
            dve.wait_ge(S["a_free"], 2 * APAIRS + CHUNKS)
            chain(v.memset(st[:, 42:43], 0.0))
            v.memset(st[:, 43:44], 0.0).then_inc(S["zeroed"], 1)

            chain(v.tensor_scalar(deg[:, :], deg[:, :], 1.0, None, ALU.max))
            chain(v.reciprocal(tt[:, :], deg[:, :]))
            root(1, deg[:, :], outn[:, :])
            v.tensor_scalar(cnt[:, :], mblk[:, 0:NB], mb[:, 0:1], None, ALU.subtract).then_inc(S["n2_sc"], 1)
            dve.wait_ge(S["n2_sce"], 1)
            dve.wait_ge(S["n2_ub"], 1)
            v.tensor_tensor(col[:, 2:3], psC[:, 0:1], w_("b0"), ALU.add).then_inc(S["n2_ubc"], 1)
            with dve.Fori(0, NG) as t:
                chain.loop(t, 26)
                T = temps
                gs = bass.ds(t * GB, GB)
                hg, xg = hst[:, gs, :], xs[:, gs, :]
                chain(v.tensor_tensor(st[:, 40:40 + GB], acc_a[:, gs, AGW - 1], endt[:, gs], ALU.mult))
                chain(v.tensor_scalar(st[:, 48:48 + GB], st[:, 40:40 + GB], 1e-9, None, ALU.add))
                chain(v.reciprocal(st[:, 40:40 + GB], st[:, 48:48 + GB]))
                chain(v.tensor_tensor(st[:, 48:48 + GB], st[:, 40:40 + GB], endt[:, gs], ALU.mult))
                dve.wait_ge(S["n2_we"], t + 1)
                chain(v.tensor_tensor(g3(T[2]), g3(psB[:, 0:GW]), acc_a[:, gs, 0:D], ALU.add))
                chain(v.tensor_tensor(g3(T[3]), over(r_("We_b"), GB), along(acc_a[:, gs, AGW - 1], D), ALU.mult))
                chain(v.tensor_tensor(T[2], T[2], T[3], ALU.add))
                chain(v.tensor_tensor(g3(T[2]), g3(T[2]), along(st[:, 48:48 + GB], D), ALU.mult))
                chain(v.tensor_tensor(hg, hg, g3(T[2]), ALU.add))
                norm(t * 2 + 3 * NG, hg, g3(T[4]), g3(T[3]))
                v.memset(st[:, 60:61], 0.0).then_inc(S["n2_z"], 1)
                dve.wait_ge(S["n2_ffn"], t + 1)
                chain(v.tensor_tensor(g3(T[2]), g3(psA[:, 0:GW]), over(r_("ffn_b2"), GB), ALU.add))
                chain(v.tensor_tensor(g3(T[2]), g3(T[2]), hg, ALU.add))
                dve.wait_ge(S["n2_xg"], t * 16 + 16)
                chain(v.tensor_tensor(T[2], T[2], xgrp, ALU.add))
                chain(v.tensor_tensor(g3(T[7]), att3[:, gs, 0:D], along(tt[:, gs], D), ALU.mult))
                chain(v.tensor_copy(xg, g3(T[2])))
                norm(t * 2 + 3 * NG + 1, g3(T[2]), g3(T[4]), g3(T[3]))
                v.tensor_scalar(T[4], T[4], 0.0, None, ALU.max).then_inc(S["n2_x"], 1)
            chain.end(NG)

            def batch_norm(i, arr):
                n = 0
                for lo in range(0, N, 512):
                    hi_ = min(lo + 512, N)
                    v.bn_stats(bns[:, n * 6:n * 6 + 6], arr[:, lo:hi_])
                    n += 1
                chain(v.memset(st[:, 60:61], 0.0))
                chain(v.bn_aggr(col[:, 16:18], bns[:, 0:n * 6]))
                chain(v.tensor_scalar(col[:, 17:18], col[:, 17:18], EPS, None, ALU.add))
                root(2 + i, col[:, 17:18], col[:, 18:19])
                a, c = col[:, 4 + 2 * i:5 + 2 * i], col[:, 5 + 2 * i:6 + 2 * i]
                chain(v.tensor_tensor(a, col[:, 18:19], w_(f"g{i}"), ALU.mult))
                chain(v.tensor_tensor(col[:, 19:20], col[:, 16:17], a, ALU.mult))
                chain(v.tensor_tensor(c, w_(f"bt{i}"), col[:, 19:20], ALU.subtract))
                v.memset(st[:, 60:61], 0.0).then_inc(S["bn_ac"], 1)

            dve.wait_ge(S["n2_r0"], NG + 1)
            batch_norm(0, h_f)
            for i, arr in ((1, big[:, 0:NP]), (2, big[:, NP:2 * NP])):
                dve.wait_ge(S["bn_bias"], i)
                v.tensor_tensor(col[:, 10 + i:11 + i], psC[:, 0:1], w_(f"b{i}"), ALU.add)
                v.tensor_scalar(chb[:, :], w_(f"W{i}"), col[:, 2 + 2 * i:3 + 2 * i], None, ALU.mult)\
                    .then_inc(S["bn_w"], 1)
                dve.wait_ge(S["l1_relu"], NG * i)
                batch_norm(i, arr)

            with dve.Fori(0, NG) as t:
                chain.loop(t, 8)
                T = temps
                gs = bass.ds(t * GB, GB)
                xg, hg = xs[:, gs, :], hst[:, gs, :]
                dve.wait_ge(S["n3_T"], t + 2)
                chain(v.tensor_tensor(xg, xg, g3(psA[:, 0:GW]), ALU.add))
                norm(t + 5 * NG, xg, g3(T[2]), g3(T[3]))
                chain(v.tensor_scalar(hg, g3(T[2]), 0.0, None, ALU.max))
                dve.wait_ge(S["n3_st"], t * 16 + 16)
                v.tensor_tensor(g3(T[4]), hg, along(outn[:, gs], D), ALU.mult).then_inc(S["n3_hs"], 1)
            chain.end(NG)

            chain(v.memset(big[:, 0:(NB + 1) * SW], 0.0))
            dve.wait_ge(S["n3_st"], 16 * NG + 16)
            v.memset(ring[:, :, D:D + 1], 1.0).then_inc(S["zeroed"], 1)
            by_dst(2)
            chain(v.tensor_copy(deg[:, :], acc_p[:, 0:NB, D]))
            chain(v.tensor_scalar(tt[:, :], deg[:, :], 1.0, None, ALU.max))
            root(5, tt[:, :], inn[:, :])

            with dve.Fori(0, NG) as t:
                chain.loop(t, 3 + 6 + 1)
                T = temps
                gs = bass.ds(t * GB, GB)
                xg, hg = xs[:, gs, :], hst[:, gs, :]
                dve.wait_ge(S["n4_in"], t + 1)
                v.tensor_tensor(T[2], T[0], T[3], ALU.mult).then_inc(S["n4_m"], 1)
                dve.wait_ge(S["n4_mm"], t + 2)
                chain(v.tensor_tensor(g3(T[7]), g3(psB[:, 0:GW]), along(inn[:, gs], D), ALU.mult))
                chain(v.tensor_tensor(T[7], T[7], psB[:, 1024:1024 + GW], ALU.add))
                chain(v.tensor_tensor(xg, xg, g3(T[7]), ALU.add))
                norm(t + 6 * NG, xg, g3(T[7]), g3(T[4]))
                chain(v.tensor_scalar(hg, g3(T[7]), 0.0, None, ALU.max))
                v.memset(st[:, 60:61], 0.0).then_inc(S["n4_h"], 1)
            chain.end(NG)
            v.reduce_sum(chb[:, :], hst[:, 0:NB - 1, :].rearrange("p b d -> p d b"), AX.X).then_inc(S["n4_sum"], 1)
            dve.wait_ge(S["n4_mean"], 1)
            chain(v.tensor_scalar(col[:, 3:4], psC[:, 0:1], 1.0 / N, None, ALU.mult))
            chain(v.tensor_tensor(col[:, 20:23], w_("b_ih"), w_("b_hh"), ALU.add))
            v.tensor_scalar(col[:, 24:27], col[:, 20:23], 0.5, None, ALU.mult).then_inc(S["n4_meanc"], 1)
            chain(v.memset(big[:, 0:(NB + 1) * SW], 0.0))
            dve.wait_ge(S["n4_st"], 16)
            v.memset(ring[:, :, D:D + 1], 1.0).then_inc(S["zeroed"], 1)
            by_dst(3)

            with dve.Fori(0, NG) as t:
                chain.loop(t, 14)
                T = temps
                gs = bass.ds(t * GB, GB)
                dve.wait_ge(S["n5_m"], t + 1)
                chain(v.tensor_tensor(g3(T[4]), over(r_("b_msg"), GB), along(deg[:, gs], D), ALU.mult))
                v.tensor_tensor(T[2], T[4], psB[:, 0:GW], ALU.add).then_inc(S["n5_msg"], 1)
                dve.wait_ge(S["n5_rza"], t + 1)
                v.tensor_scalar(T[5], T[5], 0.5, 0.5, ALU.mult, ALU.add)
                chain(v.tensor_scalar(T[4], T[4], 0.5, 0.5, ALU.mult, ALU.add))
                dve.wait_ge(S["n5_nn"], t + 1)
                chain(v.scalar_tensor_tensor(T[6], psB[:, 1024:1024 + GW], w_("b_hh", 2, 3), T[4], ALU.add, ALU.mult))
                v.tensor_tensor(T[6], T[6], psB[:, 0:GW], ALU.add).then_inc(S["n5_npre"], 1)
                dve.wait_ge(S["n5_n"], t + 1)
                chain(v.tensor_tensor(T[3], T[1], T[0], ALU.subtract))
                chain(v.tensor_tensor(T[3], T[3], T[5], ALU.mult))
                v.tensor_tensor(T[3], T[3], T[0], ALU.add).then_inc(S["n5_hn"], 1)
                dve.wait_ge(S["n5_hnT"], t + 2)
                norm(t + 7 * NG, g3(psA[:, 0:GW]), g3(T[6]), g3(T[4]))
                chain(v.tensor_tensor(g3(T[6]), g3(T[6]), over(r_("gamma"), GB), ALU.mult))
                chain(v.tensor_tensor(g3(T[6]), g3(T[6]), over(r_("beta"), GB), ALU.add))
                chain(v.tensor_tensor(T[6], T[6], T[2], ALU.add))
                dve.wait_ge(S["n5_st"], t * 16 + 16)
                v.tensor_tensor(g3(T[7]), g3(T[6]), xs[:, gs, :], ALU.add).then_inc(S["n5_out"], 1)
            chain.end(NG)

        @block.scalar
        def _(act):
            chain = Chain(act, act_step)
            a = nc.scalar

            def copy(out_, in_):
                return a.activation(out_, in_, ACT.Copy)

            def std(at):
                act.wait_ge(S["s_var"], at + 1)
                a.activation(nrm[:, 24:24 + GB], nrm[:, 16:16 + GB], ACT.Sqrt).then_inc(S["s_std"], 1)

            def rooted(at):
                act.wait_ge(S["s_root"], at)
                a.activation(rootv[:, 64:64 + NB], rootv[:, 0:NB], ACT.Sqrt).then_inc(S["s_rooted"], 1)

            opened(act, ACT_OPEN)
            with act.Fori(0, 2 * NG) as t:
                std(t)

            act.wait_ge(S["s_free"], BANKS + CHUNKS)
            with act.Fori(0, NG) as t:
                T = temps
                act.wait_ge(S["n1_lin"], t + 1)
                copy(g3(T[0]), agg[:, bass.ds(t * GB, GB), :]).then_inc(S["n1_agg"], 1)
                act.wait_ge(S["n1_T"], t * 3 + 1)
                copy(T[1], psA[:, 0:GW]).then_inc(S["n1_Tc"], 1)
                act.wait_ge(S["n1_T"], t * 3 + 2)
                copy(T[0], psA[:, 0:GW]).then_inc(S["n1_Tc"], 1)
                std(t + 2 * NG)
                act.wait_ge(S["n1_T"], t * 3 + 3)
                a.activation(T[1], psA[:, 0:GW], ACT.Identity, bias=w_("ln2_b"), scale=w_("ln2_g"))\
                    .then_inc(S["n1_Tc"], 1)
                act.wait_ge(S["n1_qky"], t + 1)
                pq = psB[:, 0:GB * HID].rearrange("p (b d) -> p b d", b=GB)
                copy(qst[:, bass.ds(t * GB, GB), :], pq[:, :, 0:ATTN]).then_inc(S["n1_q"], 1)

            act.wait_ge(S["zeroed"], 1)
            def a_turned(bt):
                act.wait_ge(S["a_T"], bt + 1)
                act.wait_ge(S["a_q"], bt)
                copy(onehotT[:, :], psT).then_inc(S["a_Tc"], 1)

            def a_tanh(bt, h):
                act.wait_ge(S["a_z"], bt + 1)
                a.activation(arows[h][:, :, KY:KY + ATTN], zt, ACT.Tanh).then_inc(S["a_e"], 1)

            def a_weights(bt, h):
                act.wait_ge(S["a_mb"], bt + 1)
                chain(copy(mb[:, h:h + 1], ps[:, MCOL + P:MCOL + P + 1]))
                chain(a.activation(mb[:, 3 + h:4 + h], mb[:, h:h + 1], ACT.Copy, scale=-1.0))
                before = (h - 1) % ADEEP
                a.activation(mb[:, 6 + h:7 + h], mb[:, before:before + 1], ACT.Exp, bias=mb[:, 3 + h:4 + h])
                chain(a.activation(wexp[:, :], sc[:, :], ACT.Exp, bias=mb[:, 3 + h:4 + h]))

            def a_weighted(bt, h):
                for k in range(BT):
                    if 2 * k >= BT:
                        act.wait_ge(S["a_w"], bt * BT + (2 * k - 9))
                    a.activation(ahot[h][:, k, :], abit[h][:, k, :], ACT.Copy, scale=wexp[:, k:k + 1])\
                        .then_inc(S["a_w"], 1)

            a_turned(0)
            a_turned(1)
            a_tanh(0, 0)
            a_weights(0, 0)
            a_weighted(0, 0)
            with act.Fori(0, BATCHES // ADEEP) as turn:
                chain.loop(turn, ADEEP * 3)
                for h in range(ADEEP):
                    bt, h1 = turn * ADEEP + h, (h + 1) % ADEEP
                    a_turned(bt + 2)
                    a_tanh(bt + 1, h1)
                    a_weights(bt + 1, h1)
                    a_weighted(bt + 1, h1)
            chain.end(BATCHES // ADEEP)

            act.wait_ge(S["zeroed"], 2)
            rooted(1)
            act.wait_ge(S["n2_sc"], 1)
            a.activation(endt[:, :], cnt[:, :], ACT.Exp).then_inc(S["n2_sce"], 1)
            act.wait_ge(S["n2_ubc"], 1)
            with act.Fori(0, NG) as t:
                T = temps
                gs = bass.ds(t * GB, GB)
                act.wait_ge(S["n2_o0"], t + 1)
                ue = T[0][:, 0:GB * ATTN]
                copy(ue.rearrange("p (b d) -> p b d", b=GB), acc_a[:, gs, D:D + ATTN]).then_inc(S["n2_ue"], 1)
                act.wait_ge(S["n2_T"], t * 4 + 1)
                copy(T[1][0:ATTN, :], psA[0:ATTN, 0:GW]).then_inc(S["n2_Tc"], 1)
                std(t * 2 + 3 * NG)
                act.wait_ge(S["n2_T"], t * 4 + 2)
                a.activation(T[1], psA[:, 0:GW], ACT.Identity, bias=w_("ln3_b"), scale=w_("ln3_g"))\
                    .then_inc(S["n2_Tc"], 1)
                act.wait_ge(S["n2_hid"], t + 1)
                for k in range(2):
                    ins = a.activation(T[5 + k], psB[:, 1024 * k:1024 * k + GW], ACT.Relu,
                                       bias=w_("ffn_b1", k, k + 1))
                ins.then_inc(S["n2_relu"], 1)
                std(t * 2 + 3 * NG + 1)
                act.wait_ge(S["n2_T"], t * 4 + 3)
                copy(T[0], psA[:, 0:GW]).then_inc(S["n2_Tc"], 1)
                act.wait_ge(S["n2_T"], t * 4 + 4)
                copy(T[1], psA[:, 0:GW]).then_inc(S["n2_Tc"], 1)
                act.wait_ge(S["n2_o0"], t + 2)
                a.activation(h_f[:, bass.ds(t * GW, GW)], psB[:, 0:GW], ACT.Relu, bias=col[:, 2:3])\
                    .then_inc(S["n2_r0"], 1)

            rooted(2)
            for i in (1, 2):
                with act.Fori(0, NG) as t:
                    act.wait_ge(S["l1_mm"], t + 1 + NG * (i - 1))
                    a.activation(big[:, bass.ds(t * GW + (i - 1) * NP, GW)], psB[:, 0:GW], ACT.Relu,
                                 bias=col[:, 10 + i:11 + i]).then_inc(S["l1_relu"], 1)
                rooted(2 + i)
            act.wait_ge(S["bn_ac"], 3)
            with act.Fori(0, NG) as t:
                act.wait_ge(S["n3_T"], t + 1)
                a.activation(temps[0], big[:, bass.ds(t * GW + NP, GW)], ACT.Identity, bias=col[:, 9:10],
                             scale=col[:, 8:9]).then_inc(S["n3_o"], 1)
                std(t + 5 * NG)

            act.wait_ge(S["added"], 1)
            rooted(5)
            with act.Fori(0, NG) as t:
                T = temps
                gs = bass.ds(t * GB, GB)
                act.wait_ge(S["n4_mm"], t + 1)
                copy(g3(T[0]), acc_p[:, gs, 0:D])
                copy(g3(T[3]), hst[:, gs, :]).then_inc(S["n4_in"], 1)
                for i, d in enumerate((1, 5, 6)):
                    act.wait_ge(S["n4_T"], t * 3 + i + 1)
                    copy(T[d], psA[:, 0:GW]).then_inc(S["n4_Tc"], 1)
                std(t + 6 * NG)

            act.wait_ge(S["added"], 2)
            act.wait_ge(S["n4_meanc"], 1)
            with act.Fori(0, NG) as t:
                T = temps
                gs = bass.ds(t * GB, GB)
                act.wait_ge(S["n5_hnT"], t + 1)
                copy(g3(T[0]), acc_p[:, gs, 0:D]).then_inc(S["n5_s"], 1)
                act.wait_ge(S["n5_sT"], t + 1)
                copy(T[1], psA[:, 0:GW]).then_inc(S["n5_sTc"], 1)
                copy(g3(T[3]), hst[:, gs, :]).then_inc(S["n5_hc"], 1)
                act.wait_ge(S["n5_T"], t * 2 + 1)
                a.activation(T[0], psA[:, 0:GW], ACT.Identity, bias=col[:, 3:4]).then_inc(S["n5_Tc"], 1)
                act.wait_ge(S["n5_T"], t * 2 + 2)
                copy(T[1], psA[:, 0:GW]).then_inc(S["n5_Tc"], 1)
                act.wait_ge(S["n5_rz"], t + 1)
                for k in range(2):
                    ins = a.activation(T[4 + k], psB[:, 1024 * k:1024 * k + GW], ACT.Tanh, scale=0.5,
                                       bias=col[:, 24 + k:25 + k])
                ins.then_inc(S["n5_rza"], 1)
                act.wait_ge(S["n5_npre"], t + 1)
                a.activation(T[0], T[6], ACT.Tanh, bias=w_("b_ih", 2, 3)).then_inc(S["n5_n"], 1)
                std(t + 7 * NG)

        @block.tensor
        def _(pe):
            m = nc.tensor
            ident = c_("ident")
            PIECES = ((0, 512), (512, GW))

            def turnT(src_, dst_=psA, n=P):
                for j in range(GB):
                    ins = m.transpose(dst_[0:n, j * P:(j + 1) * P], src_[:, j * n:(j + 1) * n], ident)
                return ins

            def nodes(dst_, pairs, width=P, stride=P):
                for j in range(GB):
                    for i, (l, r) in enumerate(pairs):
                        ins = m.matmul(dst_[:, j * stride:j * stride + width], l[:, j * P:(j + 1) * P], r,
                                       start=i == 0, stop=i == len(pairs) - 1)
                return ins

            def feats(dst_, pairs):
                for lo, hi_ in PIECES:
                    for i, (l, r) in enumerate(pairs):
                        ins = m.matmul(dst_[:, lo:hi_], l, r(lo, hi_), start=i == 0, stop=i == len(pairs) - 1)
                return ins

            def bucket():
                pe.wait_ge(S["k_counts"], 1)
                m.matmul(psC[0:NB, 0:1], cnt[:, :], c_("ones", 0, 1), start=True, stop=True)\
                    .then_inc(S["k_sums"], 1)
                pe.wait_ge(S["k_counts"], 2)
                ch = chb[0:NB, :]
                before, upto = c_("before")[0:NB, :], c_("upto")[0:NB, :]
                m.matmul(psC[:, 64:64 + NB], ch, before, start=True, stop=False)
                m.matmul(psC[:, 64:64 + NB], c_("strict"), cnt[:, :], start=False, stop=True)
                m.matmul(psC[:, 128:128 + NB], ch, upto, start=True, stop=True)
                m.matmul(psC[:, 192:192 + NB], ch, before, start=True, stop=False)
                m.matmul(psC[:, 192:192 + NB], c_("ones"), cnt[:, :], start=False, stop=True)
                m.matmul(psC[0:NB, 256:257], upto, chcol[0:NB, 0:1], start=True, stop=True).then_inc(S["k_sums"], 1)
                pe.wait_ge(S["k_counts"], 3)
                for lo in range(0, CHUNKS, 512):
                    hi_ = min(lo + 512, CHUNKS)
                    ins = m.matmul(psA[0:1, lo:hi_], c_("ones", 0, 1)[0:NB, :], ge[:, lo:hi_], start=True, stop=True)
                ins.then_inc(S["k_sums"], 1)

            regs = [pe.alloc_register(f"pe_blk{k}") for k in range(BT)]

            def by_dst_chunks():
                G = -(-EC // P)
                pe.wait_ge(S["d_keys"], 1)
                for at, keys in ((0, keyp), (1, key_d[:, :])):
                    for g in range(G):
                        n = min(P, EC - g * P)
                        o_ = at * 1024 + g * P
                        ins = m.transpose(psB[0:n, o_:o_ + P], keys[:, g * P:g * P + n], ident)
                ins.then_inc(S["d_turned"], 1)
                pe.wait_ge(S["d_keys"], 2)
                m.matmul(psC[0:1, 0:P], st[:, 24:25], ident, start=True, stop=True)
                for g in range(G):
                    n = min(P, EC - g * P)
                    ins = m.matmul(psA[:, g * P:g * P + n], lob[0:n, g, :], ident[0:n, 0:n], start=True, stop=True)
                ins.then_inc(S["d_turned"], 1)

            def by_dst(n):
                def body(bt, h, turn, count=BT):
                    pe.wait_ge(s_oh[h], turn + (1 + TURNS + (n - 2) * (SCAT_TURNS + 1)))
                    for k in range(count):
                        slot = h * BT + k
                        pe.wait_ge(s_row[slot], turn * 16 + (16 + row_base(slot, n)))
                        pe.wait_ge(S["s_free"], bt * BT + (FREE0[n] + k + 1))
                        bank = (1 + slot % BANKS) * 512
                        m.matmul(ps[:, bank:bank + SW], dhot[h][:, k, 0:P], ring[:, slot, 0:SW],
                                 start=True, stop=True)
                        m.matmul(ps[:, bank + SW:bank + 2 * SW], dhot[h][:, k, P:2 * P], ring[:, slot, 0:SW],
                                 start=True, stop=True).then_inc(S["s_ps"], 1)

                with pe.Fori(0, SCAT_TURNS) as turn:
                    for h in range(2):
                        body(turn * 2 + h, h, turn)
                body(2 * SCAT_TURNS, 0, SCAT_TURNS)
                body(2 * SCAT_TURNS + 1, 1, SCAT_TURNS, 1)
                w = pe.alloc_register(f"pe_wide{n}")
                pe.load([w], wide[0:1, 0:1])
                with pe.If_ne(w, 0):
                    with pe.Fori(0, EC) as c:
                        pe.wait_ge(S["f_row"], c * 16 + (16 + 16 * EC * (n - 2)))
                        hold(pe)
                        with pe.Fori(0, NB) as b:
                            pe.wait_ge(S["f_hot"], c * NB + b + (1 + NB * EC * (n - 2)))
                            m.matmul(ps[:, 0:SW], onehot[:, 0, :], ring[:, 0, 0:SW], start=True, stop=True)\
                                .then_inc(S["f_ps"], 1)

            opened(pe, PE_OPEN)
            pe.sem_inc(S["s_ps"], RING)
            pe.wait_ge(s_const, 64)
            bucket()
            pe.wait_ge(S["g_in"], 1)
            m.matmul(psC[:, 0:1], early[2][:, 0:D], c_("ones", 0, 1), start=True, stop=True).then_inc(S["g_out"], 1)
            pe.wait_ge(S["g_in"], 2)
            m.matmul(psC[:, 64:64 + D], chb[:, :], w_("Wg"), start=True, stop=True).then_inc(S["g_out"], 1)
            by_dst_chunks()
            pe.wait_ge(S["d_wide"], 1)
            with pe.Fori(0, TURNS) as turn:
                for h in range(2):
                    pe.wait_ge(s_oh[h], turn + 1)
                    for k in range(BT):
                        slot = h * BT + k
                        pe.wait_ge(s_row[slot], turn * 16 + (16 + row_base(slot, 0)))
                        pe.wait_ge(S["s_free"], turn * RING + (slot + 1))
                        bank = (1 + slot % BANKS) * 512
                        m.matmul(ps[:, bank:bank + D + SW], onehot[:, slot, :], ring[:, slot, 0:D + SW],
                                 start=True, stop=True).then_inc(S["s_ps"], 1)

            with pe.Fori(0, NG) as t:
                T = temps
                pe.wait_ge(S["n1_agg"], t + 1)
                turnT(T[0]).then_inc(S["n1_T"], 1)
                pe.wait_ge(S["n1_Tc"], t * 3 + 1)
                pe.wait_ge(S["n1_q"], t + 1)
                pe.wait_ge(S["n1_ky"], t + 1)
                nodes(psB, [(T[1], w_("msg"))]).then_inc(S["n1_msg"], 1)
                pe.wait_ge(S["n1_t"], t + 1)
                turnT(T[2]).then_inc(S["n1_T"], 1)
                pe.wait_ge(S["n1_Tc"], t * 3 + 2)
                nodes(psB, [(T[0], w_("lin"))]).then_inc(S["n1_lin"], 1)
                pe.wait_ge(S["n1_z"], t + 1)
                turnT(T[4]).then_inc(S["n1_T"], 1)
                pe.wait_ge(S["n1_Tc"], t * 3 + 3)
                nodes(psB, [(T[1], w_("qky"))], HID, HID).then_inc(S["n1_qky"], 1)

            pe.wait_ge(S["n1_q"], NG + 1)
            pe.wait_ge(S["n1_ky"], NG + 1)

            def a_turn(bt, h):
                pe.wait_ge(S["a_hot"], bt + 1)
                pe.wait_ge(S["a_Tc"], bt)
                for k in range(BT):
                    ins = m.transpose(psT[:, k * P:(k + 1) * P], abit[h][:, k, :], identb[:, :])
                ins.then_inc(S["a_T"], 1)

            def a_q(bt):
                pe.load(regs, blk_s[0:1, bass.ds(bt * BSTRIDE, BT)])
                bs = [pe.snap(r, min_val=0, max_val=NB - 1) for r in regs]
                pe.wait_ge(S["a_Tc"], bt + 1)
                pe.wait_ge(S["a_z"], bt)
                for k in range(BT):
                    q = qst[:, bass.ds(bs[k], 1), :].rearrange("p a d -> p (a d)")
                    ins = m.matmul(ps[:, k * ATTN:(k + 1) * ATTN], onehotT[:, k * P:(k + 1) * P], q,
                                   start=True, stop=True)
                ins.then_inc(S["a_q"], 1)

            def a_maxT(bt):
                pe.wait_ge(S["a_bm"], bt + 1)
                m.matmul(ps[0:1, MCOL:MCOL + P], st[:, 24:25], ident, start=True, stop=True).then_inc(S["a_mt"], 1)

            def a_maxb(bt):
                pe.wait_ge(S["a_mr"], bt + 1)
                m.matmul(ps[:, MCOL + P:MCOL + P + 1], c_("ones")[0:1, :], mrun[0:1, 0:1], start=True, stop=True)\
                    .then_inc(S["a_mb"], 1)

            def a_products(bt, h, pairs):
                for k in range(2 * pairs.start, 2 * pairs.stop):
                    pe.wait_ge(S["a_w"], bt * BT + (k + 1))
                    if k % 2 == 0:
                        pe.wait_ge(S["a_free"], bt * BT + (k + 2))
                    m.matmul(ps[:, pair_at(h, k):pair_at(h, k) + AGW], ahot[h][:, k, :],
                             arows[h][:, k, ATTN:ATTN + AGW], start=True, stop=True).then_inc(S["s_ps"], 1)

            a_turn(0, 0)
            a_q(0)
            a_turn(1, 1)
            a_maxT(0)
            a_maxb(0)
            with pe.Fori(0, BATCHES // ADEEP) as turn:
                for h in range(ADEEP):
                    bt, h1, h2 = turn * ADEEP + h, (h + 1) % ADEEP, (h + 2) % ADEEP
                    a_q(bt + 1)
                    a_turn(bt + 2, h2)
                    a_products(bt, h, range(0, 3))
                    a_maxT(bt + 1)
                    a_products(bt, h, range(3, 4))
                    a_maxb(bt + 1)
                    a_products(bt, h, range(4, 5))
            a_products(BATCHES - 1, 0, range(0, 5))

            pe.wait_ge(S["a_free"], 2 * APAIRS + CHUNKS)
            m.matmul(psC[:, 0:1], w_("W0", 2 * D, 3 * D), w_("u"), start=True, stop=True).then_inc(S["n2_ub"], 1)
            with pe.Fori(0, NG) as t:
                T = temps
                pe.wait_ge(S["n2_ue"], t + 1)
                hold(pe)
                turnT(T[0], psA, ATTN).then_inc(S["n2_T"], 1)
                pe.wait_ge(S["n2_Tc"], t * 4 + 1)
                pe.wait_ge(S["n2_r0"], t + 1)
                nodes(psB, [(T[1][0:ATTN, :], w_("We")[0:ATTN, :])]).then_inc(S["n2_we"], 1)
                pe.wait_ge(S["n2_z"], t + 1)
                turnT(T[4]).then_inc(S["n2_T"], 1)
                pe.wait_ge(S["n2_Tc"], t * 4 + 2)
                for k in range(2):
                    ins = feats(psB[:, 1024 * k:1024 * k + GW], [(w_("w1", k * P, (k + 1) * P), lambda l, r: T[1][:, l:r])])
                ins.then_inc(S["n2_hid"], 1)
                pe.wait_ge(S["n2_relu"], t + 1)
                nodes(psA, [(T[5], w_("w2", 0, D)), (T[6], w_("w2", D, 2 * D))]).then_inc(S["n2_ffn"], 1)
                pe.wait_ge(S["n2_x"], t + 2)
                turnT(T[4]).then_inc(S["n2_T"], 1)
                pe.wait_ge(S["n2_Tc"], t * 4 + 3)
                turnT(T[7]).then_inc(S["n2_T"], 1)
                pe.wait_ge(S["n2_Tc"], t * 4 + 4)
                feats(psB[:, 0:GW], [(w_("W0", 0, D), lambda l, r: T[0][:, l:r]),
                                     (w_("W0", D, 2 * D), lambda l, r: T[1][:, l:r])]).then_inc(S["n2_o0"], 1)

            for i in (1, 2):
                pe.wait_ge(S["bn_ac"], i)
                m.matmul(psC[:, 0:1], w_(f"W{i}"), col[:, 3 + 2 * i:4 + 2 * i], start=True, stop=True)\
                    .then_inc(S["bn_bias"], 1)
                pe.wait_ge(S["bn_w"], i)
                with pe.Fori(0, NG) as t:
                    pe.wait_ge(S["l1_relu"], t + NG * (i - 1))
                    f = (lambda l, r: h_f[:, bass.ds(t * GW + l, r - l)]) if i == 1 else \
                        (lambda l, r: big[:, bass.ds(t * GW + l, r - l)])
                    feats(psB[:, 0:GW], [(chb[:, :], f)]).then_inc(S["l1_mm"], 1)
            with pe.Fori(0, NG) as t:
                pe.wait_ge(S["n3_o"], t + 1)
                pe.wait_ge(S["n3_hs"], t + 1)
                turnT(temps[0]).then_inc(S["n3_T"], 1)

            by_dst(2)
            with pe.Fori(0, NG) as t:
                T = temps
                pe.wait_ge(S["n4_in"], t + 1)
                turnT(T[0]).then_inc(S["n4_T"], 1)
                pe.wait_ge(S["n4_m"], t + 1)
                pe.wait_ge(S["n4_Tc"], t * 3 + 1)
                turnT(T[2]).then_inc(S["n4_T"], 1)
                pe.wait_ge(S["n4_Tc"], t * 3 + 2)
                turnT(T[3]).then_inc(S["n4_T"], 1)
                pe.wait_ge(S["n4_Tc"], t * 3 + 3)
                pe.wait_ge(S["n4_h"], t + 1)
                nodes(psB[:, 0:GW], [(T[1], w_("self")), (T[5], w_("inter"))])
                nodes(psB[:, 1024:1024 + GW], [(T[6], w_("self"))]).then_inc(S["n4_mm"], 1)
            pe.wait_ge(S["n4_sum"], 1)
            m.matmul(psC[:, 0:1], chb[:, :], c_("ones", 0, 1), start=True, stop=False)
            m.matmul(psC[:, 0:1], hst[0:LAST, NB - 1, :], c_("ones", 0, 1)[0:LAST, :], start=False, stop=True)\
                .then_inc(S["n4_mean"], 1)

            by_dst(3)
            with pe.Fori(0, NG) as t:
                T = temps
                pe.wait_ge(S["n5_s"], t + 1)
                pe.wait_ge(S["n5_out"], t + 1)
                turnT(T[0]).then_inc(S["n5_sT"], 1)
                pe.wait_ge(S["n5_sTc"], t + 1)
                nodes(psB[:, 0:GW], [(T[1], w_("Wm"))]).then_inc(S["n5_m"], 1)
                pe.wait_ge(S["n5_msg"], t + 1)
                turnT(T[2]).then_inc(S["n5_T"], 1)
                pe.wait_ge(S["n5_Tc"], t * 2 + 1)
                pe.wait_ge(S["n5_hc"], t + 1)
                turnT(T[3]).then_inc(S["n5_T"], 1)
                pe.wait_ge(S["n5_Tc"], t * 2 + 2)
                for k in range(2):
                    ins = feats(psB[:, 1024 * k:1024 * k + GW],
                                [(w_("ih", k * D, (k + 1) * D), lambda l, r: T[0][:, l:r]),
                                 (w_("hh", k * D, (k + 1) * D), lambda l, r: T[1][:, l:r])])
                ins.then_inc(S["n5_rz"], 1)
                pe.wait_ge(S["n5_rza"], t + 1)
                feats(psB[:, 0:GW], [(w_("ih", 2 * D, 3 * D), lambda l, r: T[0][:, l:r])])
                feats(psB[:, 1024:1024 + GW], [(w_("hh", 2 * D, 3 * D), lambda l, r: T[1][:, l:r])])\
                    .then_inc(S["n5_nn"], 1)
                pe.wait_ge(S["n5_hn"], t + 1)
                turnT(T[3]).then_inc(S["n5_hnT"], 1)


def _constants(np):
    c = np.zeros((P, CONST_W), np.float32)

    def put(n, v):
        a, w = CONST[n]
        c[:v.shape[0], a:a + w] = v
    put("ident", np.eye(P))
    put("strict", np.triu(np.ones((P, P)), 1))
    put("ones", np.ones((P, P)))
    put("iota", np.tile(np.arange(2 * P), (P, 1)))
    put("before", np.triu(np.ones((NB, NB)), 1))
    put("upto", np.triu(np.ones((NB, NB))))
    put("blocks", np.tile(np.arange(NB), (P, 1)))
    put("starts", np.tile(P * np.arange(NB), (P, 1)))
    put("part", np.arange(P)[:, None])
    return c


def kernel(**inputs):
    import numpy as np
    import concourse.bacc as bacc
    from concourse.bass_utils import run_bass_kernel_spmd

    i = {k: np.asarray(v) for k, v in inputs.items()}
    L0 = {k[7:]: v for k, v in i.items() if k.startswith("L0_gnn_")}
    L1 = {k[7:]: v for k, v in i.items() if k.startswith("L1_gnn_")}
    L2 = {k[7:]: v for k, v in i.items() if k.startswith("L2_gnn_")}
    L3 = {k[7:]: v for k, v in i.items() if k.startswith("L3_gnn_")}

    xp = np.zeros((NP, D), np.float32)
    xp[:N] = i["x"]
    xp = np.ascontiguousarray(xp.reshape(NB, P, D).transpose(1, 0, 2))

    def columns(e):
        k = np.full((P, EC), -1, np.int32)
        k[:, :EJ] = e[:EJ * P].reshape(P, EJ)
        k[:ER, EJ] = e[EJ * P:]
        return k

    def rows_of(e, behind):
        k = np.full(EC * P, behind, np.int32)
        k[:E] = e
        return np.ascontiguousarray(k.reshape(EC, P).T)

    w = np.zeros((P, WEIGHTS_W), np.float32)

    def put(n, v):
        a, width = WEIGHTS[n]
        w[:v.shape[0], a:a + width] = v

    def halves(v):
        return v.reshape(-1, P, v.shape[1]).transpose(1, 0, 2).reshape(P, -1)

    put("Wg", L0["Wg_in_w"])
    put("msg", L0["msg_w"])
    put("lin", L0["lin_w"])
    put("qky", np.concatenate([L0["Wq"], L0["Wk"], L0["Wy_w"]], 1))
    put("We", L0["We_w"])
    put("w1", L0["ffn_w1"])
    put("w2", halves(L0["ffn_w2"]))
    put("W0", halves(L1["W0"].T))
    put("W1", L1["W1"].T)
    put("W2", L1["W2"].T)
    put("self", L2["W_self"])
    put("inter", L2["W_inter"])
    put("Wm", L3["W_msg"].T)
    put("ih", L3["w_ih"].T)
    put("hh", L3["w_hh"].T)
    put("g_token", L0["g_token"].reshape(D, 1))
    for n in ("ln2_g", "ln2_b", "ln3_g", "ln3_b"):
        put(n, L0[n][:, None])
    put("ffn_b1", L0["ffn_b1"].reshape(2, P).T)
    put("u", L1["u"][0][:, None])
    for n in ("b0", "b1", "b2", "g0", "g1", "g2", "bt0", "bt1", "bt2"):
        put(n, L1[n][:, None])
    put("b_ih", L3["b_ih"].reshape(3, P).T)
    put("b_hh", L3["b_hh"].reshape(3, P).T)

    r = np.zeros((1, ROWS_W), np.float32)
    for n, v in (("eps", L0["eps"]), ("Wg_b", L0["Wg_in_b"]), ("ln1_g", L0["ln1_g"]), ("ln1_b", L0["ln1_b"]),
                 ("msg_b", L0["msg_b"]), ("lin_b", L0["lin_b"]), ("Wy_b", L0["Wy_b"]), ("We_b", L0["We_b"]),
                 ("ffn_b2", L0["ffn_b2"]), ("b_msg", L3["b_msg"]), ("gamma", L3["ln_gamma"]),
                 ("beta", L3["ln_beta"]), ("phi", L0["Wphi"])):
        a, width = ROWS[n]
        r[0, a:a + width] = v

    arrays = {"in_x": xp, "in_src": columns(i["src"]), "in_dst": columns(i["dst"]),
              "in_src_c": rows_of(i["src"], 0), "in_dst_c": rows_of(i["dst"], -1),
              "in_edge_attr": np.ascontiguousarray(i["edge_attr_128"]), 
              "in_chunks": np.arange(CHUNKS, dtype=np.float32)[None], "in_const": _constants(np),
              "in_weights": w, "in_rows": r}
    nc = bacc.Bacc("TRN2", target_bir_lowering=False, num_devices=1)
    args = [nc.dram_tensor(n, a.shape, mybir.dt.from_np(a.dtype), kind="ExternalInput").ap()
            for n, a in arrays.items()]
    out = nc.dram_tensor("out", (P, NB, D), F32, kind="ExternalOutput").ap()
    gnn_kernel(nc, *args, out)
    got = run_bass_kernel_spmd(nc, [arrays], core_ids=[0]).results[0]["out"]
    return np.ascontiguousarray(got.transpose(1, 0, 2).reshape(NP, D)[:N])
```

```python
import math
from contextlib import ExitStack

import concourse.bass as bass
from concourse import mybir

F32 = mybir.dt.float32
I32 = mybir.dt.int32
BF16 = mybir.dt.bfloat16
ALU = mybir.AluOpType
ACT = mybir.ActivationFunctionType
AX = mybir.AxisListType

P = 128
D = 128
N = 6250
E = 106250
NB = -(-N // P)
NP = NB * P
LAST = N - (NB - 1) * P
GB = 7
NG = NB // GB
GW = GB * P
EJ = E // P
ER = E - EJ * P
EC = EJ + 1
BT = 10
RING = 2 * BT
CHUNKS = -(-(E // P + NB) // RING) * RING
TURNS = CHUNKS // RING
BATCHES = CHUNKS // BT
BSTRIDE = 12
SLOTS = CHUNKS * P
TAILS = CHUNKS - (-(-E // P))
ATTN = 64
HID = 256
PAY = D + 3
ROW = D + PAY
KY = ATTN + D
AGW = D + ATTN + 1
SW = D + 1
EPS = 1e-5
BANKS = 5
APAIRS = 3
ADEEP = 3
LOW = -1.0e30
FAR = 1.0e6

CONST = {}
_c = 0
for _n, _w in (("ident", P), ("strict", P), ("ones", P), ("iota", 2 * P), ("before", NB), ("upto", NB),
               ("blocks", NB), ("starts", NB), ("part", 1)):
    CONST[_n] = (_c, _w)
    _c += _w
CONST_W = _c

WEIGHTS = {}
_c = 0
for _n, _w in (("Wg", D), ("msg", D), ("lin", D), ("qky", 2 * ATTN + D), ("We", D), ("w1", HID), ("w2", HID),
               ("W0", 3 * D), ("W1", D), ("W2", D), ("self", D), ("inter", D), ("Wm", D), ("ih", 3 * D),
               ("hh", 3 * D), ("g_token", 1), ("ln2_g", 1), ("ln2_b", 1), ("ln3_g", 1), ("ln3_b", 1),
               ("ffn_b1", 2), ("u", 1), ("b0", 1), ("b1", 1), ("b2", 1), ("g0", 1), ("g1", 1), ("g2", 1),
               ("bt0", 1), ("bt1", 1), ("bt2", 1), ("b_ih", 3), ("b_hh", 3)):
    WEIGHTS[_n] = (_c, _w)
    _c += _w
WEIGHTS_W = _c

ROWS = {}
_c = 0
for _n, _w in (("eps", 1), ("Wg_b", D), ("ln1_g", D), ("ln1_b", D), ("msg_b", D), ("lin_b", D), ("Wy_b", D),
               ("We_b", D), ("ffn_b2", D), ("b_msg", D), ("gamma", D), ("beta", D), ("phi", ATTN)):
    ROWS[_n] = (_c, _w)
    _c += _w
ROWS_W = _c


def gnn_kernel(nc, x, src, dst, src_c, dst_c, edge_attr, chunk_numbers, const, weights, rows, out):
    ctx = ExitStack()
    with ctx:
        def sb(name, shape, dt=F32):
            return ctx.enter_context(nc.sbuf_tensor(name, shape, dt))

        def sem(name):
            return ctx.enter_context(nc.semaphore(name))

        def dram(name, shape):
            return nc.dram_tensor(name, shape, F32, kind="Internal").ap()

        payload = dram("payload", (SLOTS, PAY))
        xn_table = dram("xn_table", (NP, D))
        ky_table = dram("ky_table", (NP, KY))
        h2_table = dram("h2_table", (NP, D))
        h3_table = dram("h3_table", (NP, D))

        cst = sb("cst", [P, CONST_W])
        wts = sb("wts", [P, WEIGHTS_W])
        rws = sb("rws", [P, ROWS_W])
        big = sb("big", [P, 2 * NP])
        att = sb("att", [P, NB * SW])
        hst = sb("hst", [P, NB, D])
        qst = sb("qst", [P, NB, ATTN])
        ring = sb("ring", [P, RING, ROW])
        oh_f = sb("onehots", [P, 2 * (BT * P + 64)])
        onehot = oh_f[:, 0:RING * P].rearrange("p (k s) -> p k s", k=RING)
        identb = sb("identb", [P, P], BF16)
        onehotT = sb("onehotT", [P, BT * P])
        meta_s = sb("meta_s", [P, CHUNKS + 2 * BT, 2])
        idx_d = sb("idx_d", [P, EC])
        key_d = sb("key_d", [P, EC])
        low_d = sb("low_d", [P, EC])
        ends = meta_s[:, 0:EC, :]
        blk_s = sb("blk_s", [1, BATCHES * BSTRIDE], I32)
        blk_d = sb("blk_d", [1, (EJ // BT + 1) * BSTRIDE], I32)
        wide = sb("wide", [1, 1], I32)
        idx = sb("idx", [P, ADEEP * BT], I32)
        sidx = sb("sidx", [P, RING], I32)
        padidx = sb("padidx", [P, NB + TAILS], I32)
        kyt = sb("kyt", [P, GB, KY])
        zpr = sb("zpr", [P, 2, BT, ATTN])
        zt, pr = zpr[:, 0], zpr[:, 1]
        pos = zpr[:, :, :, :].rearrange("p a b c -> p (a b c)")[:, 0:EC]
        sc = sb("sc", [P, BT])
        wexp = sb("wexp", [P, BT])
        mrun = sb("mrun", [P, 1])
        mb = sb("mb", [P, 3 * ADEEP])
        deg = sb("deg", [P, NB])
        outn = sb("outn", [P, NB])
        inn = sb("inn", [P, NB])
        st = sb("st", [P, 64])
        bns = sb("bns", [P, 14 * 6])
        mv = sb("mv", [P, GB, 2])
        col = sb("col", [P, 32])
        cnt = sb("cnt", [P, NB])
        mblk = sb("mblk", [P, NB + BT])
        nrm = sb("nrm", [P, 32])
        rootv = sb("rootv", [P, 128])
        tm1 = sb("tm1", [P, NB])
        endt = sb("endt", [P, NB])
        tt = sb("tt", [P, NB])
        chb = sb("chb", [P, P])
        chcol = sb("chcol", [P, 8])
        chint = sb("chint", [P, 8], I32)
        ps = ctx.enter_context(nc.psum_tensor("ps", [P, 8 * 512], F32))

        def c_(n, lo=0, hi=None):
            a, w = CONST[n]
            return cst[:, a + lo:a + (w if hi is None else hi)]

        def w_(n, lo=0, hi=None):
            a, w = WEIGHTS[n]
            return wts[:, a + lo:a + (w if hi is None else hi)]

        def r_(n):
            a, w = ROWS[n]
            return rws[:, a:a + w]

        def over(v, n):
            return v.unsqueeze(1).to_broadcast([P, n, v.shape[1]])

        def along(v, w):
            return v.unsqueeze(2).to_broadcast([P, v.shape[1], w])

        HALVES = ((0, 4), (4, GB))

        def cols(v, q):
            return v[:, HALVES[q][0] * P:HALVES[q][1] * P]

        def c3(v, q):
            return cols(v, q).rearrange("p (b d) -> p b d", d=P)

        def at(t, q):
            lo, hi_ = HALVES[q]
            return bass.ds(t * GB + lo, hi_ - lo)

        def size(q):
            return HALVES[q][1] - HALVES[q][0]

        padrow = kyt[:, 0, 0:PAY]
        ring_f = ring[:, :, :].rearrange("p a b -> p (a b)")
        temps = [ring_f[:, i * GW:(i + 1) * GW] for i in range(5)] + \
                [oh_f[:, i * GW:(i + 1) * GW] for i in range(2)] + [onehotT[:, 0:GW]]
        xgrp = kyt[:, :, :].rearrange("p a b -> p (a b)")[:, 0:GW]
        q_f = qst[:, :, :].rearrange("p a b -> p (a b)")
        early = [q_f[:, i * GW:(i + 1) * GW] for i in range(3)]

        def g3(v):
            return v.rearrange("p (b d) -> p b d", b=GB)

        xn1 = big[:, 0:NP].rearrange("p (b d) -> p b d", d=D)
        agg = big[:, NP:2 * NP].rearrange("p (b d) -> p b d", d=D)
        acc_a = big[:, 0:NB * AGW].rearrange("p (b d) -> p b d", d=AGW)
        acc_p = big[:, 0:(NB + 1) * SW].rearrange("p (b d) -> p b d", d=SW)
        att3 = att[:, :].rearrange("p (b d) -> p b d", d=SW)
        xs = att[:, 0:NP].rearrange("p (b d) -> p b d", d=D)
        h_f = hst[:, :, :].rearrange("p b d -> p (b d)")
        o = NP
        hi_i = big[:, o:o + EC].bitcast(I32)
        lo_i = big[:, o + EC:o + 2 * EC].bitcast(I32)
        masks = [big[:, o + i * EC:o + (i + 1) * EC].bitcast(I32) for i in (3, 0, 5)]
        csums = [big[:, o + i * EC:o + (i + 1) * EC] for i in (4, 1, 6)]
        hi = big[:, o + 2 * EC:o + 3 * EC]
        csum = big[:, o + 4 * EC:o + 5 * EC]
        key_i = big[:, o + 5 * EC:o + 6 * EC].bitcast(I32)
        oth_i = big[:, o + 6 * EC:o + 7 * EC].bitcast(I32)
        assert 7 * EC <= NP
        keyp = hi
        lob = big[:, o + 5 * EC:o + 5 * EC + 7 * P].rearrange("p (g e) -> p g e", e=P)
        behind = big[:, NB * AGW:NB * AGW + BT * (D + 2 * ATTN + 1)].rearrange("p (k d) -> p k d", k=BT)
        arows = [ring[:, 0:BT, :], ring[:, BT:RING, :], behind]
        ky_f = kyt[:, :, :].rearrange("p a b -> p (a b)")
        hots = [oh_f[:, 0:BT * P + 64], oh_f[:, BT * P + 64:2 * (BT * P + 64)], ky_f]
        ahot = [v_[:, 0:BT * P].rearrange("p (k s) -> p k s", k=BT) for v_ in hots]
        abit = [v_[:, BT * 64 + 64:BT * P + 64].bitcast(BF16).rearrange("p (k s) -> p k s", k=BT) for v_ in hots]
        dhot = [oh_f[:, 0:BT * 2 * P].rearrange("p (k s) -> p k s", k=BT),
                q_f[:, 0:BT * 2 * P].rearrange("p (k s) -> p k s", k=BT)]
        chunks = onehotT[:, 0:CHUNKS]
        ge = oh_f[0:NB, 0:CHUNKS]
        one_e = oh_f[:, CHUNKS:CHUNKS + EC]
        padf = col

        psA = ps[:, 0:1024]
        psB = ps[:, 1024:3072]
        psC = ps[:, 3072:4096]
        psT = ps[:, 1024:1024 + BT * 64].bitcast(BF16)
        MCOL = 7 * 512

        def pair_at(h, k):
            return (4 + (h * BT + k) // 2 % APAIRS) * 512 + k % 2 * 256

        s_const = sem("s_const")
        s_weights = sem("s_weights")
        s_keys = sem("s_keys")
        s_dkeys = sem("s_dkeys")
        s_x = sem("s_x")
        dve_step = sem("dve_step")
        act_step = sem("act_step")
        names = ("k_counts k_sums pad_ready pos_ready "
                 "g_in g_out xn1_ready xn1_stored zeroed d_keys d_turned d_wide d_idx k_step k_cnt f_hot f_ps f_row f_idx f_done f_zero f_step f_add added "
                 "n1_agg n1_T n1_Tc n1_msg n1_t n1_lin n1_z n1_qky n1_q n1_ky ky_stored "
                 "a_hot a_T a_Tc a_q a_z a_e a_bm a_mt a_mr a_mb a_w a_free "
                 "n2_sc n2_sce n2_ue n2_T n2_Tc n2_we n2_z n2_hid n2_relu n2_ffn n2_x n2_xg "
                 "n2_o0 n2_r0 n2_ub n2_ubc "
                 "bn_ac bn_bias bn_w l1_mm l1_relu n3_o n3_T n3_hs n3_st "
                 "n4_in n4_m n4_T n4_Tc n4_mm n4_h n4_st n4_sum n4_mean n4_meanc "
                 "n5_s n5_sT n5_sTc n5_m n5_msg n5_T n5_Tc n5_rz n5_rza n5_nn n5_npre n5_n n5_hn n5_hnT n5_out n5_st "
                 "s_var s_std s_root s_rooted s_idx s_hold s_ps s_free").split()
        S = {n: sem(n) for n in names}
        s_pay = [sem(f"s_pay{i}") for i in range(2)]
        s_oh = [sem(f"s_oh{i}") for i in range(2)]
        s_row = [sem(f"s_row{i}") for i in range(ADEEP * BT)]

        SP_OPEN = ("ky_stored", "n3_st", "n5_st")
        DVE_OPEN = ("n2_x", "n1_ky", "n4_h", "n5_out")
        ACT_OPEN = ("n1_q", "n2_r0")
        PE_OPEN = ("n1_lin", "n2_o0", "n4_mm", "n5_hnT")

        def opened(eng, names_, by=2):
            for n in names_:
                eng.sem_inc(S[n], by)

        class Chain:

            def __init__(self, eng, s):
                self.eng, self.s, self.n, self.turn, self.per = eng, s, 0, None, 0

            def __call__(self, ins):
                ins.then_inc(self.s, 1)
                self.n += 1
                at = self.n if self.turn is None else self.turn * self.per + self.n
                self.eng.wait_ge(self.s, at)

            def loop(self, turn, per):
                self.turn, self.per, self.first = turn, per, self.n

            def end(self, turns):
                assert self.n - self.first == self.per, (self.n - self.first, self.per)
                self.turn = None
                self.n = self.first + self.per * turns

        block = ctx.enter_context(nc.Block())

        def hold(eng):
            eng.sem_inc(S["s_hold"], 1)

        SCAT_TURNS = EJ // RING
        SCAT_LEFT = EJ - SCAT_TURNS * RING
        assert SCAT_LEFT == BT and ER > 1
        PADS = NB + TAILS

        def columns_done(slot):
            return SCAT_TURNS + (slot <= SCAT_LEFT)

        def row_base(slot, n):
            if slot >= RING:
                uses = -(-(PADS - (slot - RING)) // BT) + (0 if n < 2 else len(range(2, BATCHES, ADEEP)))
            else:
                uses = columns_done(slot)
                uses += TURNS * (n > 0)
                uses += len(range(slot // BT, BATCHES, ADEEP)) * (n > 1)
                uses += columns_done(slot) * (n > 2)
            return 16 * uses

        PS0 = [0, CHUNKS, 2 * CHUNKS, 2 * CHUNKS + EC]

        def free(eng, n, bt, deep=2):
            eng.wait_ge(S["s_ps"], bt * BT + (PS0[n] + RING - (deep - 1) * BT))

        def product(n, bt, k):
            return bt * BT + (PS0[n] + RING + k + 1)

        IDX0 = [2 * SCAT_TURNS + 2]
        IDX0 += [IDX0[0] + BATCHES]
        IDX0 += [IDX0[1] + BATCHES + 2]
        IDX0 += [IDX0[2] + 2 * SCAT_TURNS + 2]

        FREE0 = {0: 0, 2: CHUNKS, 3: CHUNKS + EC}

        @block.sync
        def _(sp):
            opened(sp, SP_OPEN, 16)
            sp.dma_start(key_i, src).then_inc(s_keys, 16)
            sp.dma_start(cst[:, :], const).then_inc(s_const, 16)
            sp.dma_start(oth_i, dst).then_inc(s_keys, 16)
            sp.dma_start(chunks, chunk_numbers.to_broadcast([P, CHUNKS])).then_inc(s_const, 16)
            sp.dma_start(hst[:, :, :], x).then_inc(s_x, 16)
            sp.dma_start(rws[:, :], rows.to_broadcast([P, ROWS_W])).then_inc(s_weights, 16)
            sp.dma_start(wts[:, :], weights).then_inc(s_weights, 16)
            sp.dma_start(idx_d[:, :].bitcast(I32), src_c).then_inc(s_dkeys, 16)
            sp.dma_start(low_d[:, :].bitcast(I32), dst_c).then_inc(s_dkeys, 16)
            ea = edge_attr[0:EJ * P, :].rearrange("(p j) f -> p j f", j=EJ)
            for h in range(2):
                sp.dma_start(ring[:, h * BT:(h + 1) * BT, D:2 * D], ea[:, h * BT:(h + 1) * BT, :])\
                    .then_inc(s_pay[h], 16)
            with sp.Fori(1, SCAT_TURNS) as turn:
                for h in range(2):
                    for k in range(BT):
                        sp.wait_ge(s_row[h * BT + k], turn * 16)
                    sp.dma_start(ring[:, h * BT:(h + 1) * BT, D:2 * D],
                                 ea[:, bass.ds(turn * RING + h * BT, BT), :]).then_inc(s_pay[h], 16)
            for k in range(BT):
                sp.wait_ge(s_row[k], SCAT_TURNS * 16)
            sp.dma_start(ring[:, 0:BT, D:2 * D], ea[:, SCAT_TURNS * RING:EJ, :]).then_inc(s_pay[0], 16)
            sp.wait_ge(s_row[BT], SCAT_TURNS * 16)
            sp.dma_start(ring[0:ER, BT, D:2 * D], edge_attr[EJ * P:E, :]).then_inc(s_pay[1], 16)
            xt = xn_table.rearrange("(b p) d -> p b d", p=P)
            sp.wait_ge(S["xn1_ready"], NG)
            sp.dma_start(xt, xn1).then_inc(S["xn1_stored"], 16)
            for k in range(ADEEP * BT):
                sp.wait_ge(s_row[k], row_base(k, 0))
            pl = payload.rearrange("(c p) w -> p c w", p=P)
            with sp.Fori(0, TURNS) as turn:
                for h in range(2):
                    free(sp, 0, turn * 2 + h)
                    sp.dma_start(ring[:, h * BT:(h + 1) * BT, D:ROW],
                                 pl[:, bass.ds(turn * RING + h * BT, BT), :]).then_inc(s_pay[h], 16)
            kt = ky_table.rearrange("(b p) d -> p b d", p=P)
            with sp.Fori(0, NG) as t:
                sp.wait_ge(S["n1_ky"], t * 2 + 4)
                sp.dma_start(kt[:, bass.ds(t * GB, GB), :], kyt[:, :, :]).then_inc(S["ky_stored"], 16)
            with sp.Fori(0, NG) as t:
                sp.wait_ge(S["zeroed"], 2)
                sp.wait_ge(S["n2_x"], t * 2 + 2)
                sp.dma_start(g3(xgrp), x[:, bass.ds(t * GB, GB), :]).then_inc(S["n2_xg"], 16)
            h2 = h2_table.rearrange("(b p) d -> p b d", p=P)
            with sp.Fori(0, NG) as t:
                sp.wait_ge(S["n3_hs"], t + 2)
                sp.dma_start(h2[:, bass.ds(t * GB, GB), :], g3(temps[4])).then_inc(S["n3_st"], 16)
            h3 = h3_table.rearrange("(b p) d -> p b d", p=P)
            sp.wait_ge(S["n4_h"], 2 * NG + 2)
            sp.dma_start(h3, hst[:, :, :]).then_inc(S["n4_st"], 16)
            with sp.Fori(0, NG) as t:
                sp.wait_ge(S["n5_out"], t * 2 + 4)
                sp.dma_start(out[:, bass.ds(t * GB, GB), :], g3(temps[7])).then_inc(S["n5_st"], 16)
            sp.wait_ge(S["n5_st"], 16 * NG + 16)

        @block.gpsimd
        def _(pool):
            def batch(n, bt, lot, table, width, count=BT, deep=2):
                pool.wait_ge(S["s_idx"], bt + (IDX0[n] + 1))
                pool.wait_ge(S["s_ps"], bt * BT + (PS0[n] + RING - (deep - 1) * BT - BT // 2))
                hold(pool)
                for k in range(lot, lot + count):
                    if k == lot + BT // 2:
                        free(pool, n, bt, deep)
                        hold(pool)
                    to = ring[:, k, 0:width] if k < RING else arows[2][:, k - RING, 0:width]
                    pool.indirect_dma_start(
                        out=to, out_offset=None, in_=table,
                        in_offset=bass.IndirectOffsetOnAxis(ap=idx[:, k:k + 1], axis=0)).then_inc(s_row[k], 16)

            def by_dst(n, table):
                with pool.Fori(0, SCAT_TURNS) as turn:
                    for h in range(2):
                        batch(n, turn * 2 + h, h * BT, table, D)
                for h, count in ((0, BT), (1, 1)):
                    batch(n, SCAT_TURNS * 2 + h, h * BT, table, D, count)
                w = pool.alloc_register(f"pool_wide{n}")
                pool.load([w], wide[0:1, 0:1])
                with pool.If_ne(w, 0):
                    pool.wait_ge(S["s_ps"], PS0[n] + RING + EC)
                    with pool.Fori(0, EC) as c:
                        pool.wait_ge(S["f_done"], c + (1 + EC * (n - 2)))
                        hold(pool)
                        pool.tensor_copy(idx[:, 0:1], idx_d[:, bass.ds(c, 1)]).then_inc(S["f_idx"], 1)
                        pool.wait_ge(S["f_idx"], c + (1 + EC * (n - 2)))
                        hold(pool)
                        pool.indirect_dma_start(
                            out=ring[:, 0, 0:D], out_offset=None, in_=table,
                            in_offset=bass.IndirectOffsetOnAxis(ap=idx[:, 0:1], axis=0)).then_inc(S["f_row"], 16)

            pool.wait_ge(S["pad_ready"], 1)
            for i in range(PADS):
                if i >= BT:
                    pool.wait_ge(s_row[RING + i % BT], 16 * (i // BT))
                pool.indirect_dma_start(
                    out=payload, out_offset=bass.IndirectOffsetOnAxis(ap=padidx[:, i:i + 1], axis=0),
                    in_=padrow[:, :], in_offset=None, bounds_check=SLOTS - 1, oob_is_err=False)\
                    .then_inc(s_row[RING + i % BT], 16)
            pool.wait_ge(S["pos_ready"], 1)

            def scatter(turn, h, first=False):
                lot = slice(h * BT, (h + 1) * BT)
                pool.wait_ge(s_pay[h], turn * 16 + 16)
                for k in range(h * BT, (h + 1) * BT):
                    if not first:
                        pool.wait_ge(s_row[k], turn * 16)
                hold(pool)
                pool.tensor_copy(ring[:, lot, 2 * D + 1:ROW], ends[:, bass.ds(turn * RING + h * BT, BT), :])
                pool.tensor_copy(sidx[:, lot], pos[:, bass.ds(turn * RING + h * BT, BT)])\
                    .then_inc(S["s_idx"], 1)
                pool.wait_ge(S["s_idx"], turn * 2 + h + 1)
                hold(pool)
                for k in range(h * BT, (h + 1) * BT):
                    pool.indirect_dma_start(
                        out=payload, out_offset=bass.IndirectOffsetOnAxis(ap=sidx[:, k:k + 1], axis=0),
                        in_=ring[:, k, D:ROW], in_offset=None).then_inc(s_row[k], 16)

            for h in range(2):
                scatter(0, h, True)
            with pool.Fori(1, SCAT_TURNS) as turn:
                for h in range(2):
                    scatter(turn, h)
            pool.wait_ge(s_pay[0], SCAT_TURNS * 16 + 16)
            pool.wait_ge(s_pay[1], SCAT_TURNS * 16 + 16)
            j = SCAT_TURNS * RING
            pool.tensor_copy(ring[:, 0:BT + 1, 2 * D + 1:ROW], ends[:, j:j + BT + 1, :])
            pool.tensor_copy(sidx[:, 0:BT + 1], pos[:, j:j + BT + 1]).then_inc(S["s_idx"], 2)
            pool.wait_ge(S["s_idx"], 2 * SCAT_TURNS + 2)
            for k in range(BT + 1):
                n = P if k < BT else ER
                pool.indirect_dma_start(
                    out=payload, out_offset=bass.IndirectOffsetOnAxis(ap=sidx[0:n, k:k + 1], axis=0),
                    in_=ring[0:n, k, D:ROW], in_offset=None).then_inc(s_row[k], 16)

            pool.wait_ge(S["xn1_stored"], 16)
            with pool.Fori(0, TURNS) as turn:
                for h in range(2):
                    batch(0, turn * 2 + h, h * BT, xn_table, D)

            pool.wait_ge(S["ky_stored"], 16 * NG + 16)
            pool.wait_ge(S["n1_q"], 2 * NG + 2)
            pool.wait_ge(S["zeroed"], 1)
            with pool.Fori(0, BATCHES // ADEEP) as turn:
                for h in range(ADEEP):
                    batch(1, turn * ADEEP + h, h * BT, ky_table, KY, deep=ADEEP)
            assert BATCHES % ADEEP == 1
            batch(1, BATCHES - 1, 0, ky_table, KY, deep=ADEEP)
            pool.wait_ge(S["n3_st"], 16 * NG + 16)
            pool.wait_ge(S["zeroed"], 3)
            by_dst(2, h2_table)
            pool.wait_ge(S["n4_st"], 16)
            pool.wait_ge(S["zeroed"], 4)
            by_dst(3, h3_table)

        @block.vector
        def _(dve):
            chain = Chain(dve, dve_step)
            v = nc.vector

            def bucket():
                dve.wait_ge(s_keys, 32)
                chain(v.tensor_scalar(hi_i, key_i, 7, None, ALU.arith_shift_right))
                chain(v.tensor_scalar(lo_i, key_i, P - 1, None, ALU.bitwise_and))
                v.tensor_copy(ends[:, :, 0], lo_i)
                v.tensor_copy(ends[:, :, 1], oth_i)
                chain(v.tensor_copy(hi, hi_i))
                chain(v.memset(pos, 0.0))
                a = CONST["blocks"][0]
                spare = (csums[0], csums[1], csums[2], csums[0], csums[1], csums[2], masks[0].bitcast(F32))
                dve.sem_inc(S["k_cnt"], 2)
                with dve.Fori(0, NB // 7) as b7:
                    for j in range(7):
                        dve.wait_ge(S["k_cnt"], b7 * 7 + (j + 1))
                        v.tensor_scalar(spare[j], hi, cst[:, bass.ds(b7 * 7 + (a + j), 1)], 0.0, ALU.is_equal, ALU.add,
                                        accum_out=cnt[:, bass.ds(b7 * 7 + j, 1)]).then_inc(S["k_cnt"], 1)
                dve.wait_ge(S["k_cnt"], NB + 2)
                v.memset(st[:, 0:1], 0.0).then_inc(S["k_counts"], 1)
                dve.wait_ge(S["k_sums"], 1)
                chain(v.tensor_scalar(chint[0:NB, 0:1], psC[0:NB, 0:1], float(P - 1), None, ALU.add))
                chain(v.tensor_scalar(chint[0:NB, 1:2], chint[0:NB, 0:1], 7, None, ALU.arith_shift_right))
                chain(v.tensor_scalar(chcol[0:NB, 0:1], chint[0:NB, 1:2], 1.0, None, ALU.max))
                v.tensor_scalar(chb[0:NB, :], c_("ones")[0:NB, :], chcol[0:NB, 0:1], float(P), ALU.mult, ALU.mult)\
                    .then_inc(S["k_counts"], 1)
                dve.wait_ge(S["k_sums"], 2)
                chain(v.tensor_scalar(tm1[:, :], psC[:, 64:64 + NB], 1.0, None, ALU.subtract))
                chain(v.tensor_copy(endt[:, :], psC[:, 128:128 + NB]))
                chain(v.tensor_copy(chcol[0:NB, 1:2], psC[0:NB, 256:257]))
                v.tensor_scalar(ge, chunks[0:NB, :], chcol[0:NB, 1:2], None, ALU.is_ge)\
                    .then_inc(S["k_counts"], 1)
                chain(v.tensor_scalar(tt[:, :], psC[:, 192:192 + NB], c_("part"), None, ALU.add))
                chain(v.tensor_tensor(cnt[:, :], tt[:, :], endt[:, :], ALU.is_ge))
                chain(v.scalar_tensor_tensor(padidx[:, 0:NB], cnt[:, :], FAR, tt[:, :], ALU.mult, ALU.add))
                chain(v.tensor_scalar(chcol[:, 2:3], endt[:, NB - 1:NB], c_("part"), None, ALU.add))
                v.tensor_scalar(padidx[:, NB:NB + TAILS], chunks[:, 0:TAILS], float(P), chcol[:, 2:3],
                                ALU.mult, ALU.add).then_inc(S["pad_ready"], 1)
                dve.wait_ge(S["k_sums"], 3)
                chain(v.tensor_scalar(
                    blk_s[0:1, :].rearrange("p (b s) -> p b s", s=BSTRIDE)[:, :, 0:BT],
                    psA[0:1, 0:CHUNKS].rearrange("p (b k) -> p b k", k=BT), float(NB - 1), None, ALU.min))
                def block_mask(b, i):
                    return v.tensor_scalar(masks[i], hi, cst[:, bass.ds(b + a, 1)], None, ALU.is_equal)

                def block_count(b, i):
                    return v.tensor_tensor_scan(csums[i], one_e, masks[i], tm1[:, bass.ds(b, 1)], ALU.mult, ALU.add)

                chain(block_mask(0, 0))
                chain(block_count(0, 0))
                chain(block_mask(1, 1))
                dve.sem_inc(S["k_step"], 3)
                with dve.Fori(0, (NB - 1) // 3) as b3:
                    for j in range(1, 4):
                        b = b3 * 3 + j
                        dve.wait_ge(S["k_step"], b3 * 9 + (3 * j - 1))
                        block_count(b, j % 3).then_inc(S["k_step"], 1)
                        dve.wait_ge(S["k_step"], b3 * 9 + 3 * j)
                        block_mask(b + 1, (j + 1) % 3).then_inc(S["k_step"], 1)
                        v.copy_predicated(pos, masks[(j - 1) % 3], csums[(j - 1) % 3]).then_inc(S["k_step"], 1)
                assert (NB - 1) % 3 == 0
                dve.wait_ge(S["k_step"], 3 * NB)
                chain(v.copy_predicated(pos, masks[(NB - 1) % 3], csums[(NB - 1) % 3]))
                v.memset(st[:, 0:1], 0.0).then_inc(S["pos_ready"], 1)

            def norm(turn, x3, z3, lo=0, n=GB, done=None):
                hold(dve)
                for k in range(n):
                    ins = v.bn_stats(bns[:, (lo + k) * 6:(lo + k) * 6 + 6], x3[:, k, :])
                chain(ins)
                hold(dve)
                for k in range(n):
                    ins = v.bn_aggr(mv[:, lo + k, :], bns[:, (lo + k) * 6:(lo + k) * 6 + 6])
                chain(ins)
                v.tensor_scalar(nrm[:, 16 + lo:16 + lo + n], mv[:, lo:lo + n, 1], EPS, None, ALU.add)\
                    .then_inc(S["s_var"], 1)
                dve.wait_ge(S["s_std"], turn + 1)
                chain(v.reciprocal(nrm[:, lo:lo + n], nrm[:, 24 + lo:24 + lo + n]))
                for k in range(n):
                    ins = v.tensor_scalar(z3[:, k, :], x3[:, k, :], mv[:, lo + k, 0:1], nrm[:, lo + k:lo + k + 1],
                                          ALU.subtract, ALU.mult)
                if done:
                    ins.then_inc(S[done], 1)
                else:
                    chain(ins)

            def root(at, value, out_):
                n = value.shape[1]
                v.tensor_copy(rootv[:, 0:n], value).then_inc(S["s_root"], 1)
                dve.wait_ge(S["s_rooted"], at)
                chain(v.reciprocal(out_, rootv[:, 64:64 + n]))

            def by_dst_chunks():
                G = -(-EC // P)
                last = EC - (G - 1) * P
                dve.wait_ge(s_dkeys, 32)
                chain(v.tensor_copy(key_d[:, :], low_d[:, :].bitcast(I32)))
                v.tensor_copy(csum, idx_d[:, :].bitcast(I32)).then_inc(S["d_idx"], 1)
                dve.wait_ge(S["d_idx"], 1)
                chain(v.tensor_copy(idx_d[:, :], csum))
                chain(v.tensor_scalar(csum, key_d[:, :], 0.0, FAR, ALU.is_lt, ALU.mult))
                v.tensor_tensor(keyp, key_d[:, :], csum, ALU.add).then_inc(S["d_keys"], 1)
                dve.wait_ge(S["d_turned"], 1)
                chain(v.memset(st[:, 0:16], 0.0))
                for at, op in ((0, ALU.min), (1, ALU.max)):
                    t_ = psB[:, at * 1024:at * 1024 + G * P].rearrange("p (g e) -> p g e", e=P)
                    v.tensor_reduce(st[:, at * 8:at * 8 + G - 1], t_[:, 0:G - 1, :], AX.X, op)
                    chain(v.tensor_reduce(st[0:last, at * 8 + G - 1:at * 8 + G], t_[0:last, G - 1, :], AX.X, op))
                sti = rootv[:, 0:16].bitcast(I32)
                chain(v.tensor_copy(sti, st[:, 0:16]))
                chain(v.tensor_scalar(sti, sti, 7, None, ALU.arith_shift_right))
                chain(v.tensor_copy(st[:, 0:16], sti))
                chain(v.tensor_tensor(st[:, 16:16 + G], st[:, 8:8 + G], st[:, 0:G], ALU.subtract))
                chain(v.reduce_max(st[:, 24:25], st[:, 16:16 + G], AX.X))
                v.tensor_tensor(lob, over(c_("ones"), G), along(st[:, 0:G], P), ALU.mult).then_inc(S["d_keys"], 1)
                dve.wait_ge(S["d_turned"], 2)
                chain(v.tensor_scalar(low_d[:, :], psA[:, 0:EC], float(P), None, ALU.mult))
                chain(v.tensor_tensor(key_d[:, :], key_d[:, :], low_d[:, :], ALU.subtract))
                v.tensor_copy(blk_d[0:1, :].rearrange("p (b s) -> p b s", s=BSTRIDE)[:, 0:EJ // BT, 0:BT],
                              psA[0:1, 0:EJ].rearrange("p (b k) -> p b k", k=BT))
                v.tensor_copy(blk_d[0:1, EJ // BT * BSTRIDE:EJ // BT * BSTRIDE + 1], psA[0:1, EJ:EC])
                chain(v.reduce_max(st[0:1, 26:27], psC[0:1, 0:P], AX.X))
                v.tensor_scalar(wide[:, :], st[0:1, 26:27], 2.0, None, ALU.is_ge).then_inc(S["d_wide"], 1)

            regs = [dve.alloc_register(f"dve_blk{k}") for k in range(BT)]

            def blocks(table, bt, count=BT):
                dve.load(regs[:count], table[0:1, bass.ds(bt * BSTRIDE, count)])
                return [dve.snap(r, min_val=0, max_val=NB - 1) for r in regs[:count]]

            def by_dst(n):
                def hot(bt, h, count=BT):
                    free(dve, n, bt)
                    v.tensor_tensor(dhot[h][:, 0:count, :], over(c_("iota"), count),
                                    along(key_d[:, bass.ds(bt * BT, count)], 2 * P), ALU.is_equal)\
                        .then_inc(s_oh[h], 1)

                def sums(bt, h, count=BT):
                    bs = blocks(blk_d, bt, count)
                    for k in range(count):
                        bank = (1 + (h * BT + k) % BANKS) * 512
                        a = acc_p[:, bass.ds(bs[k], 2), :].rearrange("p a d -> p (a d)")
                        dve.wait_ge(S["s_ps"], product(n, bt, k))
                        dve.wait_ge(S["s_free"], bt * BT + (BANKS + FREE0[n] + k))
                        v.tensor_tensor(a, a, ps[:, bank:bank + 2 * SW], ALU.add).then_inc(S["s_free"], 1)

                hot(0, 0)
                with dve.Fori(0, SCAT_TURNS) as turn:
                    for h in range(2):
                        hot(turn * 2 + (h + 1), 1 - h)
                        sums(turn * 2 + h, h)
                hot(2 * SCAT_TURNS + 1, 1, 1)
                sums(2 * SCAT_TURNS, 0)
                sums(2 * SCAT_TURNS + 1, 1, 1)
                dve.wait_ge(S["s_free"], BANKS + FREE0[n] + EC)
                w = dve.alloc_register(f"dve_wide{n}")
                dve.load([w], wide[0:1, 0:1])
                with dve.If_ne(w, 0):
                    v.memset(big[:, 0:(NB + 1) * SW], 0.0).then_inc(S["f_zero"], 1)
                    dve.wait_ge(S["f_zero"], n - 1)
                    with dve.Fori(0, EC) as c:
                        with dve.Fori(0, NB) as b:
                            i = c * NB + b
                            v.tensor_tensor(st[:, 1:2], key_d[:, bass.ds(c, 1)], low_d[:, bass.ds(c, 1)], ALU.add)\
                                .then_inc(S["f_step"], 1)
                            dve.wait_ge(S["f_step"], i * 2 + (1 + 2 * NB * EC * (n - 2)))
                            v.tensor_tensor(st[:, 0:1], st[:, 1:2], c_("starts")[:, bass.ds(b, 1)], ALU.subtract)\
                                .then_inc(S["f_step"], 1)
                            dve.wait_ge(S["f_step"], i * 2 + (2 + 2 * NB * EC * (n - 2)))
                            v.tensor_scalar(onehot[:, 0, :], c_("iota", 0, P), st[:, 0:1], None, ALU.is_equal)\
                                .then_inc(S["f_hot"], 1)
                            dve.wait_ge(S["f_ps"], i + (1 + NB * EC * (n - 2)))
                            a = acc_p[:, bass.ds(b, 1), :].rearrange("p a d -> p (a d)")
                            v.tensor_tensor(a, a, ps[:, 0:SW], ALU.add).then_inc(S["f_add"], 1)
                            dve.wait_ge(S["f_add"], i + (1 + NB * EC * (n - 2)))
                        v.memset(st[:, 2:3], 0.0).then_inc(S["f_done"], 1)
                v.memset(st[:, 3:4], 0.0).then_inc(S["added"], 1)

            opened(dve, DVE_OPEN)
            opened(dve, ("n3_hs", "f_done"), 1)
            v.memset(padrow[:, :], 0.0)
            v.memset(rootv[:, :], 1.0)
            v.memset(meta_s[:, CHUNKS:CHUNKS + 2 * BT, :], 0.0)
            chain(v.memset(one_e, 1.0))
            chain(v.memset(padrow[:, D + 1:D + 2], LOW))
            chain(v.memset(ring[:, :, 2 * D:2 * D + 1], 1.0))
            dve.wait_ge(s_const, 32)
            v.tensor_copy(identb[:, :], c_("ident"))
            bucket()

            dve.wait_ge(s_x, 16)
            dve.wait_ge(s_weights, 32)
            with dve.Fori(0, NG) as t:
                chain.loop(t, 5)
                hg = hst[:, bass.ds(t * GB, GB), :]
                norm(t, hg, g3(early[0]))
                chain(v.tensor_scalar(hg, g3(early[0]), 0.0, None, ALU.max))
            chain.end(NG)
            v.reduce_sum(early[2][:, 0:D], hst[:, :, :].rearrange("p b d -> p d b"), AX.X).then_inc(S["g_in"], 1)
            dve.wait_ge(S["g_out"], 1)
            chain(v.scalar_tensor_tensor(col[:, 0:1], psC[:, 0:1], 1.0 / N, w_("g_token"), ALU.mult, ALU.add))
            v.tensor_scalar(chb[:, :], c_("ones"), col[:, 0:1], None, ALU.mult).then_inc(S["g_in"], 1)
            dve.wait_ge(S["g_out"], 2)
            chain(v.tensor_tensor(early[2][:, 0:D], psC[:, 64:64 + D], r_("Wg_b"), ALU.add))
            chain(v.tensor_tensor(hst[:, :, :], hst[:, :, :], over(early[2][:, 0:D], NB), ALU.add))
            with dve.Fori(0, NG) as t:
                chain.loop(t, 5)
                xg = xn1[:, bass.ds(t * GB, GB), :]
                norm(t + NG, hst[:, bass.ds(t * GB, GB), :], g3(early[0]))
                chain(v.tensor_tensor(g3(early[1]), g3(early[0]), over(r_("ln1_g"), GB), ALU.mult))
                v.tensor_tensor(xg, g3(early[1]), over(r_("ln1_b"), GB), ALU.add).then_inc(S["xn1_ready"], 1)
            chain.end(NG)
            by_dst_chunks()
            chain(v.memset(big[:, NP:2 * NP], 0.0))
            chain(v.memset(att[:, :], 0.0))
            chain(v.tensor_scalar(col[:, 1:2], r_("eps"), 1.0, None, ALU.add))
            dve.sem_inc(S["s_free"], BANKS)

            def p_hot(bt, h, use):
                dve.wait_ge(s_pay[h], use * 16 + 16 + 16 * (SCAT_TURNS + 1))
                lot = slice(h * BT, (h + 1) * BT)
                chain(v.tensor_copy(meta_s[:, bass.ds(bt * BT, BT), :], ring[:, lot, 2 * D + 1:ROW]))
                v.tensor_tensor(onehot[:, lot, :], over(c_("iota", 0, P), BT),
                                along(meta_s[:, bass.ds(bt * BT, BT), 0], P), ALU.is_equal).then_inc(s_oh[h], 1)

            def p_sums(bt, h, bs, chunks_):
                for k in chunks_:
                    bank = (1 + (h * BT + k) % BANKS) * 512
                    p = ps[:, bank:bank + D + SW]
                    dve.wait_ge(S["s_ps"], product(0, bt, k))
                    dve.wait_ge(S["s_free"], bt * BT + (BANKS + k))
                    a = agg[:, bass.ds(bs[k], 1), :].rearrange("p a d -> p (a d)")
                    v.tensor_tensor(a, a, p[:, 0:D], ALU.add)
                    a = att3[:, bass.ds(bs[k], 1), :].rearrange("p a d -> p (a d)")
                    v.tensor_tensor(a, a, p[:, D:D + SW], ALU.add).then_inc(S["s_free"], 1)

            p_hot(0, 0, 0)
            with dve.Fori(0, TURNS - 1) as turn:
                chain.loop(turn, 2)
                for h in range(2):
                    bt = turn * 2 + h
                    bs = blocks(blk_s, bt)
                    p_sums(bt, h, bs, range(0, BT // 2))
                    p_hot(bt + 1, 1 - h, turn + h)
                    p_sums(bt, h, bs, range(BT // 2, BT))
            chain.end(TURNS - 1)
            p_hot(BATCHES - 1, 1, TURNS - 1)
            for h in range(2):
                bt = BATCHES - 2 + h
                p_sums(bt, h, blocks(blk_s, bt), range(0, BT))
            dve.wait_ge(S["s_free"], BANKS + CHUNKS)

            chain(v.tensor_copy(deg[:, :], att3[:, :, D]))
            with dve.Fori(0, NG) as t:
                chain.loop(t, 14)
                T = temps
                for q in range(2):
                    chain(v.tensor_tensor(c3(T[3], q), over(r_("msg_b"), size(q)), along(deg[:, at(t, q)], D), ALU.mult))
                    dve.wait_ge(S["n1_msg"], t * 2 + (q + 1))
                    chain(v.scalar_tensor_tensor(c3(T[2], q), xn1[:, at(t, q), :], col[:, 1:2],
                                                 c3(psC, q), ALU.mult, ALU.add))
                    v.tensor_tensor(cols(T[2], q), cols(T[2], q), cols(T[3], q), ALU.add).then_inc(S["n1_t"], 1)
                for q in range(2):
                    dve.wait_ge(S["n1_lin"], t * 2 + (q + 3))
                    chain(v.tensor_tensor(c3(T[3], q), c3(psC, q), over(r_("lin_b"), size(q)), ALU.add))
                    hg = hst[:, at(t, q), :]
                    chain(v.scalar_tensor_tensor(hg, c3(T[3], q), 0.0, hg, ALU.max, ALU.add))
                    norm(t * 2 + (2 * NG + q), hg, c3(T[4], q), HALVES[q][0], size(q), "n1_z")
                for q in range(2):
                    lo, hi_ = HALVES[q]
                    dve.wait_ge(S["n1_q"], t * 2 + (q + 3))
                    dve.wait_ge(S["ky_stored"], t * 16 + 16)
                    pq = psB[:, lo * HID:hi_ * HID].rearrange("p (b d) -> p b d", d=HID)
                    v.tensor_copy(kyt[:, lo:hi_, 0:ATTN], pq[:, :, ATTN:2 * ATTN])
                    v.tensor_tensor(kyt[:, lo:hi_, ATTN:KY], pq[:, :, 2 * ATTN:HID], over(r_("Wy_b"), size(q)), ALU.add)\
                        .then_inc(S["n1_ky"], 1)
            chain.end(NG)

            dve.wait_ge(S["n1_q"], 2 * NG + 2)
            chain(v.memset(behind[:, :, D + 2 * ATTN:D + 2 * ATTN + 1], 1.0))
            chain(v.memset(ring[:, :, D + 2 * ATTN:D + 2 * ATTN + 1], 1.0))
            chain(v.memset(mrun[:, :], LOW))
            v.memset(mb[:, :], LOW).then_inc(S["zeroed"], 1)
            dve.sem_inc(S["a_free"], 2 * APAIRS)

            def a_hot(bt, h):
                free(dve, 1, bt, ADEEP)
                v.tensor_tensor(abit[h], over(c_("iota", 0, P), BT), along(meta_s[:, bass.ds(bt * BT, BT), 0], P),
                                ALU.is_equal).then_inc(S["a_hot"], 1)

            def a_args(bt, h, use):
                for k in range(h * BT, (h + 1) * BT):
                    dve.wait_ge(s_row[k], use * 16 + (16 + row_base(k, 1)))
                dve.wait_ge(S["a_q"], bt + 1)
                v.tensor_tensor(zt, ps[:, 0:BT * ATTN].rearrange("p (c a) -> p c a", a=ATTN),
                                arows[h][:, :, 0:ATTN], ALU.add).then_inc(S["a_z"], 1)

            def a_scores(bt, h):
                dve.wait_ge(S["a_e"], bt + 1)
                chain(v.tensor_tensor(pr, arows[h][:, :, KY:KY + ATTN], over(r_("phi"), BT), ALU.mult))
                chain(v.reduce_sum(sc[:, :], pr, AX.X))
                chain(v.scalar_tensor_tensor(sc[:, :], meta_s[:, bass.ds(bt * BT, BT), 0], 0.0, sc[:, :],
                                             ALU.min, ALU.add))
                v.reduce_max(st[:, 24:25], sc[:, :], AX.X).then_inc(S["a_bm"], 1)

            def a_max(bt):
                dve.wait_ge(S["a_mt"], bt + 1)
                chain(v.reduce_max(st[0:1, 25:26], ps[0:1, MCOL:MCOL + P], AX.X))
                v.tensor_tensor(mrun[0:1, 0:1], mrun[0:1, 0:1], st[0:1, 25:26], ALU.max).then_inc(S["a_mr"], 1)

            def a_sums(bt, h, bs, pairs):
                for k in range(2 * pairs.start, 2 * pairs.stop):
                    dve.wait_ge(S["s_ps"], product(1, bt, k | 1))
                    dve.wait_ge(S["a_free"], bt * BT + (2 * APAIRS + k))
                    a = acc_a[:, bass.ds(bs[k], 1), :].rearrange("p a d -> p (a d)")
                    p = ps[:, pair_at(h, k):pair_at(h, k) + AGW]
                    if k == 0:
                        v.tensor_copy(mblk[:, bass.ds(bs[0], BT)], mb[:, h:h + 1].to_broadcast([P, BT]))
                        ins = v.scalar_tensor_tensor(a, a, mb[:, 6 + h:7 + h], p, ALU.mult, ALU.add)
                    else:
                        ins = v.tensor_tensor(a, a, p, ALU.add)
                    ins.then_inc(S["a_free"], 1)

            a_hot(0, 0)
            a_hot(1, 1)
            chain(v.memset(big[:, 0:NB * AGW], 0.0))
            a_args(0, 0, 0)
            a_scores(0, 0)
            a_max(0)
            with dve.Fori(0, BATCHES // ADEEP) as turn:
                chain.loop(turn, ADEEP * 4)
                for h in range(ADEEP):
                    bt, h1, h2 = turn * ADEEP + h, (h + 1) % ADEEP, (h + 2) % ADEEP
                    bs = blocks(blk_s, bt)
                    a_args(bt + 1, h1, turn + (h + 1) // ADEEP)
                    a_hot(bt + 2, h2)
                    a_scores(bt + 1, h1)
                    a_sums(bt, h, bs, range(0, 1))
                    a_max(bt + 1)
                    a_sums(bt, h, bs, range(1, BT // 2))
            chain.end(BATCHES // ADEEP)
            bs = blocks(blk_s, BATCHES - 1)
            a_sums(BATCHES - 1, 0, bs, range(0, BT // 2))
            dve.wait_ge(S["a_free"], 2 * APAIRS + CHUNKS)
            chain(v.memset(st[:, 42:43], 0.0))
            v.memset(st[:, 43:44], 0.0).then_inc(S["zeroed"], 1)

            chain(v.tensor_scalar(deg[:, :], deg[:, :], 1.0, None, ALU.max))
            chain(v.reciprocal(tt[:, :], deg[:, :]))
            root(1, deg[:, :], outn[:, :])
            v.tensor_scalar(cnt[:, :], mblk[:, 0:NB], mb[:, 0:1], None, ALU.subtract).then_inc(S["n2_sc"], 1)
            dve.wait_ge(S["n2_sce"], 1)
            dve.wait_ge(S["n2_ub"], 1)
            v.tensor_tensor(col[:, 2:3], psC[:, 0:1], w_("b0"), ALU.add).then_inc(S["n2_ubc"], 1)
            with dve.Fori(0, NG) as t:
                chain.loop(t, 4 + 2 * (5 + 3) + 2 * (4 + 4))
                T = temps
                gs = bass.ds(t * GB, GB)
                chain(v.tensor_tensor(st[:, 40:40 + GB], acc_a[:, gs, AGW - 1], endt[:, gs], ALU.mult))
                chain(v.tensor_scalar(st[:, 48:48 + GB], st[:, 40:40 + GB], 1e-9, None, ALU.add))
                chain(v.reciprocal(st[:, 40:40 + GB], st[:, 48:48 + GB]))
                chain(v.tensor_tensor(st[:, 48:48 + GB], st[:, 40:40 + GB], endt[:, gs], ALU.mult))
                for q in range(2):
                    lo, hi_ = HALVES[q]
                    g, hg = at(t, q), hst[:, at(t, q), :]
                    chain(v.tensor_tensor(c3(T[3], q), over(r_("We_b"), size(q)), along(acc_a[:, g, AGW - 1], D), ALU.mult))
                    dve.wait_ge(S["n2_we"], t * 2 + (q + 1))
                    chain(v.tensor_tensor(c3(T[2], q), c3(psB, q), acc_a[:, g, 0:D], ALU.add))
                    chain(v.tensor_tensor(cols(T[2], q), cols(T[2], q), cols(T[3], q), ALU.add))
                    chain(v.tensor_tensor(c3(T[2], q), c3(T[2], q), along(st[:, 48 + lo:48 + hi_], D), ALU.mult))
                    chain(v.tensor_tensor(hg, hg, c3(T[2], q), ALU.add))
                    norm(t * 4 + (4 * NG + q), hg, c3(T[4], q), lo, size(q), "n2_z")
                for q in range(2):
                    lo, hi_ = HALVES[q]
                    g, hg = at(t, q), hst[:, at(t, q), :]
                    v.tensor_tensor(c3(T[7], q), att3[:, g, 0:D], along(tt[:, g], D), ALU.mult)
                    dve.wait_ge(S["n2_ffn"], t * 2 + (q + 1))
                    chain(v.tensor_tensor(c3(T[2], q), c3(psA, q), over(r_("ffn_b2"), size(q)), ALU.add))
                    chain(v.tensor_tensor(c3(T[2], q), c3(T[2], q), hg, ALU.add))
                    dve.wait_ge(S["n2_xg"], t * 16 + 16)
                    chain(v.tensor_tensor(cols(T[2], q), cols(T[2], q), cols(xgrp, q), ALU.add))
                    norm(t * 4 + (4 * NG + 2 + q), c3(T[2], q), c3(T[4], q), lo, size(q))
                    v.tensor_scalar(cols(T[4], q), cols(T[4], q), 0.0, None, ALU.max).then_inc(S["n2_x"], 1)
                for q in range(2):
                    chain(v.tensor_copy(xs[:, at(t, q), :], c3(T[2], q)))
            chain.end(NG)

            def batch_norm(i, arr, signal, before, each):
                n = 0
                for g in range(NG):
                    dve.wait_ge(S[signal], before + each * (g + 1))
                    for q in range(2):
                        lo = g * GW + HALVES[q][0] * P
                        v.bn_stats(bns[:, n * 6:n * 6 + 6], arr[:, lo:min(lo + size(q) * P, N)])
                        n += 1
                chain(v.memset(st[:, 60:61], 0.0))
                chain(v.bn_aggr(col[:, 16:18], bns[:, 0:n * 6]))
                chain(v.tensor_scalar(col[:, 17:18], col[:, 17:18], EPS, None, ALU.add))
                root(2 + i, col[:, 17:18], col[:, 18:19])
                a, c = col[:, 4 + 2 * i:5 + 2 * i], col[:, 5 + 2 * i:6 + 2 * i]
                chain(v.tensor_tensor(a, col[:, 18:19], w_(f"g{i}"), ALU.mult))
                chain(v.tensor_tensor(col[:, 19:20], col[:, 16:17], a, ALU.mult))
                chain(v.tensor_tensor(c, w_(f"bt{i}"), col[:, 19:20], ALU.subtract))
                v.memset(st[:, 60:61], 0.0).then_inc(S["bn_ac"], 1)

            batch_norm(0, h_f, "n2_r0", 2, 2)
            for i, arr in ((1, big[:, 0:NP]), (2, big[:, NP:2 * NP])):
                dve.wait_ge(S["bn_bias"], i)
                v.tensor_tensor(col[:, 10 + i:11 + i], psC[:, 0:1], w_(f"b{i}"), ALU.add)
                v.tensor_scalar(chb[:, :], w_(f"W{i}"), col[:, 2 + 2 * i:3 + 2 * i], None, ALU.mult)\
                    .then_inc(S["bn_w"], 1)
                batch_norm(i, arr, "l1_relu", NG * (i - 1), 1)

            with dve.Fori(0, NG) as t:
                chain.loop(t, 6)
                T = temps
                gs = bass.ds(t * GB, GB)
                xg, hg = xs[:, gs, :], hst[:, gs, :]
                dve.wait_ge(S["n3_T"], t + 2)
                chain(v.tensor_tensor(xg, xg, g3(psA[:, 0:GW]), ALU.add))
                norm(t + 8 * NG, xg, g3(T[2]))
                chain(v.tensor_scalar(hg, g3(T[2]), 0.0, None, ALU.max))
                dve.wait_ge(S["n3_st"], t * 16 + 16)
                v.tensor_tensor(g3(T[4]), hg, along(outn[:, gs], D), ALU.mult).then_inc(S["n3_hs"], 1)
            chain.end(NG)

            chain(v.memset(big[:, 0:(NB + 1) * SW], 0.0))
            dve.wait_ge(S["n3_st"], 16 * NG + 16)
            v.memset(ring[:, :, D:D + 1], 1.0).then_inc(S["zeroed"], 1)
            by_dst(2)
            chain(v.tensor_copy(deg[:, :], acc_p[:, 0:NB, D]))
            chain(v.tensor_scalar(tt[:, :], deg[:, :], 1.0, None, ALU.max))
            root(5, tt[:, :], inn[:, :])

            with dve.Fori(0, NG) as t:
                chain.loop(t, 2 * (3 + 4))
                T = temps
                for q in range(2):
                    dve.wait_ge(S["n4_in"], t * 2 + (q + 1))
                    v.tensor_tensor(cols(T[2], q), cols(T[0], q), cols(T[3], q), ALU.mult).then_inc(S["n4_m"], 1)
                for q in range(2):
                    lo, hi_ = HALVES[q]
                    g = at(t, q)
                    xg, hg = xs[:, g, :], hst[:, g, :]
                    dve.wait_ge(S["n4_mm"], t * 2 + (q + 3))
                    chain(v.tensor_tensor(c3(T[7], q), c3(psB, q), along(inn[:, g], D), ALU.mult))
                    chain(v.tensor_tensor(cols(T[7], q), cols(T[7], q), cols(psB[:, 1024:], q), ALU.add))
                    chain(v.tensor_tensor(xg, xg, c3(T[7], q), ALU.add))
                    norm(t * 2 + (9 * NG + q), xg, c3(T[7], q), lo, size(q))
                    v.tensor_scalar(hg, c3(T[7], q), 0.0, None, ALU.max).then_inc(S["n4_h"], 1)
            chain.end(NG)
            dve.wait_ge(S["n4_h"], 2 * NG + 2)
            v.reduce_sum(chb[:, :], hst[:, 0:NB - 1, :].rearrange("p b d -> p d b"), AX.X).then_inc(S["n4_sum"], 1)
            dve.wait_ge(S["n4_mean"], 1)
            chain(v.tensor_scalar(col[:, 3:4], psC[:, 0:1], 1.0 / N, None, ALU.mult))
            chain(v.tensor_tensor(col[:, 20:23], w_("b_ih"), w_("b_hh"), ALU.add))
            v.tensor_scalar(col[:, 24:27], col[:, 20:23], 0.5, None, ALU.mult).then_inc(S["n4_meanc"], 1)
            chain(v.memset(big[:, 0:(NB + 1) * SW], 0.0))
            dve.wait_ge(S["n4_st"], 16)
            v.memset(ring[:, :, D:D + 1], 1.0).then_inc(S["zeroed"], 1)
            by_dst(3)

            with dve.Fori(0, NG) as t:
                chain.loop(t, 2 * (1 + 2 + 2 + 4 + 3))
                T = temps
                for q in range(2):
                    chain(v.tensor_tensor(c3(T[4], q), over(r_("b_msg"), size(q)), along(deg[:, at(t, q)], D), ALU.mult))
                    dve.wait_ge(S["n5_m"], t * 2 + (q + 1))
                    v.tensor_tensor(cols(T[2], q), cols(T[4], q), cols(psB, q), ALU.add).then_inc(S["n5_msg"], 1)
                for q in range(2):
                    dve.wait_ge(S["n5_rza"], t * 2 + (q + 1))
                    v.tensor_scalar(cols(T[5], q), cols(T[5], q), 0.5, 0.5, ALU.mult, ALU.add)
                    chain(v.tensor_scalar(cols(T[4], q), cols(T[4], q), 0.5, 0.5, ALU.mult, ALU.add))
                    dve.wait_ge(S["n5_nn"], t * 2 + (q + 1))
                    chain(v.scalar_tensor_tensor(cols(T[6], q), cols(psB[:, 1024:], q), w_("b_hh", 2, 3), cols(T[4], q),
                                                 ALU.add, ALU.mult))
                    v.tensor_tensor(cols(T[6], q), cols(T[6], q), cols(psB, q), ALU.add).then_inc(S["n5_npre"], 1)
                for q in range(2):
                    dve.wait_ge(S["n5_n"], t * 2 + (q + 1))
                    chain(v.tensor_tensor(cols(T[3], q), cols(T[1], q), cols(T[0], q), ALU.subtract))
                    chain(v.tensor_tensor(cols(T[3], q), cols(T[3], q), cols(T[5], q), ALU.mult))
                    v.tensor_tensor(cols(T[3], q), cols(T[3], q), cols(T[0], q), ALU.add).then_inc(S["n5_hn"], 1)
                for q in range(2):
                    dve.wait_ge(S["n5_hnT"], t * 2 + (q + 3))
                    norm(t * 2 + (11 * NG + q), c3(psA, q), c3(T[6], q), HALVES[q][0], size(q))
                    chain(v.tensor_tensor(c3(T[6], q), c3(T[6], q), over(r_("gamma"), size(q)), ALU.mult))
                    chain(v.tensor_tensor(c3(T[6], q), c3(T[6], q), over(r_("beta"), size(q)), ALU.add))
                    chain(v.tensor_tensor(cols(T[6], q), cols(T[6], q), cols(T[2], q), ALU.add))
                    dve.wait_ge(S["n5_st"], t * 16 + 16)
                    v.tensor_tensor(c3(T[7], q), c3(T[6], q), xs[:, at(t, q), :], ALU.add).then_inc(S["n5_out"], 1)
            chain.end(NG)

        @block.scalar
        def _(act):
            chain = Chain(act, act_step)
            a = nc.scalar

            def copy(out_, in_):
                return a.activation(out_, in_, ACT.Copy)

            def std(turn, lo=0, n=GB):
                act.wait_ge(S["s_var"], turn + 1)
                a.activation(nrm[:, 24 + lo:24 + lo + n], nrm[:, 16 + lo:16 + lo + n], ACT.Sqrt)\
                    .then_inc(S["s_std"], 1)

            def stds(turn):
                for q in range(2):
                    std(turn + q, HALVES[q][0], size(q))

            def rooted(at):
                act.wait_ge(S["s_root"], at)
                a.activation(rootv[:, 64:64 + NB], rootv[:, 0:NB], ACT.Sqrt).then_inc(S["s_rooted"], 1)

            def indices(n):
                def lay(bt, h, turn, count=BT):
                    for k in range(h * BT, h * BT + count):
                        act.wait_ge(s_row[k], turn * 16 + row_base(k, n))
                    copy(idx[:, h * BT:h * BT + count], idx_d[:, bass.ds(bt * BT, count)]).then_inc(S["s_idx"], 1)

                with act.Fori(0, SCAT_TURNS) as turn:
                    for h in range(2):
                        lay(turn * 2 + h, h, turn)
                lay(2 * SCAT_TURNS, 0, SCAT_TURNS)
                lay(2 * SCAT_TURNS + 1, 1, SCAT_TURNS, 1)

            opened(act, ACT_OPEN)
            with act.Fori(0, 2 * NG) as t:
                std(t)

            with act.Fori(0, TURNS) as turn:
                for h in range(2):
                    act.wait_ge(s_pay[h], turn * 16 + 16 + 16 * (SCAT_TURNS + 1))
                    copy(idx[:, h * BT:(h + 1) * BT], ring[:, h * BT:(h + 1) * BT, ROW - 1]).then_inc(S["s_idx"], 1)

            act.wait_ge(S["s_free"], BANKS + CHUNKS)
            with act.Fori(0, NG) as t:
                T = temps
                for q in range(2):
                    act.wait_ge(S["n1_lin"], t * 2 + (q + 1))
                    copy(c3(T[0], q), agg[:, at(t, q), :]).then_inc(S["n1_agg"], 1)
                for q in range(2):
                    act.wait_ge(S["n1_T"], t * 6 + (q + 1))
                    copy(cols(T[1], q), cols(psA, q)).then_inc(S["n1_Tc"], 1)
                for q in range(2):
                    act.wait_ge(S["n1_T"], t * 6 + (q + 3))
                    copy(cols(T[0], q), cols(psA, q)).then_inc(S["n1_Tc"], 1)
                stds(t * 2 + 2 * NG)
                for q in range(2):
                    act.wait_ge(S["n1_T"], t * 6 + (q + 5))
                    a.activation(cols(T[1], q), cols(psA, q), ACT.Identity, bias=w_("ln2_b"), scale=w_("ln2_g"))\
                        .then_inc(S["n1_Tc"], 1)
                for q in range(2):
                    lo, hi_ = HALVES[q]
                    act.wait_ge(S["n1_qky"], t * 2 + (q + 1))
                    pq = psB[:, lo * HID:hi_ * HID].rearrange("p (b d) -> p b d", d=HID)
                    copy(qst[:, at(t, q), :], pq[:, :, 0:ATTN]).then_inc(S["n1_q"], 1)

            act.wait_ge(S["zeroed"], 1)
            def a_turned(bt):
                act.wait_ge(S["a_T"], bt + 1)
                act.wait_ge(S["a_q"], bt)
                copy(onehotT[:, :], psT).then_inc(S["a_Tc"], 1)

            def a_tanh(bt, h):
                act.wait_ge(S["a_z"], bt + 1)
                a.activation(arows[h][:, :, KY:KY + ATTN], zt, ACT.Tanh).then_inc(S["a_e"], 1)

            def a_weights(bt, h):
                act.wait_ge(S["a_mb"], bt + 1)
                chain(copy(mb[:, h:h + 1], ps[:, MCOL + P:MCOL + P + 1]))
                chain(a.activation(mb[:, 3 + h:4 + h], mb[:, h:h + 1], ACT.Copy, scale=-1.0))
                before = (h - 1) % ADEEP
                a.activation(mb[:, 6 + h:7 + h], mb[:, before:before + 1], ACT.Exp, bias=mb[:, 3 + h:4 + h])
                chain(a.activation(wexp[:, :], sc[:, :], ACT.Exp, bias=mb[:, 3 + h:4 + h]))

            def a_weighted(bt, h):
                for k in range(BT):
                    if 2 * k >= BT:
                        act.wait_ge(S["a_w"], bt * BT + (2 * k - 9))
                    a.activation(ahot[h][:, k, :], abit[h][:, k, :], ACT.Copy, scale=wexp[:, k:k + 1])\
                        .then_inc(S["a_w"], 1)

            def a_index(bt, h):
                copy(idx[:, h * BT:(h + 1) * BT], meta_s[:, bass.ds(bt * BT, BT), 1]).then_inc(S["s_idx"], 1)

            for h in range(ADEEP):
                a_index(h, h)
            a_turned(0)
            a_turned(1)
            a_tanh(0, 0)
            a_weights(0, 0)
            a_weighted(0, 0)
            with act.Fori(0, BATCHES // ADEEP) as turn:
                chain.loop(turn, ADEEP * 3)
                for h in range(ADEEP):
                    bt, h1 = turn * ADEEP + h, (h + 1) % ADEEP
                    a_tanh(bt + 1, h1)
                    a_index(bt + 3, h)
                    a_turned(bt + 2)
                    a_weights(bt + 1, h1)
                    a_weighted(bt + 1, h1)
            chain.end(BATCHES // ADEEP)

            act.wait_ge(S["zeroed"], 2)
            rooted(1)
            act.wait_ge(S["n2_sc"], 1)
            a.activation(endt[:, :], cnt[:, :], ACT.Exp).then_inc(S["n2_sce"], 1)
            act.wait_ge(S["n2_ubc"], 1)
            with act.Fori(0, NG) as t:
                T = temps
                act.wait_ge(S["n2_o0"], t * 2 + 2)
                for q in range(2):
                    lo, hi_ = HALVES[q]
                    ue = T[0][:, lo * ATTN:hi_ * ATTN].rearrange("p (b d) -> p b d", d=ATTN)
                    copy(ue, acc_a[:, at(t, q), D:D + ATTN]).then_inc(S["n2_ue"], 1)
                for q in range(2):
                    act.wait_ge(S["n2_T"], t * 6 + (q + 1))
                    copy(cols(T[1][0:ATTN, :], q), cols(psA[0:ATTN, :], q)).then_inc(S["n2_Tc"], 1)
                stds(t * 4 + 4 * NG)
                for q in range(2):
                    act.wait_ge(S["n2_T"], t * 6 + (q + 3))
                    a.activation(cols(T[1], q), cols(psA, q), ACT.Identity, bias=w_("ln3_b"), scale=w_("ln3_g"))\
                        .then_inc(S["n2_Tc"], 1)
                for q in range(2):
                    act.wait_ge(S["n2_hid"], t * 2 + (q + 1))
                    for k in range(2):
                        ins = a.activation(cols(T[5 + k], q), cols(psB[:, 1024 * k:], q), ACT.Relu,
                                           bias=w_("ffn_b1", k, k + 1))
                    ins.then_inc(S["n2_relu"], 1)
                stds(t * 4 + (4 * NG + 2))
                for q in range(2):
                    act.wait_ge(S["n2_T"], t * 6 + (q + 5))
                    copy(cols(T[0], q), cols(psA, q))
                    copy(cols(T[1], q), cols(psC, q)).then_inc(S["n2_Tc"], 1)
                for q in range(2):
                    act.wait_ge(S["n2_o0"], t * 2 + (q + 3))
                    a.activation(h_f[:, bass.ds(t * GW + HALVES[q][0] * P, size(q) * P)], cols(psB, q), ACT.Relu,
                                 bias=col[:, 2:3]).then_inc(S["n2_r0"], 1)

            rooted(2)
            for i in (1, 2):
                with act.Fori(0, NG) as t:
                    act.wait_ge(S["l1_mm"], t + 1 + NG * (i - 1))
                    a.activation(big[:, bass.ds(t * GW + (i - 1) * NP, GW)], psB[:, 0:GW], ACT.Relu,
                                 bias=col[:, 10 + i:11 + i]).then_inc(S["l1_relu"], 1)
                rooted(2 + i)
            act.wait_ge(S["bn_ac"], 3)
            with act.Fori(0, NG) as t:
                act.wait_ge(S["n3_T"], t + 1)
                a.activation(temps[0], big[:, bass.ds(t * GW + NP, GW)], ACT.Identity, bias=col[:, 9:10],
                             scale=col[:, 8:9]).then_inc(S["n3_o"], 1)
                std(t + 8 * NG)

            indices(2)
            act.wait_ge(S["added"], 1)
            rooted(5)
            with act.Fori(0, NG) as t:
                T = temps
                for q in range(2):
                    act.wait_ge(S["n4_mm"], t * 2 + (q + 1))
                    copy(c3(T[0], q), acc_p[:, at(t, q), 0:D])
                    copy(c3(T[3], q), hst[:, at(t, q), :]).then_inc(S["n4_in"], 1)
                for i, (to, bank) in enumerate(((1, psA), (6, psC), (5, psA))):
                    for q in range(2):
                        act.wait_ge(S["n4_T"], t * 6 + (2 * i + q + 1))
                        copy(cols(T[to], q), cols(bank, q)).then_inc(S["n4_Tc"], 1)
                stds(t * 2 + 9 * NG)

            act.wait_ge(S["n4_meanc"], 1)
            indices(3)
            act.wait_ge(S["added"], 2)
            with act.Fori(0, NG) as t:
                T = temps
                for q in range(2):
                    act.wait_ge(S["n5_hnT"], t * 2 + (q + 1))
                    copy(c3(T[0], q), acc_p[:, at(t, q), 0:D])
                    copy(c3(T[3], q), hst[:, at(t, q), :]).then_inc(S["n5_s"], 1)
                for q in range(2):
                    act.wait_ge(S["n5_sT"], t * 2 + (q + 1))
                    copy(cols(T[1], q), cols(psA, q)).then_inc(S["n5_sTc"], 1)
                for q in range(2):
                    act.wait_ge(S["n5_T"], t * 2 + (q + 1))
                    a.activation(cols(T[0], q), cols(psA, q), ACT.Identity, bias=col[:, 3:4])
                    copy(cols(T[1], q), cols(psC, q)).then_inc(S["n5_Tc"], 1)
                for q in range(2):
                    act.wait_ge(S["n5_rz"], t * 2 + (q + 1))
                    for k in range(2):
                        ins = a.activation(cols(T[4 + k], q), cols(psB[:, 1024 * k:], q), ACT.Tanh, scale=0.5,
                                           bias=col[:, 24 + k:25 + k])
                    ins.then_inc(S["n5_rza"], 1)
                for q in range(2):
                    act.wait_ge(S["n5_npre"], t * 2 + (q + 1))
                    a.activation(cols(T[0], q), cols(T[6], q), ACT.Tanh, bias=w_("b_ih", 2, 3)).then_inc(S["n5_n"], 1)
                stds(t * 2 + 11 * NG)

        @block.tensor
        def _(pe):
            m = nc.tensor
            ident = c_("ident")

            def turnT(src_, dst_, q, n=P):
                for j in range(*HALVES[q]):
                    ins = m.transpose(dst_[0:n, j * P:(j + 1) * P], src_[:, j * n:(j + 1) * n], ident)
                return ins

            def nodes(dst_, pairs, q, width=P, stride=P):
                for j in range(*HALVES[q]):
                    for i, (l, r) in enumerate(pairs):
                        ins = m.matmul(dst_[:, j * stride:j * stride + width], l[:, j * P:(j + 1) * P], r,
                                       start=i == 0, stop=i == len(pairs) - 1)
                return ins

            def feats(dst_, pairs, q):
                lo, hi_ = HALVES[q][0] * P, HALVES[q][1] * P
                for i, (l, r) in enumerate(pairs):
                    ins = m.matmul(dst_[:, lo:hi_], l, r(lo, hi_), start=i == 0, stop=i == len(pairs) - 1)
                return ins

            def part(v):
                return lambda l, r: v[:, l:r]

            def bucket():
                pe.wait_ge(S["k_counts"], 1)
                m.matmul(psC[0:NB, 0:1], cnt[:, :], c_("ones", 0, 1), start=True, stop=True)\
                    .then_inc(S["k_sums"], 1)
                pe.wait_ge(S["k_counts"], 2)
                ch = chb[0:NB, :]
                before, upto = c_("before")[0:NB, :], c_("upto")[0:NB, :]
                m.matmul(psC[:, 64:64 + NB], ch, before, start=True, stop=False)
                m.matmul(psC[:, 64:64 + NB], c_("strict"), cnt[:, :], start=False, stop=True)
                m.matmul(psC[:, 128:128 + NB], ch, upto, start=True, stop=True)
                m.matmul(psC[:, 192:192 + NB], ch, before, start=True, stop=False)
                m.matmul(psC[:, 192:192 + NB], c_("ones"), cnt[:, :], start=False, stop=True)
                m.matmul(psC[0:NB, 256:257], upto, chcol[0:NB, 0:1], start=True, stop=True).then_inc(S["k_sums"], 1)
                pe.wait_ge(S["k_counts"], 3)
                for lo in range(0, CHUNKS, 512):
                    hi_ = min(lo + 512, CHUNKS)
                    ins = m.matmul(psA[0:1, lo:hi_], c_("ones", 0, 1)[0:NB, :], ge[:, lo:hi_], start=True, stop=True)
                ins.then_inc(S["k_sums"], 1)

            regs = [pe.alloc_register(f"pe_blk{k}") for k in range(BT)]

            def by_dst_chunks():
                G = -(-EC // P)
                pe.wait_ge(S["d_keys"], 1)
                for at, keys in ((0, keyp), (1, key_d[:, :])):
                    for g in range(G):
                        n = min(P, EC - g * P)
                        o_ = at * 1024 + g * P
                        ins = m.transpose(psB[0:n, o_:o_ + P], keys[:, g * P:g * P + n], ident)
                ins.then_inc(S["d_turned"], 1)
                pe.wait_ge(S["d_keys"], 2)
                m.matmul(psC[0:1, 0:P], st[:, 24:25], ident, start=True, stop=True)
                for g in range(G):
                    n = min(P, EC - g * P)
                    ins = m.matmul(psA[:, g * P:g * P + n], lob[0:n, g, :], ident[0:n, 0:n], start=True, stop=True)
                ins.then_inc(S["d_turned"], 1)

            def by_dst(n):
                def body(bt, h, turn, count=BT):
                    pe.wait_ge(s_oh[h], turn + (1 + TURNS + (n - 2) * (SCAT_TURNS + 1)))
                    for k in range(count):
                        slot = h * BT + k
                        pe.wait_ge(s_row[slot], turn * 16 + (16 + row_base(slot, n)))
                        pe.wait_ge(S["s_free"], bt * BT + (FREE0[n] + k + 1))
                        bank = (1 + slot % BANKS) * 512
                        m.matmul(ps[:, bank:bank + SW], dhot[h][:, k, 0:P], ring[:, slot, 0:SW],
                                 start=True, stop=True)
                        m.matmul(ps[:, bank + SW:bank + 2 * SW], dhot[h][:, k, P:2 * P], ring[:, slot, 0:SW],
                                 start=True, stop=True).then_inc(S["s_ps"], 1)

                with pe.Fori(0, SCAT_TURNS) as turn:
                    for h in range(2):
                        body(turn * 2 + h, h, turn)
                body(2 * SCAT_TURNS, 0, SCAT_TURNS)
                body(2 * SCAT_TURNS + 1, 1, SCAT_TURNS, 1)
                w = pe.alloc_register(f"pe_wide{n}")
                pe.load([w], wide[0:1, 0:1])
                with pe.If_ne(w, 0):
                    with pe.Fori(0, EC) as c:
                        pe.wait_ge(S["f_row"], c * 16 + (16 + 16 * EC * (n - 2)))
                        hold(pe)
                        with pe.Fori(0, NB) as b:
                            pe.wait_ge(S["f_hot"], c * NB + b + (1 + NB * EC * (n - 2)))
                            m.matmul(ps[:, 0:SW], onehot[:, 0, :], ring[:, 0, 0:SW], start=True, stop=True)\
                                .then_inc(S["f_ps"], 1)

            opened(pe, PE_OPEN)
            opened(pe, ("n3_T",), 1)
            pe.sem_inc(S["s_ps"], RING)
            pe.wait_ge(s_const, 32)
            bucket()
            pe.wait_ge(S["g_in"], 1)
            m.matmul(psC[:, 0:1], early[2][:, 0:D], c_("ones", 0, 1), start=True, stop=True).then_inc(S["g_out"], 1)
            pe.wait_ge(S["g_in"], 2)
            m.matmul(psC[:, 64:64 + D], chb[:, :], w_("Wg"), start=True, stop=True).then_inc(S["g_out"], 1)
            by_dst_chunks()
            pe.wait_ge(S["d_wide"], 1)
            with pe.Fori(0, TURNS) as turn:
                for h in range(2):
                    pe.wait_ge(s_oh[h], turn + 1)
                    for k in range(BT):
                        slot = h * BT + k
                        pe.wait_ge(s_row[slot], turn * 16 + (16 + row_base(slot, 0)))
                        pe.wait_ge(S["s_free"], turn * RING + (slot + 1))
                        bank = (1 + slot % BANKS) * 512
                        m.matmul(ps[:, bank:bank + D + SW], onehot[:, slot, :], ring[:, slot, 0:D + SW],
                                 start=True, stop=True).then_inc(S["s_ps"], 1)

            with pe.Fori(0, NG) as t:
                T = temps
                for q in range(2):
                    pe.wait_ge(S["n1_agg"], t * 2 + (q + 1))
                    turnT(T[0], psA, q).then_inc(S["n1_T"], 1)
                for q in range(2):
                    pe.wait_ge(S["n1_Tc"], t * 6 + (q + 1))
                    nodes(psC, [(T[1], w_("msg"))], q).then_inc(S["n1_msg"], 1)
                for q in range(2):
                    pe.wait_ge(S["n1_t"], t * 2 + (q + 1))
                    turnT(T[2], psA, q).then_inc(S["n1_T"], 1)
                for q in range(2):
                    pe.wait_ge(S["n1_Tc"], t * 6 + (q + 3))
                    nodes(psC, [(T[0], w_("lin"))], q).then_inc(S["n1_lin"], 1)
                for q in range(2):
                    pe.wait_ge(S["n1_z"], t * 2 + (q + 1))
                    turnT(T[4], psA, q).then_inc(S["n1_T"], 1)
                for q in range(2):
                    pe.wait_ge(S["n1_Tc"], t * 6 + (q + 5))
                    pe.wait_ge(S["n1_q"], t * 2 + (q + 1))
                    pe.wait_ge(S["n1_ky"], t * 2 + (q + 1))
                    nodes(psB, [(T[1], w_("qky"))], q, HID, HID).then_inc(S["n1_qky"], 1)

            pe.wait_ge(S["n1_q"], 2 * NG + 2)
            pe.wait_ge(S["n1_ky"], 2 * NG + 2)

            def a_turn(bt, h):
                pe.wait_ge(S["a_hot"], bt + 1)
                pe.wait_ge(S["a_Tc"], bt)
                for k in range(BT):
                    ins = m.transpose(psT[:, k * P:(k + 1) * P], abit[h][:, k, :], identb[:, :])
                ins.then_inc(S["a_T"], 1)

            def a_q(bt):
                pe.load(regs, blk_s[0:1, bass.ds(bt * BSTRIDE, BT)])
                bs = [pe.snap(r, min_val=0, max_val=NB - 1) for r in regs]
                pe.wait_ge(S["a_Tc"], bt + 1)
                pe.wait_ge(S["a_z"], bt)
                for k in range(BT):
                    q = qst[:, bass.ds(bs[k], 1), :].rearrange("p a d -> p (a d)")
                    ins = m.matmul(ps[:, k * ATTN:(k + 1) * ATTN], onehotT[:, k * P:(k + 1) * P], q,
                                   start=True, stop=True)
                ins.then_inc(S["a_q"], 1)

            def a_maxT(bt):
                pe.wait_ge(S["a_bm"], bt + 1)
                m.matmul(ps[0:1, MCOL:MCOL + P], st[:, 24:25], ident, start=True, stop=True).then_inc(S["a_mt"], 1)

            def a_maxb(bt):
                pe.wait_ge(S["a_mr"], bt + 1)
                m.matmul(ps[:, MCOL + P:MCOL + P + 1], c_("ones")[0:1, :], mrun[0:1, 0:1], start=True, stop=True)\
                    .then_inc(S["a_mb"], 1)

            def a_products(bt, h, pairs):
                for k in range(2 * pairs.start, 2 * pairs.stop):
                    pe.wait_ge(S["a_w"], bt * BT + (k + 1))
                    if k % 2 == 0:
                        pe.wait_ge(S["a_free"], bt * BT + (k + 2))
                    m.matmul(ps[:, pair_at(h, k):pair_at(h, k) + AGW], ahot[h][:, k, :],
                             arows[h][:, k, ATTN:ATTN + AGW], start=True, stop=True).then_inc(S["s_ps"], 1)

            a_turn(0, 0)
            a_q(0)
            a_turn(1, 1)
            a_maxT(0)
            a_maxb(0)
            with pe.Fori(0, BATCHES // ADEEP) as turn:
                for h in range(ADEEP):
                    bt, h1, h2 = turn * ADEEP + h, (h + 1) % ADEEP, (h + 2) % ADEEP
                    a_q(bt + 1)
                    a_products(bt, h, range(0, 1))
                    a_turn(bt + 2, h2)
                    a_products(bt, h, range(1, 2))
                    a_maxT(bt + 1)
                    a_products(bt, h, range(2, 3))
                    a_maxb(bt + 1)
                    a_products(bt, h, range(3, 5))
            a_products(BATCHES - 1, 0, range(0, 5))

            pe.wait_ge(S["a_free"], 2 * APAIRS + CHUNKS)
            m.matmul(psC[:, 0:1], w_("W0", 2 * D, 3 * D), w_("u"), start=True, stop=True).then_inc(S["n2_ub"], 1)
            with pe.Fori(0, NG) as t:
                T = temps
                for q in range(2):
                    pe.wait_ge(S["n2_ue"], t * 2 + (q + 1))
                    hold(pe)
                    turnT(T[0], psA, q, ATTN).then_inc(S["n2_T"], 1)
                for q in range(2):
                    pe.wait_ge(S["n2_Tc"], t * 6 + (q + 1))
                    pe.wait_ge(S["n2_r0"], t * 2 + (q + 1))
                    nodes(psB, [(T[1][0:ATTN, :], w_("We")[0:ATTN, :])], q).then_inc(S["n2_we"], 1)
                for q in range(2):
                    pe.wait_ge(S["n2_z"], t * 2 + (q + 1))
                    turnT(T[4], psA, q).then_inc(S["n2_T"], 1)
                for q in range(2):
                    pe.wait_ge(S["n2_Tc"], t * 6 + (q + 3))
                    for k in range(2):
                        ins = feats(psB[:, 1024 * k:], [(w_("w1", k * P, (k + 1) * P), part(T[1]))], q)
                    ins.then_inc(S["n2_hid"], 1)
                for q in range(2):
                    pe.wait_ge(S["n2_relu"], t * 2 + (q + 1))
                    nodes(psA, [(T[5], w_("w2", 0, D)), (T[6], w_("w2", D, 2 * D))], q).then_inc(S["n2_ffn"], 1)
                for q in range(2):
                    pe.wait_ge(S["n2_x"], t * 2 + (q + 3))
                    turnT(T[4], psA, q)
                    turnT(T[7], psC, q).then_inc(S["n2_T"], 1)
                for q in range(2):
                    pe.wait_ge(S["n2_Tc"], t * 6 + (q + 5))
                    feats(psB, [(w_("W0", 0, D), part(T[0])), (w_("W0", D, 2 * D), part(T[1]))], q)\
                        .then_inc(S["n2_o0"], 1)

            for i in (1, 2):
                pe.wait_ge(S["bn_ac"], i)
                m.matmul(psC[:, 0:1], w_(f"W{i}"), col[:, 3 + 2 * i:4 + 2 * i], start=True, stop=True)\
                    .then_inc(S["bn_bias"], 1)
                pe.wait_ge(S["bn_w"], i)
                with pe.Fori(0, NG) as t:
                    pe.wait_ge(S["l1_relu"], t + NG * (i - 1))
                    f = (lambda l, r: h_f[:, bass.ds(t * GW + l, r - l)]) if i == 1 else \
                        (lambda l, r: big[:, bass.ds(t * GW + l, r - l)])
                    for q in range(2):
                        ins = feats(psB, [(chb[:, :], f)], q)
                    ins.then_inc(S["l1_mm"], 1)
            with pe.Fori(0, NG) as t:
                pe.wait_ge(S["n3_o"], t + 1)
                pe.wait_ge(S["n3_hs"], t + 1)
                for q in range(2):
                    ins = turnT(temps[0], psA, q)
                ins.then_inc(S["n3_T"], 1)

            by_dst(2)
            with pe.Fori(0, NG) as t:
                T = temps
                for q in range(2):
                    pe.wait_ge(S["n4_in"], t * 2 + (q + 1))
                    turnT(T[0], psA, q).then_inc(S["n4_T"], 1)
                for q in range(2):
                    turnT(T[3], psC, q).then_inc(S["n4_T"], 1)
                for q in range(2):
                    pe.wait_ge(S["n4_m"], t * 2 + (q + 1))
                    pe.wait_ge(S["n4_Tc"], t * 6 + (q + 1))
                    turnT(T[2], psA, q).then_inc(S["n4_T"], 1)
                for q in range(2):
                    pe.wait_ge(S["n4_Tc"], t * 6 + (q + 5))
                    pe.wait_ge(S["n4_h"], t * 2 + (q + 1))
                    nodes(psB, [(T[1], w_("self")), (T[5], w_("inter"))], q)
                    nodes(psB[:, 1024:], [(T[6], w_("self"))], q).then_inc(S["n4_mm"], 1)
            pe.wait_ge(S["n4_sum"], 1)
            m.matmul(psC[:, 0:1], chb[:, :], c_("ones", 0, 1), start=True, stop=False)
            m.matmul(psC[:, 0:1], hst[0:LAST, NB - 1, :], c_("ones", 0, 1)[0:LAST, :], start=False, stop=True)\
                .then_inc(S["n4_mean"], 1)

            by_dst(3)
            with pe.Fori(0, NG) as t:
                T = temps
                for q in range(2):
                    pe.wait_ge(S["n5_s"], t * 2 + (q + 1))
                    pe.wait_ge(S["n5_out"], t * 2 + (q + 1))
                    turnT(T[0], psA, q).then_inc(S["n5_sT"], 1)
                for q in range(2):
                    turnT(T[3], psC, q)
                for q in range(2):
                    pe.wait_ge(S["n5_sTc"], t * 2 + (q + 1))
                    nodes(psB, [(T[1], w_("Wm"))], q).then_inc(S["n5_m"], 1)
                for q in range(2):
                    pe.wait_ge(S["n5_msg"], t * 2 + (q + 1))
                    turnT(T[2], psA, q).then_inc(S["n5_T"], 1)
                for q in range(2):
                    pe.wait_ge(S["n5_Tc"], t * 2 + (q + 1))
                    for k in range(2):
                        ins = feats(psB[:, 1024 * k:], [(w_("ih", k * D, (k + 1) * D), part(T[0])),
                                                        (w_("hh", k * D, (k + 1) * D), part(T[1]))], q)
                    ins.then_inc(S["n5_rz"], 1)
                for q in range(2):
                    pe.wait_ge(S["n5_rza"], t * 2 + (q + 1))
                    feats(psB, [(w_("ih", 2 * D, 3 * D), part(T[0]))], q)
                    feats(psB[:, 1024:], [(w_("hh", 2 * D, 3 * D), part(T[1]))], q).then_inc(S["n5_nn"], 1)
                for q in range(2):
                    pe.wait_ge(S["n5_hn"], t * 2 + (q + 1))
                    turnT(T[3], psA, q).then_inc(S["n5_hnT"], 1)


def _constants(np):
    c = np.zeros((P, CONST_W), np.float32)

    def put(n, v):
        a, w = CONST[n]
        c[:v.shape[0], a:a + w] = v
    put("ident", np.eye(P))
    put("strict", np.triu(np.ones((P, P)), 1))
    put("ones", np.ones((P, P)))
    put("iota", np.tile(np.arange(2 * P), (P, 1)))
    put("before", np.triu(np.ones((NB, NB)), 1))
    put("upto", np.triu(np.ones((NB, NB))))
    put("blocks", np.tile(np.arange(NB), (P, 1)))
    put("starts", np.tile(P * np.arange(NB), (P, 1)))
    put("part", np.arange(P)[:, None])
    return c


def kernel(**inputs):
    import numpy as np
    import concourse.bacc as bacc
    from concourse.bass_utils import run_bass_kernel_spmd

    i = {k: np.asarray(v) for k, v in inputs.items()}
    L0 = {k[7:]: v for k, v in i.items() if k.startswith("L0_gnn_")}
    L1 = {k[7:]: v for k, v in i.items() if k.startswith("L1_gnn_")}
    L2 = {k[7:]: v for k, v in i.items() if k.startswith("L2_gnn_")}
    L3 = {k[7:]: v for k, v in i.items() if k.startswith("L3_gnn_")}

    xp = np.zeros((NP, D), np.float32)
    xp[:N] = i["x"]
    xp = np.ascontiguousarray(xp.reshape(NB, P, D).transpose(1, 0, 2))

    def columns(e):
        k = np.full((P, EC), -1, np.int32)
        k[:, :EJ] = e[:EJ * P].reshape(P, EJ)
        k[:ER, EJ] = e[EJ * P:]
        return k

    def rows_of(e, behind):
        k = np.full(EC * P, behind, np.int32)
        k[:E] = e
        return np.ascontiguousarray(k.reshape(EC, P).T)

    w = np.zeros((P, WEIGHTS_W), np.float32)

    def put(n, v):
        a, width = WEIGHTS[n]
        w[:v.shape[0], a:a + width] = v

    def halves(v):
        return v.reshape(-1, P, v.shape[1]).transpose(1, 0, 2).reshape(P, -1)

    put("Wg", L0["Wg_in_w"])
    put("msg", L0["msg_w"])
    put("lin", L0["lin_w"])
    put("qky", np.concatenate([L0["Wq"], L0["Wk"], L0["Wy_w"]], 1))
    put("We", L0["We_w"])
    put("w1", L0["ffn_w1"])
    put("w2", halves(L0["ffn_w2"]))
    put("W0", halves(L1["W0"].T))
    put("W1", L1["W1"].T)
    put("W2", L1["W2"].T)
    put("self", L2["W_self"])
    put("inter", L2["W_inter"])
    put("Wm", L3["W_msg"].T)
    put("ih", L3["w_ih"].T)
    put("hh", L3["w_hh"].T)
    put("g_token", L0["g_token"].reshape(D, 1))
    for n in ("ln2_g", "ln2_b", "ln3_g", "ln3_b"):
        put(n, L0[n][:, None])
    put("ffn_b1", L0["ffn_b1"].reshape(2, P).T)
    put("u", L1["u"][0][:, None])
    for n in ("b0", "b1", "b2", "g0", "g1", "g2", "bt0", "bt1", "bt2"):
        put(n, L1[n][:, None])
    put("b_ih", L3["b_ih"].reshape(3, P).T)
    put("b_hh", L3["b_hh"].reshape(3, P).T)

    r = np.zeros((1, ROWS_W), np.float32)
    for n, v in (("eps", L0["eps"]), ("Wg_b", L0["Wg_in_b"]), ("ln1_g", L0["ln1_g"]), ("ln1_b", L0["ln1_b"]),
                 ("msg_b", L0["msg_b"]), ("lin_b", L0["lin_b"]), ("Wy_b", L0["Wy_b"]), ("We_b", L0["We_b"]),
                 ("ffn_b2", L0["ffn_b2"]), ("b_msg", L3["b_msg"]), ("gamma", L3["ln_gamma"]),
                 ("beta", L3["ln_beta"]), ("phi", L0["Wphi"])):
        a, width = ROWS[n]
        r[0, a:a + width] = v

    arrays = {"in_x": xp, "in_src": columns(i["src"]), "in_dst": columns(i["dst"]),
              "in_src_c": rows_of(i["src"], 0), "in_dst_c": rows_of(i["dst"], -1),
              "in_edge_attr": np.ascontiguousarray(i["edge_attr_128"]), 
              "in_chunks": np.arange(CHUNKS, dtype=np.float32)[None], "in_const": _constants(np),
              "in_weights": w, "in_rows": r}
    nc = bacc.Bacc("TRN2", target_bir_lowering=False, num_devices=1)
    args = [nc.dram_tensor(n, a.shape, mybir.dt.from_np(a.dtype), kind="ExternalInput").ap()
            for n, a in arrays.items()]
    out = nc.dram_tensor("out", (P, NB, D), F32, kind="ExternalOutput").ap()
    gnn_kernel(nc, *args, out)
    got = run_bass_kernel_spmd(nc, [arrays], core_ids=[0]).results[0]["out"]
    return np.ascontiguousarray(got.transpose(1, 0, 2).reshape(NP, D)[:N])
```
